# Optimizing a Trainium2 kernel written in Bass

```python
import numpy as np
import jax
import jax.numpy as jnp

def _softmax(x, axis=-1):
    return jax.nn.softmax(x, axis=axis)

def _gelu(x):
    return jax.nn.gelu(x, approximate=True)

def _silu(x):
    return jax.nn.silu(x)

def _sigmoid(x):
    return jax.nn.sigmoid(x)

def _layernorm(x, axis=-1, eps=1e-05):
    m = jnp.mean(x, axis=axis, keepdims=True)
    v = jnp.var(x, axis=axis, keepdims=True)
    return (x - m) / jnp.sqrt(v + eps)

def _scatter_add(tgt, idx, src, axis=0):
    return tgt.at[idx].add(src)

def _segment_sum(src, seg, n):
    return jax.ops.segment_sum(src, seg, n)
kernel_name = 'mk_sandwich_d2_jaxref_r8_e75578'

def setup_inputs(seed: int=0):
    np.random.seed(seed)
    _w = jnp.asarray

    def _L0_attn_setup():
        import jax, jax.numpy as jnp
        import numpy as np
        B, N, D = (8, 128, 512)
        H = 8
        HEAD_DIM = D // H
        E = HEAD_DIM // H
        key = jax.random.key(seed)
        ks = jax.random.split(key, 7)
        s = 0.02
        return {'x': jax.random.normal(ks[0], (B, N, D), dtype=jnp.float32), 'Wqk_w': jax.random.normal(ks[1], (2 * HEAD_DIM, D), dtype=jnp.float32) * s, 'Wqk_b': jnp.zeros((2 * HEAD_DIM,), dtype=jnp.float32), 'Wv_w': jax.random.normal(ks[2], (HEAD_DIM, D), dtype=jnp.float32) * s, 'Wv_b': jnp.zeros((HEAD_DIM,), dtype=jnp.float32), 'Wo_w': jax.random.normal(ks[3], (D, HEAD_DIM), dtype=jnp.float32) * s, 'Wo_b': jnp.zeros((D,), dtype=jnp.float32)}
    _L0_attn_in = _L0_attn_setup()

    def _L0_ffn_setup():
        import jax, jax.numpy as jnp
        import numpy as np
        H = 512
        I = 1376
        R = 32
        NLEV = 16
        Q_ZERO = 7.5
        Q_STEP = 0.005
        LR_SCALE = 0.02

        def _qlinear(x, q, scale, A, Bm):
            w = (q.astype(jnp.float32) - Q_ZERO) * (scale * Q_STEP)[:, None]
            y = jnp.einsum('bsh,oh->bso', x, w)
            return y + LR_SCALE * (x @ A @ Bm)
        key = jax.random.key(seed)
        ks = jax.random.split(key, 13)
        B, S = (2, 256)
        inp = {'x': jax.random.normal(ks[0], (B, S, H), jnp.float32), 'gate_q': jax.random.randint(ks[1], (I, H), 0, NLEV, jnp.int32), 'gate_scale': jax.random.uniform(ks[2], (I,), jnp.float32), 'gate_A': jax.random.normal(ks[3], (H, R), jnp.float32), 'gate_B': jax.random.normal(ks[4], (R, I), jnp.float32), 'up_q': jax.random.randint(ks[5], (I, H), 0, NLEV, jnp.int32), 'up_scale': jax.random.uniform(ks[6], (I,), jnp.float32), 'up_A': jax.random.normal(ks[7], (H, R), jnp.float32), 'up_B': jax.random.normal(ks[8], (R, I), jnp.float32), 'down_q': jax.random.randint(ks[9], (H, I), 0, NLEV, jnp.int32), 'down_scale': jax.random.uniform(ks[10], (H,), jnp.float32), 'down_A': jax.random.normal(ks[11], (I, R), jnp.float32), 'down_B': jax.random.normal(ks[12], (R, H), jnp.float32)}
        return inp
    _L0_ffn_in = _L0_ffn_setup()

    def _L1_attn_setup():
        import jax, jax.numpy as jnp
        import numpy as np
        HIDDEN = 512
        HEAD_DIM = 128
        N_Q_HEADS = 32
        N_KV_HEADS = 8
        SLIDING_WINDOW = 128
        ROPE_THETA = 10000.0
        BATCH, SEQ = (1, 256)

        def _rope(t, pos):
            d = t.shape[-1]
            half = d // 2
            inv_freq = ROPE_THETA ** (-jnp.arange(half, dtype=jnp.float32) / half)
            ang = pos[:, None].astype(jnp.float32) * inv_freq[None, :]
            cos = jnp.cos(ang)[None, :, None, :]
            sin = jnp.sin(ang)[None, :, None, :]
            t1, t2 = (t[..., :half], t[..., half:])
            return jnp.concatenate([t1 * cos - t2 * sin, t1 * sin + t2 * cos], axis=-1)
        key = jax.random.key(seed)
        ks = jax.random.split(key, 5)
        w_scale = HIDDEN ** (-0.5)
        return {'x': jax.random.normal(ks[0], (BATCH, SEQ, HIDDEN), jnp.float32), 'wq': jax.random.normal(ks[1], (HIDDEN, N_Q_HEADS * HEAD_DIM), jnp.float32) * w_scale, 'wk': jax.random.normal(ks[2], (HIDDEN, N_KV_HEADS * HEAD_DIM), jnp.float32) * w_scale, 'wv': jax.random.normal(ks[3], (HIDDEN, N_KV_HEADS * HEAD_DIM), jnp.float32) * w_scale, 'wo': jax.random.normal(ks[4], (N_Q_HEADS * HEAD_DIM, HIDDEN), jnp.float32) * w_scale}
    _L1_attn_in = _L1_attn_setup()

    def _L1_ffn_setup():
        import jax, jax.numpy as jnp
        import numpy as np
        B, S, IN, OUT = (4, 256, 512, 512)
        E, K, R = (8, 2, 16)
        CAP_FACTOR = 3.0
        ALPHA = 1.0 / R
        LN_EPS = 1e-05
        key = jax.random.key(seed)
        ks = jax.random.split(key, 6)
        return {'x': jax.random.normal(ks[0], (B, S, IN), dtype=jnp.float32), 'weight': jax.random.normal(ks[1], (OUT, IN), dtype=jnp.float32) * 0.02, 'lora_A': jax.random.normal(ks[2], (E, IN, R), dtype=jnp.float32) / np.sqrt(R), 'lora_B': jax.random.normal(ks[3], (E, R, OUT), dtype=jnp.float32) * 0.02, 'gw1': jax.random.normal(ks[4], (4 * E, IN), dtype=jnp.float32) * 0.02, 'gb1': jnp.zeros((4 * E,), dtype=jnp.float32), 'ln_gamma': jnp.ones((4 * E,), dtype=jnp.float32), 'ln_beta': jnp.zeros((4 * E,), dtype=jnp.float32), 'gw2': jax.random.normal(ks[5], (E, 4 * E), dtype=jnp.float32) * 0.02, 'gb2': jnp.zeros((E,), dtype=jnp.float32)}
    _L1_ffn_in = _L1_ffn_setup()
    _d = {'L0_attn_x': _L0_attn_in['x'], 'L0_attn_Wqk_w': _L0_attn_in['Wqk_w'], 'L0_attn_Wqk_b': _L0_attn_in['Wqk_b'], 'L0_attn_Wv_w': _L0_attn_in['Wv_w'], 'L0_attn_Wv_b': _L0_attn_in['Wv_b'], 'L0_attn_Wo_w': _L0_attn_in['Wo_w'], 'L0_attn_Wo_b': _L0_attn_in['Wo_b'], 'L0_ffn_gate_q': _L0_ffn_in['gate_q'], 'L0_ffn_gate_scale': _L0_ffn_in['gate_scale'], 'L0_ffn_gate_A': _L0_ffn_in['gate_A'], 'L0_ffn_gate_B': _L0_ffn_in['gate_B'], 'L0_ffn_up_q': _L0_ffn_in['up_q'], 'L0_ffn_up_scale': _L0_ffn_in['up_scale'], 'L0_ffn_up_A': _L0_ffn_in['up_A'], 'L0_ffn_up_B': _L0_ffn_in['up_B'], 'L0_ffn_down_q': _L0_ffn_in['down_q'], 'L0_ffn_down_scale': _L0_ffn_in['down_scale'], 'L0_ffn_down_A': _L0_ffn_in['down_A'], 'L0_ffn_down_B': _L0_ffn_in['down_B'], 'L1_attn_wq': _L1_attn_in['wq'], 'L1_attn_wk': _L1_attn_in['wk'], 'L1_attn_wv': _L1_attn_in['wv'], 'L1_attn_wo': _L1_attn_in['wo'], 'L1_ffn_weight': _L1_ffn_in['weight'], 'L1_ffn_lora_A': _L1_ffn_in['lora_A'], 'L1_ffn_lora_B': _L1_ffn_in['lora_B'], 'L1_ffn_gw1': _L1_ffn_in['gw1'], 'L1_ffn_gb1': _L1_ffn_in['gb1'], 'L1_ffn_ln_gamma': _L1_ffn_in['ln_gamma'], 'L1_ffn_ln_beta': _L1_ffn_in['ln_beta'], 'L1_ffn_gw2': _L1_ffn_in['gw2'], 'L1_ffn_gb2': _L1_ffn_in['gb2']}
    _x0 = _d['L0_attn_x']
    _d['L0_attn_x'] = jax.random.normal(jax.random.fold_in(jax.random.key(seed), 1), (8, 256, 512), dtype=_x0.dtype)
    del _x0
    return _d

def reference(L0_attn_x, L0_attn_Wqk_w, L0_attn_Wqk_b, L0_attn_Wv_w, L0_attn_Wv_b, L0_attn_Wo_w, L0_attn_Wo_b, L0_ffn_gate_q, L0_ffn_gate_scale, L0_ffn_gate_A, L0_ffn_gate_B, L0_ffn_up_q, L0_ffn_up_scale, L0_ffn_up_A, L0_ffn_up_B, L0_ffn_down_q, L0_ffn_down_scale, L0_ffn_down_A, L0_ffn_down_B, L1_attn_wq, L1_attn_wk, L1_attn_wv, L1_attn_wo, L1_ffn_weight, L1_ffn_lora_A, L1_ffn_lora_B, L1_ffn_gw1, L1_ffn_gb1, L1_ffn_ln_gamma, L1_ffn_ln_beta, L1_ffn_gw2, L1_ffn_gb2):

    def _L0_attn_ref(x, Wqk_w, Wqk_b, Wv_w, Wv_b, Wo_w, Wo_b):
        import jax, jax.numpy as jnp
        import numpy as np
        B, N, D = (8, 128, 512)
        H = 8
        HEAD_DIM = D // H
        E = HEAD_DIM // H
        b, n, _ = x.shape
        qk = (x @ Wqk_w.T + Wqk_b).reshape(b, n, H, E, 2)
        q = jnp.transpose(qk[..., 0], (0, 2, 1, 3))
        k = jnp.transpose(qk[..., 1], (0, 2, 1, 3))
        v = (x @ Wv_w.T + Wv_b).reshape(b, n, H, E)
        v = jnp.transpose(v, (0, 2, 1, 3))
        scores = jnp.einsum('bhqd,bhkd->bhqk', q, k)
        attn = jax.nn.softmax(scores, axis=-1) / jnp.asarray(HEAD_DIM ** 0.5, x.dtype)
        out = jnp.einsum('bhsl,bhlv->bhsv', attn, v)
        out = jnp.transpose(out, (0, 2, 1, 3)).reshape(b, n, H * E)
        return out @ Wo_w.T + Wo_b

    def _L0_ffn_ref(x, gate_q, gate_scale, gate_A, gate_B, up_q, up_scale, up_A, up_B, down_q, down_scale, down_A, down_B):
        import jax, jax.numpy as jnp
        import numpy as np
        H = 512
        I = 1376
        R = 32
        NLEV = 16
        Q_ZERO = 7.5
        Q_STEP = 0.005
        LR_SCALE = 0.02

        def _qlinear(x, q, scale, A, Bm):
            w = (q.astype(jnp.float32) - Q_ZERO) * (scale * Q_STEP)[:, None]
            y = jnp.einsum('bsh,oh->bso', x, w)
            return y + LR_SCALE * (x @ A @ Bm)
        g = _qlinear(x, gate_q, gate_scale, gate_A, gate_B)
        u = _qlinear(x, up_q, up_scale, up_A, up_B)
        h = jax.nn.silu(g) * u
        return _qlinear(h, down_q, down_scale, down_A, down_B)

    def _L1_attn_ref(x, wq, wk, wv, wo):
        import jax, jax.numpy as jnp
        import numpy as np
        HIDDEN = 512
        HEAD_DIM = 128
        N_Q_HEADS = 32
        N_KV_HEADS = 8
        SLIDING_WINDOW = 128
        ROPE_THETA = 10000.0
        BATCH, SEQ = (1, 256)

        def _rope(t, pos):
            d = t.shape[-1]
            half = d // 2
            inv_freq = ROPE_THETA ** (-jnp.arange(half, dtype=jnp.float32) / half)
            ang = pos[:, None].astype(jnp.float32) * inv_freq[None, :]
            cos = jnp.cos(ang)[None, :, None, :]
            sin = jnp.sin(ang)[None, :, None, :]
            t1, t2 = (t[..., :half], t[..., half:])
            return jnp.concatenate([t1 * cos - t2 * sin, t1 * sin + t2 * cos], axis=-1)
        B, S, _ = x.shape
        G = N_Q_HEADS // N_KV_HEADS
        sm_scale = HEAD_DIM ** (-0.5)
        q = (x @ wq).reshape(B, S, N_Q_HEADS, HEAD_DIM)
        k = (x @ wk).reshape(B, S, N_KV_HEADS, HEAD_DIM)
        v = (x @ wv).reshape(B, S, N_KV_HEADS, HEAD_DIM)
        pos = jnp.arange(S)
        q = _rope(q, pos)
        k = _rope(k, pos)
        qg = q.reshape(B, S, N_KV_HEADS, G, HEAD_DIM)
        scores = jnp.einsum('bqhgd,bshd->bhgqs', qg, k) * sm_scale
        i = pos[:, None]
        j = pos[None, :]
        allowed = (j <= i) & (j > i - SLIDING_WINDOW)
        neg = jnp.finfo(scores.dtype).min
        scores = jnp.where(allowed[None, None, None], scores, neg)
        attn = jax.nn.softmax(scores, axis=-1)
        out = jnp.einsum('bhgqs,bshd->bqhgd', attn, v).reshape(B, S, N_Q_HEADS * HEAD_DIM)
        return out @ wo

    def _L1_ffn_ref(x, weight, lora_A, lora_B, gw1, gb1, ln_gamma, ln_beta, gw2, gb2):
        import jax, jax.numpy as jnp
        import numpy as np
        B, S, IN, OUT = (4, 256, 512, 512)
        E, K, R = (8, 2, 16)
        CAP_FACTOR = 3.0
        ALPHA = 1.0 / R
        LN_EPS = 1e-05
        orig_shape = x.shape
        xf = x.reshape(-1, orig_shape[-1])
        N = xf.shape[0]
        capacity = int(CAP_FACTOR * N / E)
        h = xf @ gw1.T + gb1
        mu = jnp.mean(h, axis=-1, keepdims=True)
        var = jnp.mean((h - mu) ** 2, axis=-1, keepdims=True)
        h = (h - mu) * jax.lax.rsqrt(var + LN_EPS) * ln_gamma + ln_beta
        h = jax.nn.relu(h)
        gates = h @ gw2.T + gb2
        top_v, top_i = jax.lax.top_k(gates, K)
        top_g = jax.nn.softmax(top_v, axis=-1)
        onehot = (top_i[..., None] == jnp.arange(E)).astype(xf.dtype)
        counts = onehot.sum(axis=0)
        allowed = (counts <= capacity).astype(xf.dtype)
        w = jnp.einsum('nke,nk,ke->ne', onehot, top_g, allowed)
        main = xf @ weight.T
        tmp = jnp.einsum('ni,eir->enr', xf, lora_A)
        tmp = tmp * w.T[:, :, None]
        lora = jnp.einsum('enr,ero->no', tmp, lora_B) * ALPHA
        out = main + lora
        return out.reshape(*orig_shape[:-1], weight.shape[0])
    x = L0_attn_x
    x = x + _layernorm(_L0_attn_ref(_layernorm(x, axis=-1), L0_attn_Wqk_w, L0_attn_Wqk_b, L0_attn_Wv_w, L0_attn_Wv_b, L0_attn_Wo_w, L0_attn_Wo_b), axis=-1)
    x = x + _layernorm(_L0_ffn_ref(_layernorm(x, axis=-1), L0_ffn_gate_q, L0_ffn_gate_scale, L0_ffn_gate_A, L0_ffn_gate_B, L0_ffn_up_q, L0_ffn_up_scale, L0_ffn_up_A, L0_ffn_up_B, L0_ffn_down_q, L0_ffn_down_scale, L0_ffn_down_A, L0_ffn_down_B), axis=-1)
    x = x + _layernorm(_L1_attn_ref(_layernorm(x, axis=-1), L1_attn_wq, L1_attn_wk, L1_attn_wv, L1_attn_wo), axis=-1)
    x = x + _layernorm(_L1_ffn_ref(_layernorm(x, axis=-1), L1_ffn_weight, L1_ffn_lora_A, L1_ffn_lora_B, L1_ffn_gw1, L1_ffn_gb1, L1_ffn_ln_gamma, L1_ffn_ln_beta, L1_ffn_gw2, L1_ffn_gb2), axis=-1)
    return x

_drawn_inputs = setup_inputs


def setup_inputs(seed=0):
    import zlib

    import numpy as np

    out = dict(_drawn_inputs(seed))
    spreads = {'L0_attn_Wqk_b': (0.0, 0.8),
     'L0_attn_Wv_b': (0.0, 0.335),
     'L0_attn_Wo_b': (0.0, 0.1),
     'L1_ffn_gb1': (0.0, 0.8),
     'L1_ffn_ln_gamma': (1.0, 0.6),
     'L1_ffn_ln_beta': (0.0, 0.751),
     'L1_ffn_gb2': (0.0, 0.503)}
    factors = {'L0_attn_Wqk_w': 4.968,
     'L0_attn_Wv_w': 3.384,
     'L1_ffn_lora_A': 4.675,
     'L1_ffn_lora_B': 4.867,
     'L1_ffn_gw1': 5.822,
     'L1_ffn_gw2': 5.81}
    for name, (base, spread) in spreads.items():
        noise = np.random.default_rng([zlib.crc32(name.encode()), seed]).standard_normal(out[name].shape)
        drawn = base * np.exp(spread * noise) if base else spread * noise
        out[name] = jnp.asarray(drawn.astype(out[name].dtype))
    for name, factor in factors.items():
        out[name] = (out[name] * factor).astype(out[name].dtype)
    return out
```

```python
from contextlib import ExitStack

import numpy as np

import concourse.bass as bass
from concourse import mybir

F32, F32R, I32, U32 = mybir.dt.float32, mybir.dt.float32r, mybir.dt.int32, mybir.dt.uint32
ALU, ACT, AX = mybir.AluOpType, mybir.ActivationFunctionType, mybir.AxisListType

P = 128
BATCH, SEQ, D = 8, 256, 512
T = BATCH * SEQ
NT = T // P
KD = D // P
C, CT = 4, 4
CW = CT * P
CB = CW // SEQ
EPS = 1e-5

HEADS0, E0 = 8, 8
ROWS0 = 32

INNER, RANK = 1376, 32
NI = -(-INNER // P)
IP = NI * P
PIECE = IP // 4
Q_ZERO, Q_STEP, LR_SCALE = 7.5, 0.005, 0.02

KV, G, HD = 8, 4, 128
SCALE1 = HD ** -0.5
MASKED = -1e30

NE, ER = 8, 16
NH = 4 * NE
CAPACITY = int(3.0 * T / NE)


class Count:

    def __init__(self, sem, per=0):
        self.sem, self.per, self.base, self.n = sem, per, 0, 0

    def turn(self, c):
        self.base, self.n = c * self.per, 0

    def mark(self, ins):
        self.n += 1
        return ins.then_inc(self.sem, 1)

    def link(self, eng, ins):
        self.mark(ins)
        eng.wait_ge(self.sem, self.base + self.n)


def product(nc, out, lhs, rhs, start, stop):
    nc.tensor.matmul(out, lhs[0], rhs[0], start=start, stop=False)
    nc.tensor.matmul(out, lhs[0], rhs[1], start=False, stop=False)
    return nc.tensor.matmul(out, lhs[1], rhs[0], start=False, stop=stop)


def f32(ap):
    return ap.bitcast(F32)


class Constants:

    def __init__(self, nc, ctx, a):
        self.ident = ctx.enter_context(nc.sbuf_tensor("ident", [P, P], F32))
        self.masks = ctx.enter_context(nc.sbuf_tensor("masks", [P, 4], F32))
        self.minus_half = ctx.enter_context(nc.sbuf_tensor("minus_half", [P, CT], F32))
        self.ready = ctx.enter_context(nc.semaphore("consts_ready"))
        self.passed = {e.engine: ctx.enter_context(nc.semaphore(f"passed{i}")) for i, e in enumerate((nc.vector, nc.gpsimd, nc.tensor))}
        with nc.Block() as block:
            @block.sync
            def _(sp):
                sp.dma_start(self.ident[:], a.ident).then_inc(self.ready, 16)
                sp.dma_start(self.masks[:], a.masks).then_inc(self.ready, 16)
                sp.wait_ge(self.ready, 32)

            @block.gpsimd
            def _(pool):
                nc.gpsimd.memset(self.minus_half[:], -0.5)


class Signals:

    def __init__(self, nc, tag):
        self.nc, self.tag, self.made = nc, tag, []

    def sem(self, name):
        self.made.append(self.nc.alloc_semaphore(f"{self.tag}_{name}"))
        return self.made[-1]

    def clear(self):
        numbers = sorted(s.num for s in self.made)
        firsts = [x for x in numbers if x - 1 not in numbers]
        with self.nc.Block() as block:
            @block.sync
            def _(sp):
                for first in firsts:
                    stop = next(x for x in range(first, numbers[-1] + 2) if x not in numbers)
                    sp.sem_clear(range(first, stop))
        for s in self.made:
            self.nc.release_semaphore(s)


class Norm:

    def __init__(self, nc, ctx, signals, tag, xt_width=CW):
        def sb(name, shape, dt=F32):
            return ctx.enter_context(nc.sbuf_tensor(f"{signals.tag}_{tag}_{name}", shape, dt))

        def sem(name):
            return signals.sem(f"{tag}_{name}")

        self.raw = sb("raw", [P, CT, 6])
        self.stats = sb("stats", [P, CT, 2])
        self.rstd = sb("rstd", [P, CT])
        self.xn = sb("xn", [P, CT, D])
        if xt_width:
            self.xth, self.xtl = sb("xth", [P, KD, xt_width], F32R), sb("xtl", [P, KD, xt_width], F32R)
        self.raw_y = sb("raw_y", [P, CT, 6])
        self.stats_y = sb("stats_y", [P, CT, 2])
        self.rstd_y = sb("rstd_y", [P, CT])
        self.raw_done, self.stats_done, self.var_eps, self.rstd_done = sem("raw_done"), sem("stats_done"), sem("var_eps"), sem("rstd_done")
        self.rows_done, self.turned, self.hi_done, self.lo_done = sem("rows_done"), sem("turned"), sem("hi_done"), sem("lo_done")
        self.y_raw_done, self.y_stats_done, self.y_var_eps, self.y_rstd_done = sem("y_raw_done"), sem("y_stats_done"), sem("y_var_eps"), sem("y_rstd_done")
        self.y_rows_done, self.x_done = sem("y_rows_done"), sem("x_done")


def statistics(nc, eng, consts, raw, stats, raw_done, stats_done, rows, c):
    for t in range(CT):
        nc.vector.bn_stats(raw[:, t, :], rows(t)).then_inc(raw_done, 1)
    for t in range(CT):
        eng.wait_ge(raw_done, c * CT + t + 1)
        eng.sem_inc(consts.passed[eng.engine], 1)
        nc.vector.bn_aggr(stats[:, t, :], raw[:, t, :]).then_inc(stats_done, 1)


def inverse_deviation(nc, eng, consts, stats, rstd, stats_done, var_eps, rstd_done, c):
    eng.wait_ge(stats_done, (c + 1) * CT)
    eng.sem_inc(consts.passed[eng.engine], 1)
    nc.gpsimd.tensor_scalar(rstd[:, :], stats[:, :, 1], EPS, None, ALU.add).then_inc(var_eps, 1)
    eng.wait_ge(var_eps, c + 1)
    nc.gpsimd.tensor_tensor(rstd[:, :], rstd[:, :], consts.minus_half[:], ALU.pow).then_inc(rstd_done, 1)


def normalise(nc, eng, out, rows, stats, rstd, rstd_done, done, c):
    eng.wait_ge(rstd_done, c + 1)
    for t in range(CT):
        nc.vector.tensor_scalar(out[:, t, :], rows(t), stats[:, t, 0:1], rstd[:, t:t + 1],
                                ALU.subtract, ALU.mult).then_inc(done, 1)


def turn_rows(nc, eng, norm, consts, bank_of, c):
    eng.wait_ge(norm.rows_done, (c + 1) * CT)
    for k in range(KD):
        for t in range(CT):
            last = nc.tensor.transpose(bank_of(k)[:, t * P:(t + 1) * P], norm.xn[:, t, k * P:(k + 1) * P], consts.ident[:])
        last.then_inc(norm.turned, 1)


def residual(nc, eng, norm, X, c):
    for t in range(CT):
        eng.wait_ge(norm.y_rows_done, c * CT + t + 1)
        nc.gpsimd.tensor_tensor(X[:, c * CT + t, :], X[:, c * CT + t, :], norm.xn[:, t, :], ALU.add).then_inc(norm.x_done, 1)


def part1(nc, a, X, ffn, consts, banks):
    ctx, signals = ExitStack(), Signals(nc, "p1")
    with ctx:
        def sb(name, shape, dt=F32):
            return ctx.enter_context(nc.sbuf_tensor(f"p1_{name}", shape, dt))

        def sem(name):
            return signals.sem(name)

        M4 = 4
        NU, UNIT = 4 * CB * 2, 4
        VC = HEADS0 * E0
        n = Norm(nc, ctx, signals, "n")
        wqk_h, wqk_l = sb("wqk_h", [P, KD, M4 * P], F32R), sb("wqk_l", [P, KD, M4 * P], F32R)
        wv_h, wv_l = sb("wv_h", [P, KD, VC], F32R), sb("wv_l", [P, KD, VC], F32R)
        wo_h, wo_l = sb("wo_h", [VC, D], F32R), sb("wo_l", [VC, D], F32R)
        bqk, bv, bo = sb("bqk", [P, M4]), sb("bv", [P, VC]), sb("bo", [P, D])
        x_first, x_rest, w_in = sem("x_first"), sem("x_rest"), sem("w_in")
        w_hi, w_lo = sem("w_hi"), sem("w_lo")
        xv = a.x.rearrange("(t p) d -> p t d", p=P)

        with ExitStack() as raw_ctx:
            wqk_raw, wv_raw, wo_raw = (raw_ctx.enter_context(nc.sbuf_tensor(f"p1_{name}", shape, F32)) for name, shape in
                                       (("wqk_raw", [P, KD, M4 * P]), ("wv_raw", [P, KD, VC]), ("wo_raw", [VC, D])))
            block = raw_ctx.enter_context(nc.Block())

            @block.sync
            def _(sp):
                sp.dma_start(wqk_raw[:], a.wqk.rearrange("(k p) m -> p k m", p=P)).then_inc(w_in, 16)
                sp.dma_start(wv_raw[:], a.wv.rearrange("(k p) m -> p k m", p=P)).then_inc(w_in, 16)
                sp.dma_start(wo_raw[:], a.wo0).then_inc(w_in, 16)
                for dst, src in ((bqk[:], a.bqk),
                                 (bv[:], a.bv.rearrange("(o n) -> o n", o=1).to_broadcast([P, VC])),
                                 (bo[:], a.bo.rearrange("(o n) -> o n", o=1).to_broadcast([P, D]))):
                    sp.dma_start(dst, src).then_inc(w_in, 16)
                sp.dma_start(X[:, 0:CT, :], xv[:, 0:CT, :]).then_inc(x_first, 16)

            @block.scalar
            def _(act):
                act.wait_ge(w_in, 16 * 6)
                nc.scalar.copy(wqk_h[:], wqk_raw[:]).then_inc(w_hi, 1)
                nc.scalar.copy(wv_h[:], wv_raw[:]).then_inc(w_hi, 1)
                nc.scalar.copy(wo_h[:], wo_raw[:]).then_inc(w_hi, 1)

            @block.vector
            def _(dve):
                for i, (lo, raw, hi) in enumerate(((wqk_l, wqk_raw, wqk_h), (wv_l, wv_raw, wv_h), (wo_l, wo_raw, wo_h))):
                    dve.wait_ge(w_hi, i + 1)
                    nc.vector.tensor_tensor(lo[:], raw[:], f32(hi[:]), ALU.subtract).then_inc(w_lo, 1)

        qk32, qkh = sb("qk32", [P, 2, CW]), sb("qkh", [P, 2, CW], F32R)
        stack = sb("stack", [P, M4, CW], F32R)
        v32, v2 = sb("v32", [P, CT, VC]), sb("v2", [P, CT, HEADS0, 2 * E0], F32R)
        negmax, sums, rsums = sb("negmax", [P, NU, 2]), sb("sums", [P, 2 * CB, HEADS0]), sb("rsums", [P, 2 * CB, HEADS0])
        probs = sb("probs", [P, 3, 512])
        pth, ptl = sb("pth", [P, 3, 512], F32R), sb("ptl", [P, 3, 512], F32R)
        osum, on = sb("osum", [P, 2 * CB, VC]), sb("on", [P, 2 * CB, VC])
        oth, otl = qkh[0:VC, 0, :], qkh[0:VC, 1, :]
        q_raw = sb("q_raw", [P, 2, PIECE], I32)
        b_raw, b_hi = sb("b_raw", [P, D]), sb("b_hi", [P, D], F32R)

        q_in = [sem("q_in0"), sem("q_in1")]
        q_used, small_in, b_in, b_hi_done = sem("q_used"), sem("small_in"), sem("b_in"), sem("b_hi_done")
        qk_done, qk_hi, stacked = sem("qk_done"), sem("qk_hi"), sem("stacked")
        v_done, v_sum, v_hi, v_lo = sem("v_done"), sem("v_sum"), sem("v_hi"), sem("v_lo")
        scored, maxed, exped, pt_done, pt_hi, pt_lo, pv_done = (sem(x) for x in "scored maxed exped pt_done pt_hi pt_lo pv_done".split())
        o_chain, o_normed, ot_done, ot_hi, ot_lo = (sem(x) for x in "o_chain o_normed ot_done ot_hi ot_lo".split())
        wo_done, y_ready = sem("wo_done"), sem("y_ready")

        pieces = ffn.pieces

        block = ctx.enter_context(nc.Block())

        @block.sync
        def _(sp):
            sp.dma_start(X[:, CT:NT, :], xv[:, CT:NT, :]).then_inc(x_rest, 16)
            for dst, src in ffn.small:
                sp.dma_start(dst, src).then_inc(small_in, 16)
            for i, (dst, src) in enumerate(pieces):
                if i >= 2:
                    sp.wait_ge(q_used, i - 1)
                sp.dma_start(q_raw[:, i % 2, 0:src.shape[1]], src).then_inc(q_in[i % 2], 16)
            for i, (dst, src, w) in enumerate(ffn.stacks):
                if i >= 1:
                    sp.wait_ge(b_hi_done, 4 * i)
                sp.dma_start(b_raw[:, 0:w], src).then_inc(b_in, 16)
            sp.wait_ge(small_in, 16 * len(ffn.small))

        @block.gpsimd
        def _(pool):
            inverse_deviation(nc, pool, consts, n.stats, n.rstd, n.stats_done, n.var_eps, n.rstd_done, 0)
            for i, (dst, src) in enumerate(pieces):
                pool.wait_ge(q_in[i % 2], 16 * (i // 2 + 1))
                nc.gpsimd.tensor_scalar(dst, q_raw[:, i % 2, 0:src.shape[1]],
                                        -Q_ZERO, None, ALU.add).then_inc(q_used, 1)
            for i, (dst, src, w) in enumerate(ffn.stacks):
                pool.wait_ge(b_in, 16 * (i + 1))
                nc.gpsimd.tensor_scalar(b_raw[:, 0:w], b_raw[:, 0:w], LR_SCALE, None, ALU.mult).then_inc(b_hi_done, 1)
                pool.wait_ge(b_hi_done, 4 * i + 1)
                nc.gpsimd.tensor_copy(b_hi[:, 0:w], b_raw[:, 0:w]).then_inc(b_hi_done, 1)
                pool.wait_ge(b_hi_done, 4 * i + 2)
                nc.gpsimd.tensor_scalar(b_hi[:, 0:w], f32(b_hi[:, 0:w]), consts.masks[:, 2:3], None, ALU.mult).then_inc(b_hi_done, 1)
                pool.wait_ge(b_hi_done, 4 * i + 3)
                nc.gpsimd.tensor_tensor(dst, b_raw[:, 0:w], f32(b_hi[:, 0:w]), ALU.add).then_inc(b_hi_done, 1)
                pool.wait_ge(b_hi_done, 4 * i + 4)

            def turn(c, ahead):
                if ahead:
                    inverse_deviation(nc, pool, consts, n.stats, n.rstd, n.stats_done, n.var_eps, n.rstd_done, c + 1)
                inverse_deviation(nc, pool, consts, n.stats_y, n.rstd_y, n.y_stats_done, n.y_var_eps, n.y_rstd_done, c)
                residual(nc, pool, n, X, c)

            with nc.gpsimd.Fori(0, C - 1) as c:
                turn(c, True)
            turn(C - 1, False)

        @block.scalar
        def _(act):
            def hi_rows(c):
                for k in range(KD):
                    act.wait_ge(n.turned, c * KD + k + 1)
                    nc.scalar.copy(n.xth[:, k, :], banks[k][:]).then_inc(n.hi_done, 1)

            hi_rows(0)

            def turn(c, ahead):
                for m in range(M4):
                    act.wait_ge(qk_done, c * M4 + m + 1)
                    if m >= 2:
                        act.wait_ge(stacked, c * M4 + m - 1)
                    nc.scalar.activation(qk32[:, m % 2, :], banks[m][:], ACT.Identity, bias=bqk[:, m:m + 1])
                    nc.scalar.activation(qkh[:, m % 2, :], banks[m][:], ACT.Identity, bias=bqk[:, m:m + 1]).then_inc(qk_hi, 1)
                act.wait_ge(v_sum, c + 1)
                nc.scalar.copy(v2[:, :, :, 0:E0], v32[:].rearrange("p t (h e) -> p t h e", e=E0)).then_inc(v_hi, 1)
                for s in range(NU + 3):
                    if s < NU:
                        act.wait_ge(maxed, c * NU + s + 1)
                        if s >= 3:
                            act.wait_ge(pt_done, c * NU + s - 2)
                        for j in range(2):
                            nc.scalar.activation(probs[:, s % 3, j * SEQ:(j + 1) * SEQ], banks[s % 4][:, j * SEQ:(j + 1) * SEQ],
                                                 ACT.Exp, bias=negmax[:, s, j:j + 1],
                                                 accum_out=sums[:, s // 4, 4 * j + s % 4:4 * j + s % 4 + 1]).then_inc(exped, 1)
                    if s >= 3:
                        u = s - 3
                        act.wait_ge(pt_done, c * NU + u + 1)
                        if u >= 3:
                            act.wait_ge(pv_done, c * NU + u - 2)
                        nc.scalar.copy(pth[:, u % 3, :], banks[4 + u % 2][:]).then_inc(pt_hi, 1)
                if ahead:
                    hi_rows(c + 1)
                act.wait_ge(ot_done, c + 1)
                nc.scalar.copy(oth, banks[6][0:VC, :]).then_inc(ot_hi, 1)

            with nc.scalar.Fori(0, C - 1) as c:
                turn(c, True)
            turn(C - 1, False)

        @block.vector
        def _(dve):
            def lo_rows(c):
                for k in range(KD):
                    dve.wait_ge(n.hi_done, c * KD + k + 1)
                    nc.vector.tensor_tensor(n.xtl[:, k, :], banks[k][:], f32(n.xth[:, k, :]), ALU.subtract).then_inc(n.lo_done, 1)

            def rows(c):
                return lambda t: X[:, c * CT + t, :]

            dve.wait_ge(x_first, 16)
            statistics(nc, dve, consts, n.raw, n.stats, n.raw_done, n.stats_done, rows(0), 0)
            normalise(nc, dve, n.xn, rows(0), n.stats, n.rstd, n.rstd_done, n.rows_done, 0)
            lo_rows(0)
            dve.wait_ge(x_rest, 16)

            def turn(c, ahead):
                for m in range(M4):
                    dve.wait_ge(qk_hi, c * M4 + m + 1)
                    nc.vector.scalar_tensor_tensor(out=stack[:, m, :], in0=f32(qkh[:, m % 2, :]), scalar=consts.masks[:, m // 2:m // 2 + 1],
                                                   in1=qk32[:, m % 2, :], op0=ALU.mult, op1=ALU.add).then_inc(stacked, 1)
                dve.wait_ge(v_done, c + 1)
                nc.vector.tensor_tensor(v32[:], banks[7][:, 0:CT * VC].rearrange("p (t v) -> p t v", v=VC),
                                        bv[:].rearrange("p (o v) -> p o v", o=1).to_broadcast([P, CT, VC]), ALU.add).then_inc(v_sum, 1)
                dve.wait_ge(v_hi, c + 1)
                nc.vector.tensor_tensor(v2[:, :, :, E0:2 * E0], v32[:].rearrange("p t (h e) -> p t h e", e=E0),
                                        f32(v2[:, :, :, 0:E0]), ALU.subtract).then_inc(v_lo, 1)
                if ahead:
                    statistics(nc, dve, consts, n.raw, n.stats, n.raw_done, n.stats_done, rows(c + 1), c + 1)
                dve.wait_ge(n.x_done, c * CT)
                for s in range(NU + 8):
                    if s < NU:
                        dve.wait_ge(scored, c * NU + s + 1)
                        nc.vector.tensor_reduce(negmax[:, s, :], banks[s % 4][:].rearrange("p (j k) -> p j k", j=2), AX.X, ALU.max,
                                                negate=True).then_inc(maxed, 1)
                    if 3 <= s < NU + 3:
                        u = s - 3
                        dve.wait_ge(pt_hi, c * NU + u + 1)
                        nc.vector.tensor_tensor(ptl[:, u % 3, :], banks[4 + u % 2][:], f32(pth[:, u % 3, :]), ALU.subtract).then_inc(pt_lo, 1)
                    if s >= 10 and (s - 10) % 4 == 0:
                        g = (s - 10) // 4
                        dve.wait_ge(pv_done, c * NU + 4 * g + 4)
                        nc.vector.tensor_reduce(osum[:, g, :], banks[6 + g % 2][:, 0:2 * VC].rearrange("p (h s e) -> p h e s", s=2, e=E0),
                                                AX.X, ALU.add)
                        nc.vector.reciprocal(rsums[:, g, :], sums[:, g, :]).then_inc(o_chain, 1)
                        dve.wait_ge(o_chain, c * 2 * CB + g + 1)
                        nc.vector.scalar_tensor_tensor(out=on[:, g, :].rearrange("p (h e) -> p h e", e=E0),
                                                       in0=osum[:, g, :].rearrange("p (h e) -> p h e", e=E0), scalar=float((HEADS0 * E0) ** -0.5),
                                                       in1=rsums[:, g, :].rearrange("p (h o) -> p h o", o=1).to_broadcast([P, HEADS0, E0]),
                                                       op0=ALU.mult, op1=ALU.mult).then_inc(o_normed, 1)
                    if s == 8 and ahead:
                        normalise(nc, dve, n.xn, rows(c + 1), n.stats, n.rstd, n.rstd_done, n.rows_done, c + 1)
                if ahead:
                    lo_rows(c + 1)
                dve.wait_ge(ot_hi, c + 1)
                nc.vector.tensor_tensor(otl, banks[6][0:VC, :], f32(oth), ALU.subtract).then_inc(ot_lo, 1)
                for t in range(CT):
                    dve.wait_ge(wo_done, c * CT + t + 1)
                    nc.vector.tensor_tensor(n.xn[:, t, :], banks[4 + t % 2][:], bo[:], ALU.add).then_inc(y_ready, 1)
                dve.wait_ge(y_ready, (c + 1) * CT)
                statistics(nc, dve, consts, n.raw_y, n.stats_y, n.y_raw_done, n.y_stats_done, lambda t: n.xn[:, t, :], c)
                normalise(nc, dve, n.xn, lambda t: n.xn[:, t, :], n.stats_y, n.rstd_y, n.y_rstd_done, n.y_rows_done, c)

            with nc.vector.Fori(0, C - 1) as c:
                turn(c, True)
            turn(C - 1, False)

        @block.tensor
        def _(pe):
            turn_rows(nc, pe, n, consts, lambda k: banks[k], 0)

            def turn(c, ahead):
                pe.wait_ge(n.lo_done, (c + 1) * KD)
                for m in range(M4):
                    for k in range(KD):
                        last = product(nc, banks[m][:], (wqk_h[:, k, m * P:(m + 1) * P], wqk_l[:, k, m * P:(m + 1) * P]),
                                       (n.xth[:, k, :], n.xtl[:, k, :]), k == 0, k == KD - 1)
                    last.then_inc(qk_done, 1)
                for t in range(CT):
                    for k in range(KD):
                        last = product(nc, banks[7][:, t * VC:(t + 1) * VC], (n.xth[:, k, t * P:(t + 1) * P], n.xtl[:, k, t * P:(t + 1) * P]),
                                       (wv_h[:, k, :], wv_l[:, k, :]), k == 0, k == KD - 1)
                last.then_inc(v_done, 1)
                for s in range(NU + 5):
                    if s < NU:
                        b, qt, i = s // 8, (s // 4) % 2, s % 4
                        if s == 0:
                            pe.wait_ge(stacked, (c + 1) * M4)
                        if s >= 4:
                            pe.wait_ge(exped, 2 * (c * NU + s - 3))
                        r = slice(i * ROWS0, (i + 1) * ROWS0)
                        q0 = (b * 2 + qt) * P
                        for j in range(2):
                            last = nc.tensor.matmul(banks[i][:, j * SEQ:(j + 1) * SEQ], stack[r, j, q0:q0 + P],
                                                    stack[r, 2 + j, b * SEQ:(b + 1) * SEQ], start=True, stop=True)
                        last.then_inc(scored, 1)
                    if 3 <= s < NU + 3:
                        u = s - 3
                        pe.wait_ge(exped, 2 * (c * NU + u + 1))
                        if u >= 2:
                            pe.wait_ge(pt_lo, c * NU + u - 1)
                        for f in range(4):
                            last = nc.tensor.transpose(banks[4 + u % 2][:, f * P:(f + 1) * P], probs[:, u % 3, f * P:(f + 1) * P], consts.ident[:])
                        last.then_inc(pt_done, 1)
                    if s >= 5:
                        u = s - 5
                        b, i, g = u // 8, u % 4, u // 4
                        if u == 0:
                            pe.wait_ge(v_lo, c + 1)
                        pe.wait_ge(pt_lo, c * NU + u + 1)
                        if i == 0 and g >= 2:
                            pe.wait_ge(o_normed, c * 2 * CB + g - 1)
                        for j in range(2):
                            h = 4 * j + i
                            out = banks[6 + g % 2][:, h * 2 * E0:(h + 1) * 2 * E0]
                            for f in range(2):
                                nc.tensor.matmul(out, pth[:, u % 3, (2 * j + f) * P:(2 * j + f + 1) * P], v2[:, 2 * b + f, h, :],
                                                 start=f == 0, stop=False)
                            for f in range(2):
                                last = nc.tensor.matmul(out[:, 0:E0], ptl[:, u % 3, (2 * j + f) * P:(2 * j + f + 1) * P],
                                                        v2[:, 2 * b + f, h, 0:E0], start=False, stop=f == 1)
                        last.then_inc(pv_done, 1)
                if ahead:
                    turn_rows(nc, pe, n, consts, lambda k: banks[k], c + 1)
                pe.wait_ge(o_normed, (c + 1) * 2 * CB)
                pe.sem_inc(consts.passed[pe.engine], 1)
                for g in range(2 * CB):
                    last = nc.tensor.transpose(banks[6][0:VC, g * P:(g + 1) * P], on[:, g, :], consts.ident[:])
                last.then_inc(ot_done, 1)
                pe.wait_ge(ot_lo, c + 1)
                for t in range(CT):
                    if t >= 2:
                        pe.wait_ge(y_ready, c * CT + t - 1)
                    product(nc, banks[4 + t % 2][:], (oth[:, t * P:(t + 1) * P], otl[:, t * P:(t + 1) * P]),
                            (wo_h[:], wo_l[:]), True, True).then_inc(wo_done, 1)

            with nc.tensor.Fori(0, C - 1) as c:
                turn(c, True)
            turn(C - 1, False)
    signals.clear()


class FfnWeights:

    def __init__(self, nc, ctx, a):
        def sb(name, shape, dt=F32):
            return ctx.enter_context(nc.sbuf_tensor(f"ffn_{name}", shape, dt))

        self.gate, self.up, self.down = sb("gate", [P, KD, IP], F32R), sb("up", [P, KD, IP], F32R), sb("down", [P, NI, D], F32R)
        self.scales = sb("scales", [P, 2, NI])
        self.down_scale = sb("down_scale", [P, D])
        self.b_gate, self.b_up, self.b_down = sb("b_gate", [P, IP], F32R), sb("b_up", [P, IP], F32R), sb("b_down", [P, D], F32R)
        gq, uq, dq = (w.rearrange("(k p) n -> p k n", p=P) for w in (a.gate_q, a.up_q, a.down_q))
        self.pieces = [(w[:, k, s:s + PIECE], q[:, k, s:s + PIECE]) for k in range(KD) for s in range(0, IP, PIECE)
                       for w, q in ((self.gate, gq), (self.up, uq))]
        self.pieces += [(self.down[:, i, s:s + D // 2], dq[:, i, s:s + D // 2]) for i in range(NI) for s in (0, D // 2)]
        self.small = [(self.scales[:, 0, :], a.gate_scale),
                      (self.scales[:, 1, :], a.up_scale),
                      (self.down_scale[:], a.down_scale.rearrange("(o n) -> o n", o=1).to_broadcast([P, D]))]
        self.stacks = [(w[:, s:min(s + D, w.shape[1])], b[:, s:min(s + D, w.shape[1])], min(D, w.shape[1] - s)) for w, b in
                       ((self.b_gate, a.gate_B), (self.b_up, a.up_B), (self.b_down, a.down_B)) for s in range(0, w.shape[1], D)]


def part2(nc, a, X, ffn, consts, banks):
    ctx, signals = ExitStack(), Signals(nc, "p2")
    with ctx:
        def sb(name, shape, dt=F32):
            return ctx.enter_context(nc.sbuf_tensor(f"p2_{name}", shape, dt))

        def sem(name):
            return signals.sem(name)

        RING = 4
        BG, BU, BL, BR, BY = banks[0], banks[1], banks[2], banks[3], banks[4:8]
        ag_h, ag_l = sb("ag_h", [P, KD, P], F32R), sb("ag_l", [P, KD, P], F32R)
        au_h, au_l = sb("au_h", [P, KD, P], F32R), sb("au_l", [P, KD, P], F32R)
        ad_h, ad_l = sb("ad_h", [P, NI, P], F32R), sb("ad_l", [P, NI, P], F32R)
        a_in, a_hi, a_lo, scales_done = sem("a_in"), sem("a_hi"), sem("a_lo"), sem("scales_done")

        with ExitStack() as raw_ctx:
            raws = [raw_ctx.enter_context(nc.sbuf_tensor(f"p2_raw{i}", [P, k, P], F32)) for i, k in enumerate((KD, KD, NI))]
            block = raw_ctx.enter_context(nc.Block())

            @block.sync
            def _(sp):
                for raw, src in zip(raws, (a.gate_A, a.up_A, a.down_A)):
                    sp.dma_start(raw[:], src.rearrange("(k p) n -> p k n", p=P)).then_inc(a_in, 16)

            @block.scalar
            def _(act):
                act.wait_ge(a_in, 48)
                for raw, hi in zip(raws, (ag_h, au_h, ad_h)):
                    nc.scalar.copy(hi[:], raw[:]).then_inc(a_hi, 1)

            @block.vector
            def _(dve):
                nc.vector.tensor_scalar(ffn.scales[:], ffn.scales[:], Q_STEP, None, ALU.mult).then_inc(scales_done, 1)
                nc.vector.tensor_scalar(ffn.down_scale[:], ffn.down_scale[:], Q_STEP, None, ALU.mult).then_inc(scales_done, 1)
                for i, (raw, hi, lo) in enumerate(zip(raws, (ag_h, au_h, ad_h), (ag_l, au_l, ad_l))):
                    dve.wait_ge(a_hi, i + 1)
                    nc.vector.tensor_tensor(lo[:], raw[:], f32(hi[:]), ALU.subtract).then_inc(a_lo, 1)

        n = Norm(nc, ctx, signals, "n")
        r32, rh = sb("r32", [P, 2, CW]), sb("rh", [P, 2, CW], F32R)
        rstack = sb("rstack", [P, 3, CW], F32R)
        gu = sb("gu", [P, 2, 2, CW])
        hh, hl = sb("hh", [P, RING, CW], F32R), sb("hl", [P, RING, CW], F32R)
        (r_done, r_hi, r_stacked, main_done, rank_done, scaled, summed, silued, multiplied, h_hi, h_lo, down_done, rank_down_done,
         y_scaled, y_ready) = (sem(x) for x in "r_done r_hi r_stacked main_done rank_done scaled summed silued multiplied h_hi h_lo down_done rank_down_done y_scaled y_ready".split())

        block = ctx.enter_context(nc.Block())

        @block.gpsimd
        def _(pool):
            inverse_deviation(nc, pool, consts, n.stats, n.rstd, n.stats_done, n.var_eps, n.rstd_done, 0)

            def turn(c, ahead):
                for s in range(NI):
                    pool.wait_ge(silued, c * NI + s + 1)
                    pool.wait_ge(summed, c * 2 * NI + 2 * s + 2)
                    nc.gpsimd.tensor_tensor(gu[:, s % 2, 0, :], gu[:, s % 2, 0, :], gu[:, s % 2, 1, :], ALU.mult).then_inc(multiplied, 1)
                    if s == 4 and ahead:
                        inverse_deviation(nc, pool, consts, n.stats, n.rstd, n.stats_done, n.var_eps, n.rstd_done, c + 1)
                inverse_deviation(nc, pool, consts, n.stats_y, n.rstd_y, n.y_stats_done, n.y_var_eps, n.y_rstd_done, c)
                residual(nc, pool, n, X, c)

            with nc.gpsimd.Fori(0, C - 1) as c:
                turn(c, True)
            turn(C - 1, False)

        @block.scalar
        def _(act):
            def hi_rows(c):
                for k in range(KD):
                    act.wait_ge(n.turned, c * KD + k + 1)
                    nc.scalar.copy(n.xth[:, k, :], banks[k][:]).then_inc(n.hi_done, 1)

            def h_hi_of(c, s):
                act.wait_ge(multiplied, c * NI + s + 1)
                if s >= RING:
                    act.wait_ge(down_done, c * NI + s - RING + 1)
                nc.scalar.copy(hh[:, s % RING, :], gu[:, s % 2, 0, :]).then_inc(h_hi, 1)

            def r_hi_of(bank, slot):
                nc.scalar.copy(r32[:, slot, :], bank[:])
                nc.scalar.copy(rh[:, slot, :], bank[:]).then_inc(r_hi, 1)

            hi_rows(0)

            def turn(c, ahead):
                for m, bank in enumerate((BG, BU)):
                    act.wait_ge(r_done, c * 2 + m + 1)
                    r_hi_of(bank, m)
                for s in range(NI):
                    act.wait_ge(main_done, c * 2 * NI + 2 * s + 1)
                    if s >= 2:
                        act.wait_ge(h_lo, c * NI + s - 1)
                    nc.scalar.activation(gu[:, s % 2, 0, :], BG[:], ACT.Copy, scale=ffn.scales[:, 0, s:s + 1]).then_inc(scaled, 1)
                    if s >= 1:
                        h_hi_of(c, s - 1)
                    act.wait_ge(main_done, c * 2 * NI + 2 * s + 2)
                    nc.scalar.activation(gu[:, s % 2, 1, :], BU[:], ACT.Copy, scale=ffn.scales[:, 1, s:s + 1]).then_inc(scaled, 1)
                    act.wait_ge(summed, c * 2 * NI + 2 * s + 1)
                    nc.scalar.activation(gu[:, s % 2, 0, :], gu[:, s % 2, 0, :], ACT.Silu).then_inc(silued, 1)
                h_hi_of(c, NI - 1)
                act.wait_ge(down_done, (c + 1) * NI)
                r_hi_of(BR, 0)
                if ahead:
                    hi_rows(c + 1)

            with nc.scalar.Fori(0, C - 1) as c:
                turn(c, True)
            turn(C - 1, False)

        @block.vector
        def _(dve):
            def lo_rows(c):
                for k in range(KD):
                    dve.wait_ge(n.hi_done, c * KD + k + 1)
                    nc.vector.tensor_tensor(n.xtl[:, k, :], banks[k][:], f32(n.xth[:, k, :]), ALU.subtract).then_inc(n.lo_done, 1)

            def rows(c):
                return lambda t: X[:, c * CT + t, :]

            def h_lo_of(c, s):
                dve.wait_ge(h_hi, c * NI + s + 1)
                nc.vector.tensor_tensor(hl[:, s % RING, :], gu[:, s % 2, 0, :], f32(hh[:, s % RING, :]), ALU.subtract).then_inc(h_lo, 1)

            def r_stack_of(c, m, slot):
                dve.wait_ge(r_hi, c * 3 + m + 1)
                nc.vector.scalar_tensor_tensor(out=rstack[:, m, :], in0=f32(rh[:, slot, :]), scalar=consts.masks[:, 3:4],
                                               in1=r32[:, slot, :], op0=ALU.mult, op1=ALU.add).then_inc(r_stacked, 1)

            statistics(nc, dve, consts, n.raw, n.stats, n.raw_done, n.stats_done, rows(0), 0)
            normalise(nc, dve, n.xn, rows(0), n.stats, n.rstd, n.rstd_done, n.rows_done, 0)
            lo_rows(0)

            def turn(c, ahead):
                r_stack_of(c, 0, 0)
                r_stack_of(c, 1, 1)
                for s in range(NI):
                    for m in range(2):
                        dve.wait_ge(scaled, c * 2 * NI + 2 * s + m + 1)
                        dve.wait_ge(rank_done, c * 2 * NI + 2 * s + m + 1)
                        nc.vector.tensor_tensor(gu[:, s % 2, m, :], gu[:, s % 2, m, :], BL[:], ALU.add).then_inc(summed, 1)
                        if m == 0 and s >= 1:
                            h_lo_of(c, s - 1)
                    if s == 1 and ahead:
                        statistics(nc, dve, consts, n.raw, n.stats, n.raw_done, n.stats_done, rows(c + 1), c + 1)
                    if s == 7:
                        dve.wait_ge(n.x_done, c * CT)
                        if ahead:
                            normalise(nc, dve, n.xn, rows(c + 1), n.stats, n.rstd, n.rstd_done, n.rows_done, c + 1)
                h_lo_of(c, NI - 1)
                r_stack_of(c, 2, 0)
                if ahead:
                    lo_rows(c + 1)
                dve.wait_ge(down_done, (c + 1) * NI)
                for t in range(CT):
                    nc.vector.tensor_tensor(n.xn[:, t, :], BY[t][:], ffn.down_scale[:], ALU.mult).then_inc(y_scaled, 1)
                for t in range(CT):
                    dve.wait_ge(y_scaled, c * CT + t + 1)
                    dve.wait_ge(rank_down_done, c * CT + t + 1)
                    nc.vector.tensor_tensor(n.xn[:, t, :], n.xn[:, t, :], banks[t][:], ALU.add).then_inc(y_ready, 1)
                dve.wait_ge(y_ready, (c + 1) * CT)
                statistics(nc, dve, consts, n.raw_y, n.stats_y, n.y_raw_done, n.y_stats_done, lambda t: n.xn[:, t, :], c)
                normalise(nc, dve, n.xn, lambda t: n.xn[:, t, :], n.stats_y, n.rstd_y, n.y_rstd_done, n.y_rows_done, c)

            with nc.vector.Fori(0, C - 1) as c:
                turn(c, True)
            turn(C - 1, False)

        @block.tensor
        def _(pe):
            turn_rows(nc, pe, n, consts, lambda k: banks[k], 0)

            def main(bank, w, s):
                for k in range(KD):
                    nc.tensor.matmul(bank[:], w[:, k, s * P:(s + 1) * P], n.xth[:, k, :], start=k == 0, stop=False)
                    last = nc.tensor.matmul(bank[:], w[:, k, s * P:(s + 1) * P], n.xtl[:, k, :], start=False, stop=k == KD - 1)
                return last

            def turn(c, ahead):
                pe.wait_ge(y_ready, c * CT)
                pe.wait_ge(n.lo_done, (c + 1) * KD)
                for bank, hi, lo in ((BG, ag_h, ag_l), (BU, au_h, au_l)):
                    for k in range(KD):
                        last = product(nc, bank[:], (hi[:, k, :], lo[:, k, :]), (n.xth[:, k, :], n.xtl[:, k, :]), k == 0, k == KD - 1)
                    last.then_inc(r_done, 1)
                for s in range(NI + 2):
                    if s < NI:
                        for m, (bank, w, b) in enumerate(((BG, ffn.gate, ffn.b_gate), (BU, ffn.up, ffn.b_up))):
                            if s == 0:
                                pe.wait_ge(r_stacked, c * 3 + m + 1)
                            else:
                                pe.wait_ge(scaled, c * 2 * NI + 2 * s + m - 1)
                            main(bank, w, s).then_inc(main_done, 1)
                            pe.wait_ge(summed, c * 2 * NI + 2 * s + m)
                            nc.tensor.matmul(BL[:], b[:, s * P:(s + 1) * P], rstack[:, m, :], start=True, stop=True).then_inc(rank_done, 1)
                    if s >= 2:
                        j = s - 2
                        if j == 0:
                            pe.wait_ge(y_scaled, c * CT)
                        pe.wait_ge(h_lo, c * NI + j + 1)
                        for t in range(CT):
                            tok = slice(t * P, (t + 1) * P)
                            nc.tensor.matmul(BY[t][:], hh[:, j % RING, tok], ffn.down[:, j, :], start=j == 0, stop=False)
                            nc.tensor.matmul(BY[t][:], hl[:, j % RING, tok], ffn.down[:, j, :], start=False, stop=j == NI - 1)
                        last = product(nc, BR[:], (ad_h[:, j, :], ad_l[:, j, :]), (hh[:, j % RING, :], hl[:, j % RING, :]), j == 0, j == NI - 1)
                        last.then_inc(down_done, 1)
                if ahead:
                    pe.wait_ge(r_stacked, c * 3 + 3)
                    turn_rows(nc, pe, n, consts, lambda k: banks[k], c + 1)
                pe.wait_ge(r_stacked, c * 3 + 3)
                for t in range(CT):
                    if ahead:
                        pe.wait_ge(n.lo_done, (c + 1) * KD + t + 1)
                    nc.tensor.matmul(banks[t][:], rstack[:, 2, t * P:(t + 1) * P], ffn.b_down[:], start=True, stop=True).then_inc(rank_down_done, 1)

            with nc.tensor.Fori(0, C - 1) as c:
                turn(c, True)
            turn(C - 1, False)
    signals.clear()


def part3(nc, a, X, consts, banks):
    ctx, signals = ExitStack(), Signals(nc, "p3")
    with ctx:
        def sb(name, shape, dt=F32):
            return ctx.enter_context(nc.sbuf_tensor(f"p3_{name}", shape, dt))

        def sem(name):
            return signals.sem(name)

        GW = G * HD
        NM = 1 + G
        NJ = NM + 1
        NU = G * CB
        NW = 3 * CB
        NV = 2 * CB
        UW = 3 * P
        SECOND, FIRST = slice(0, 2 * P), slice(2 * P, 3 * P)

        parked_done, x_back = sem("parked_done"), sem("x_back")
        tables_in, q_raw_in, o_raw_in, w_split, qkv_split, o_split = (sem(x) for x in "tables_in q_raw_in o_raw_in w_split qkv_split o_split".split())
        with ExitStack() as mid_ctx:
            def mid(name, shape, dt=F32):
                return mid_ctx.enter_context(nc.sbuf_tensor(f"p3_{name}", shape, dt))

            xth, xtl = mid("xth", [P, KD, T], F32R), mid("xtl", [P, KD, T], F32R)
            wq_h, wq_l = mid("wq_h", [P, KD, GW], F32R), mid("wq_l", [P, KD, GW], F32R)
            wk_h, wk_l = mid("wk_h", [P, KD, HD], F32R), mid("wk_l", [P, KD, HD], F32R)
            wv_h, wv_l = mid("wv_h", [P, KD, HD], F32R), mid("wv_l", [P, KD, HD], F32R)
            wo_h, wo_l = mid("wo_h", [P, G, D], F32R), mid("wo_l", [P, G, D], F32R)
            raw = mid("raw", [P, KD, GW])
            raw_k, raw_v = mid("raw_k", [P, KD, HD]), mid("raw_v", [P, KD, HD])
            cos, sin = mid("cos", [P, SEQ]), mid("sin", [P, SEQ])
            window = mid("window", [P, 2 * P])

            wq_g, wk_g, wv_g = (w.rearrange("(k p) n -> p k n", p=P) for w in (a.wq1, a.wk1, a.wv1))
            wo_g = a.wo1.rearrange("(h p) n -> p h n", p=P)

            def split_qkv(pool, g):
                pool.wait_ge(q_raw_in, g * 48 + 48)
                pool.sem_inc(consts.passed[pool.engine], 1)
                for i, (r, hi, lo) in enumerate(((raw, wq_h, wq_l), (raw_k, wk_h, wk_l), (raw_v, wv_h, wv_l))):
                    nc.gpsimd.tensor_copy(hi[:], r[:]).then_inc(w_split, 1)
                    pool.wait_ge(w_split, g * 4 + i + 1)
                    nc.gpsimd.tensor_tensor(lo[:], r[:], f32(hi[:]), ALU.subtract).then_inc(qkv_split, 1)

            def split_o(pool, g):
                pool.wait_ge(o_raw_in, g * 16 + 16)
                pool.sem_inc(consts.passed[pool.engine], 1)
                nc.gpsimd.tensor_copy(wo_h[:], raw[:]).then_inc(w_split, 1)
                pool.wait_ge(w_split, g * 4 + 4)
                nc.gpsimd.tensor_tensor(wo_l[:], raw[:], f32(wo_h[:]), ALU.subtract).then_inc(o_split, 1)

            def load_qkv(sp, g):
                sp.dma_start(raw[:], wq_g[:, :, bass.ds(g * GW, GW)]).then_inc(q_raw_in, 16)
                sp.dma_start(raw_k[:], wk_g[:, :, bass.ds(g * HD, HD)]).then_inc(q_raw_in, 16)
                sp.dma_start(raw_v[:], wv_g[:, :, bass.ds(g * HD, HD)]).then_inc(q_raw_in, 16)

            with ExitStack() as pre_ctx:
                pre = [Norm(nc, pre_ctx, signals, f"n{i}", xt_width=0) for i in range(2)]
                block = pre_ctx.enter_context(nc.Block())

                @block.sync
                def _(sp):
                    load_qkv(sp, 0)
                    sp.dma_start(a.parked.rearrange("(t p) d -> p t d", p=P), X[:]).then_inc(parked_done, 16)
                    sp.dma_start(cos[:], a.cos).then_inc(tables_in, 16)
                    sp.dma_start(sin[:], a.sin).then_inc(tables_in, 16)
                    sp.dma_start(window[:], a.window).then_inc(tables_in, 16)

                @block.gpsimd
                def _(pool):
                    for c in range(C):
                        n = pre[c % 2]
                        inverse_deviation(nc, pool, consts, n.stats, n.rstd, n.stats_done, n.var_eps, n.rstd_done, c // 2)
                    split_qkv(pool, 0)

                @block.scalar
                def _(act):
                    for c in range(C):
                        n = pre[c % 2]
                        for k in range(KD):
                            act.wait_ge(n.turned, c // 2 * KD + k + 1)
                            nc.scalar.copy(xth[:, k, c * CW:(c + 1) * CW], banks[4 * (c % 2) + k][:]).then_inc(n.hi_done, 1)

                @block.vector
                def _(dve):
                    def lo_rows(c):
                        n = pre[c % 2]
                        for k in range(KD):
                            dve.wait_ge(n.hi_done, c // 2 * KD + k + 1)
                            cols = slice(c * CW, (c + 1) * CW)
                            nc.vector.tensor_tensor(xtl[:, k, cols], banks[4 * (c % 2) + k][:], f32(xth[:, k, cols]), ALU.subtract).then_inc(n.lo_done, 1)

                    for c in range(C + 1):
                        if c < C:
                            n = pre[c % 2]
                            if c >= 2:
                                dve.wait_ge(n.turned, KD)
                            statistics(nc, dve, consts, n.raw, n.stats, n.raw_done, n.stats_done, lambda t: X[:, c * CT + t, :], c // 2)
                            normalise(nc, dve, n.xn, lambda t: X[:, c * CT + t, :], n.stats, n.rstd, n.rstd_done, n.rows_done, c // 2)
                        if c >= 1:
                            lo_rows(c - 1)

                @block.tensor
                def _(pe):
                    for c in range(C):
                        n = pre[c % 2]
                        if c >= 2:
                            pe.wait_ge(n.lo_done, KD)
                        turn_rows(nc, pe, n, consts, lambda k: banks[4 * (c % 2) + k], c // 2)

            qh, ql = mid("qh", [P, G, CW], F32R), mid("ql", [P, G, CW], F32R)
            kh, kl = mid("kh", [P, CW], F32R), mid("kl", [P, CW], F32R)
            vh, vl = mid("vh", [P, CT, HD], F32R), mid("vl", [P, CT, HD], F32R)
            swap, turn_cos = mid("swap", [P, 2, CW]), mid("turn_cos", [P, 2, CW])
            probs = mid("probs", [P, NU, UW])
            top, neg, sums, rsums = (mid(x, [P, NU, 2]) for x in ("top", "neg", "sums", "rsums"))
            pth, ptl = mid("pth", [P, 2, G * P], F32R), mid("ptl", [P, 2, G * P], F32R)
            oth, otl = mid("oth", [P, G, CW], F32R), mid("otl", [P, G, CW], F32R)
            (cleared, proj_done, swapped, cosed, sined, rotated, rot_hi, rot_lo, v_hi, v_lo, scored, masked, negated, exped, inverted, normed,
             pt_done, pt_hi, pt_lo, pv_done, o_hi, o_lo, wo_done, y_added) = (sem(x) for x in (
                 "cleared proj_done swapped cosed sined rotated rot_hi rot_lo v_hi v_lo scored masked negated exped inverted normed "
                 "pt_done pt_hi pt_lo pv_done o_hi o_lo wo_done y_added").split())

            def wait(eng, sem, value):
                if not isinstance(value, int) or value > 0:
                    eng.wait_ge(sem, value)

            def groups(eng, item, last):
                item(0, 0)
                with eng.Fori(0, KV - 1) as g:
                    for c in range(1, C):
                        item(g, c)
                    item(g + 1, 0)
                for c in range(1, C):
                    item(KV - 1, c)
                last()

            block = mid_ctx.enter_context(nc.Block())

            @block.sync
            def _(sp):
                sp.wait_ge(parked_done, 16)

                def item(g, c):
                    if c == 0:
                        sp.wait_ge(qkv_split, g * 3 + 3)
                        sp.dma_start(raw[:], wo_g[:, bass.ds(g * G, G), :]).then_inc(o_raw_in, 16)
                    if c == 1 and not (isinstance(g, int) and g == KV - 1):
                        sp.wait_ge(o_split, g + 1)
                        load_qkv(sp, g + 1)

                groups(nc.sync, item, lambda: None)

            @block.gpsimd
            def _(pool):
                pool.wait_ge(parked_done, 16)
                pool.wait_ge(tables_in, 48)
                nc.gpsimd.memset(X[:], 0.0).then_inc(cleared, 1)

                def item(g, c):
                    n = g * C + c
                    for m in range(NM):
                        par = (c + m) % 2
                        shape = [P, CB, SEQ]
                        wait(pool, swapped, n * NM + m + 1)
                        nc.gpsimd.tensor_tensor(swap[:, par, :].rearrange("p (b s) -> p b s", b=CB), swap[:, par, :].rearrange("p (b s) -> p b s", b=CB),
                                                sin[:].rearrange("p (o s) -> p o s", o=1).to_broadcast(shape), ALU.mult).then_inc(sined, 1)
                        wait(pool, cosed, n * NM + m + 1)
                        wait(pool, sined, n * NM + m + 1)
                        nc.gpsimd.tensor_tensor(turn_cos[:, par, :], turn_cos[:, par, :], swap[:, par, :], ALU.add).then_inc(rotated, 1)
                    if c == 0:
                        wait(pool, wo_done, n * CT)
                        split_o(pool, g)
                    if c == C - 1 and not (isinstance(g, int) and g == KV - 1):
                        pool.wait_ge(proj_done, (n + 1) * NJ)
                        split_qkv(pool, g + 1)

                groups(nc.gpsimd, item, lambda: None)

            @block.scalar
            def _(act):
                half = HD // 2

                def item(g, c):
                    n = g * C + c
                    for m in range(NM + 1):
                        if m < NM:
                            par = (c + m) % 2
                            wait(act, proj_done, n * NJ + m + 1)
                            wait(act, rotated, n * NM + m - 1)
                            nc.scalar.copy(swap[0:half, par, :], banks[m % 2][half:HD, :])
                            nc.scalar.copy(swap[half:HD, par, :], banks[m % 2][0:half, :]).then_inc(swapped, 1)
                        if m >= 1:
                            par = (c + m - 1) % 2
                            wait(act, rotated, n * NM + m)
                            nc.scalar.copy(kh[:] if m == 1 else qh[:, m - 2, :], turn_cos[:, par, :]).then_inc(rot_hi, 1)
                    wait(act, proj_done, (n + 1) * NJ)
                    nc.scalar.copy(vh[:].rearrange("p t d -> p (t d)"), banks[1][:]).then_inc(v_hi, 1)
                    for u in range(NU):
                        wait(act, negated, n * NU + u + 1)
                        for q, cols in enumerate((FIRST, SECOND)):
                            nc.scalar.activation(probs[:, u, cols], probs[:, u, cols], ACT.Exp, bias=neg[:, u, q:q + 1], scale=SCALE1,
                                                 accum_out=sums[:, u, q:q + 1]).then_inc(exped, 1)
                    for w in range(NW):
                        wait(act, pt_done, n * NW + w + 1)
                        wait(act, pv_done, n * NW + w - 1)
                        nc.scalar.copy(pth[:, w % 2, :], banks[4 + w % 2][:]).then_inc(pt_hi, 1)
                        if w % 3 == 2:
                            b = w // 3
                            for q in range(2):
                                wait(act, pv_done, n * NW + 3 * b + (1, 3)[q])
                                tok = slice(b * SEQ + q * P, b * SEQ + (q + 1) * P)
                                nc.scalar.copy(oth[:, :, tok], banks[6 + q][:].rearrange("p (h t) -> p h t", h=G)).then_inc(o_hi, 1)

                groups(nc.scalar, item, lambda: None)

            @block.vector
            def _(dve):
                def add_result(n, c):
                    for t in range(CT):
                        wait(dve, wo_done, n * CT + t + 1)
                        nc.vector.tensor_tensor(X[:, c * CT + t, :], X[:, c * CT + t, :], banks[6 + t % 2][:], ALU.add).then_inc(y_added, 1)

                def item(g, c):
                    n = g * C + c
                    for m in range(NM + 1):
                        if m < NM:
                            par = (c + m) % 2
                            wait(dve, swapped, n * NM + m + 1)
                            wait(dve, rot_lo, n * NM + m - 1)
                            nc.vector.tensor_tensor(turn_cos[:, par, :].rearrange("p (b s) -> p b s", b=CB),
                                                    banks[m % 2][:].rearrange("p (b s) -> p b s", b=CB),
                                                    cos[:].rearrange("p (o s) -> p o s", o=1).to_broadcast([P, CB, SEQ]), ALU.mult).then_inc(cosed, 1)
                        if m >= 1:
                            par = (c + m - 1) % 2
                            wait(dve, rot_hi, n * NM + m)
                            hi, lo = (kh[:], kl[:]) if m == 1 else (qh[:, m - 2, :], ql[:, m - 2, :])
                            nc.vector.tensor_tensor(lo, turn_cos[:, par, :], f32(hi), ALU.subtract).then_inc(rot_lo, 1)
                    wait(dve, v_hi, n + 1)
                    nc.vector.tensor_tensor(vl[:].rearrange("p t d -> p (t d)"), banks[1][:], f32(vh[:].rearrange("p t d -> p (t d)")), ALU.subtract).then_inc(v_lo, 1)
                    for u in range(NU + 1):
                        if u < NU:
                            wait(dve, scored, n * NU + u + 1)
                            dve.sem_inc(consts.passed[dve.engine], 1)
                            bank = banks[2 + u % 2]
                            for q, (cols, win) in enumerate(((FIRST, window[:, P:2 * P]), (SECOND, window[:]))):
                                nc.vector.tensor_tensor_reduce(out=probs[:, u, cols], in0=bank[:, cols], in1=win, scale=1.0, scalar=4 * MASKED,
                                                               op0=ALU.add, op1=ALU.max, accum_out=top[:, u, q:q + 1]).then_inc(masked, 1)
                            wait(dve, masked, 2 * (n * NU + u + 1))
                            nc.vector.tensor_scalar(neg[:, u, :], top[:, u, :], -SCALE1, None, ALU.mult).then_inc(negated, 1)
                        if u >= 1:
                            wait(dve, exped, 2 * (n * NU + u))
                            nc.vector.reciprocal(rsums[:, u - 1, :], sums[:, u - 1, :]).then_inc(inverted, 1)
                            wait(dve, inverted, n * NU + u)
                            for q, cols in enumerate((FIRST, SECOND)):
                                nc.vector.tensor_scalar(probs[:, u - 1, cols], probs[:, u - 1, cols], rsums[:, u - 1, q:q + 1], None, ALU.mult).then_inc(normed, 1)
                    if not (isinstance(n, int) and n == 0):
                        add_result(n - 1, (c - 1) % C)
                    for w in range(NW):
                        wait(dve, pt_hi, n * NW + w + 1)
                        nc.vector.tensor_tensor(ptl[:, w % 2, :], banks[4 + w % 2][:], f32(pth[:, w % 2, :]), ALU.subtract).then_inc(pt_lo, 1)
                        if w % 3 == 2:
                            b = w // 3
                            for q in range(2):
                                wait(dve, o_hi, n * NV + 2 * b + q + 1)
                                tok = slice(b * SEQ + q * P, b * SEQ + (q + 1) * P)
                                nc.vector.tensor_tensor(otl[:, :, tok], banks[6 + q][:].rearrange("p (h t) -> p h t", h=G),
                                                        f32(oth[:, :, tok]), ALU.subtract).then_inc(o_lo, 1)

                dve.wait_ge(tables_in, 48)
                dve.wait_ge(cleared, 1)
                groups(nc.vector, item, lambda: add_result(KV * C - 1, C - 1))

            @block.tensor
            def _(pe):
                def output(n):
                    wait(pe, o_lo, (n + 1) * NV)
                    for t in range(CT):
                        if t == 0:
                            wait(pe, o_split, out_group)
                        if t >= 2:
                            wait(pe, y_added, n * CT + t - 1)
                        for h in range(G):
                            tok = slice(t * P, (t + 1) * P)
                            last = product(nc, banks[6 + t % 2][:], (oth[:, h, tok], otl[:, h, tok]), (wo_h[:, h, :], wo_l[:, h, :]), h == 0, h == G - 1)
                        last.then_inc(wo_done, 1)

                def item(g, c):
                    nonlocal out_group
                    n = g * C + c
                    cols = slice(c * CW, (c + 1) * CW)
                    if c == 0:
                        wait(pe, qkv_split, g * 3 + 3)
                    for m in range(NM):
                        if m == 1:
                            wait(pe, v_lo, n)
                        else:
                            wait(pe, swapped, n * NM + m - (m > 0))
                            wait(pe, cosed, n * NM + m - (m > 0))
                        for k in range(KD):
                            w = (wk_h[:, k, :], wk_l[:, k, :]) if m == 0 else tuple(x[:, k, (m - 1) * HD:m * HD] for x in (wq_h, wq_l))
                            last = product(nc, banks[m % 2][:], w, (xth[:, k, cols], xtl[:, k, cols]), k == 0, k == KD - 1)
                        last.then_inc(proj_done, 1)
                    wait(pe, swapped, n * NM + NM - 1)
                    wait(pe, cosed, n * NM + NM - 1)
                    for t in range(CT):
                        tok = slice(c * CW + t * P, c * CW + (t + 1) * P)
                        for k in range(KD):
                            last = product(nc, banks[1][:, t * HD:(t + 1) * HD], (xth[:, k, tok], xtl[:, k, tok]),
                                           (wv_h[:, k, :], wv_l[:, k, :]), k == 0, k == KD - 1)
                    last.then_inc(proj_done, 1)
                    for u in range(NU):
                        h, b = u // CB, u % CB
                        if b == 0:
                            wait(pe, rot_lo, n * NM + h + 2)
                        wait(pe, masked, 2 * (n * NU + u - 1))
                        bank, s0 = banks[2 + u % 2], b * SEQ
                        product(nc, bank[:, FIRST], (qh[:, h, s0:s0 + P], ql[:, h, s0:s0 + P]), (kh[:, s0:s0 + P], kl[:, s0:s0 + P]), True, True)
                        product(nc, bank[:, SECOND], (qh[:, h, s0 + P:s0 + SEQ], ql[:, h, s0 + P:s0 + SEQ]),
                                (kh[:, s0:s0 + SEQ], kl[:, s0:s0 + SEQ]), True, True).then_inc(scored, 1)
                    if not (isinstance(n, int) and n == 0):
                        out_group = g if c == 0 else g + 1
                        output(n - 1)
                    for w in range(NW + 1):
                        if w < NW:
                            b, part = w // 3, (2, 0, 1)[w % 3]
                            if w % 3 == 0:
                                wait(pe, normed, 2 * n * NU + 2 * ((G - 1) * CB + b + 1))
                            wait(pe, pt_lo, n * NW + w - 1)
                            for h in range(G):
                                last = nc.tensor.transpose(banks[4 + w % 2][:, h * P:(h + 1) * P], probs[:, h * CB + b, part * P:(part + 1) * P], consts.ident[:])
                            last.then_inc(pt_done, 1)
                        if w >= 1:
                            x = w - 1
                            b, part = x // 3, x % 3
                            q, kt = (0, 0) if part == 0 else (1, part - 1)
                            if x == 0:
                                wait(pe, v_lo, n + 1)
                                wait(pe, y_added, n * CT)
                            if part < 2 and b == 1:
                                wait(pe, o_lo, n * NV + q + 1)
                            wait(pe, pt_lo, n * NW + x + 1)
                            last = product(nc, banks[6 + q][:], (vh[:, 2 * b + kt, :], vl[:, 2 * b + kt, :]), (pth[:, x % 2, :], ptl[:, x % 2, :]),
                                           part < 2, part != 1)
                            last.then_inc(pv_done, 1)

                out_group = 0

                def last():
                    output(KV * C - 1)

                groups(nc.tensor, item, last)

        n = Norm(nc, ctx, signals, "ny", xt_width=0)
        xr = sb("xr", [P, NT, D])
        block = ctx.enter_context(nc.Block())

        @block.sync
        def _(sp):
            sp.dma_start(xr[:], a.parked.rearrange("(t p) d -> p t d", p=P)).then_inc(x_back, 16)

        @block.gpsimd
        def _(pool):
            pool.wait_ge(x_back, 16)
            for c in range(C):
                inverse_deviation(nc, pool, consts, n.stats_y, n.rstd_y, n.y_stats_done, n.y_var_eps, n.y_rstd_done, c)
                for t in range(CT):
                    pool.wait_ge(n.y_rows_done, c * CT + t + 1)
                    nc.gpsimd.tensor_tensor(X[:, c * CT + t, :], xr[:, c * CT + t, :], n.xn[:, t, :], ALU.add).then_inc(n.x_done, 1)

        @block.vector
        def _(dve):
            for c in range(C):
                def rows(t):
                    return X[:, c * CT + t, :]
                statistics(nc, dve, consts, n.raw_y, n.stats_y, n.y_raw_done, n.y_stats_done, rows, c)
                if c >= 1:
                    dve.wait_ge(n.x_done, c * CT)
                normalise(nc, dve, n.xn, rows, n.stats_y, n.rstd_y, n.y_rstd_done, n.y_rows_done, c)
    signals.clear()


def part4(nc, a, X, out, consts, banks):
    ctx, signals = ExitStack(), Signals(nc, "p4")
    with ctx:
        def sb(name, shape, dt=F32):
            return ctx.enter_context(nc.sbuf_tensor(f"p4_{name}", shape, dt))

        sem = signals.sem
        ER_ALL = NE * ER
        CATW = ER_ALL + NH
        BCAT, BDENSE, BGATE, BLORA = banks[4], banks[5:7], banks[7], banks[4:7]
        w_in, w_hi, w_lo, ones_set = sem("w_in"), sem("w_hi"), sem("w_lo"), sem("ones_set")
        cat_h, cat_l = sb("cat_h", [P, KD, CATW], F32R), sb("cat_l", [P, KD, CATW], F32R)
        dense_h, dense_l = sb("dense_h", [P, KD, D], F32R), sb("dense_l", [P, KD, D], F32R)
        lb_h, lb_l = sb("lb_h", [ER_ALL, D], F32R), sb("lb_l", [ER_ALL, D], F32R)
        gw2 = sb("gw2", [P, CT * NE])
        gb1, gamma, beta, gb2, experts = sb("gb1", [P, NH]), sb("gamma", [P, NH]), sb("beta", [P, NH]), sb("gb2", [P, NE]), sb("experts", [P, NE])
        ones = sb("ones", [P, P])
        pre = [Norm(nc, ctx, signals, f"n{i}", xt_width=0) for i in range(2)]
        xth, xtl = sb("xth", [P, KD, T], F32R), sb("xtl", [P, KD, T], F32R)
        y = sb("y", [P, NT, D])
        low = sb("low", [P, NT, ER_ALL])
        hidden = sb("hidden", [P, 2, CT, NH])
        h_raw, h_stats, h_rstd = sb("h_raw", [P, CT, 6]), sb("h_stats", [P, CT, 2]), sb("h_rstd", [P, CT])
        hidden_t = sb("hidden_t", [P, P])
        gates, top, where, where_f = sb("gates", [P, CT, NE]), sb("top", [P, CT, 8]), sb("where", [P, CT, 8], U32), sb("where_f", [P, CT, 8])
        second, share = sb("second", [P, CT]), sb("share", [P, NT, 2])
        chosen = sb("chosen", [P, NT, 2, NE])
        allowed, part, weight = sb("allowed", [P, 2, NE]), sb("part", [P, 2, NT, NE]), sb("weight", [P, NT, NE])
        scaled = sb("scaled", [P, 3, ER_ALL])
        sth, stl = sb("sth", [P, 3, P], F32R), sb("stl", [P, 3, P], F32R)

        with ExitStack() as raw_ctx:
            cat_raw, dense_raw, lb_raw = (raw_ctx.enter_context(nc.sbuf_tensor(f"p4_{name}", shape, F32)) for name, shape in
                                          (("cat_raw", [P, KD, CATW]), ("dense_raw", [P, KD, D]), ("lb_raw", [ER_ALL, D])))
            block = raw_ctx.enter_context(nc.Block())

            @block.sync
            def _(sp):
                sp.dma_start(cat_raw[:, :, 0:ER_ALL], a.lora_A.rearrange("(k p) n -> p k n", p=P)).then_inc(w_in, 16)
                sp.dma_start(cat_raw[:, :, ER_ALL:CATW], a.gw1.rearrange("(k p) n -> p k n", p=P)).then_inc(w_in, 16)
                sp.dma_start(dense_raw[:], a.dense.rearrange("(k p) n -> p k n", p=P)).then_inc(w_in, 16)
                sp.dma_start(lb_raw[:], a.lora_B).then_inc(w_in, 16)
                sp.dma_start(gw2[:], a.gw2).then_inc(w_in, 16)
                sp.dma_start(experts[:], a.experts).then_inc(w_in, 16)
                for dst, src, w in ((gb1, a.gb1, NH), (gamma, a.ln_gamma, NH), (beta, a.ln_beta, NH), (gb2, a.gb2, NE)):
                    sp.dma_start(dst[:], src.rearrange("(o n) -> o n", o=1).to_broadcast([P, w])).then_inc(w_in, 16)

            @block.gpsimd
            def _(pool):
                nc.gpsimd.memset(ones[:], 1.0).then_inc(ones_set, 1)

            @block.scalar
            def _(act):
                act.wait_ge(w_in, 160)
                for hi, raw in ((cat_h, cat_raw), (dense_h, dense_raw), (lb_h, lb_raw)):
                    nc.scalar.copy(hi[:], raw[:]).then_inc(w_hi, 1)

            @block.vector
            def _(dve):
                for i, (lo, raw, hi) in enumerate(((cat_l, cat_raw, cat_h), (dense_l, dense_raw, dense_h), (lb_l, lb_raw, lb_h))):
                    dve.wait_ge(w_hi, i + 1)
                    nc.vector.tensor_tensor(lo[:], raw[:], f32(hi[:]), ALU.subtract).then_inc(w_lo, 1)

        (cat_done, dense_done, low_read, hidden_sum, h_raw_done, h_stats_done, h_var, h_rstd_done, h_ready, ht_done, ht_copied, gates_done,
         gap_ready, gap_exp, is_chosen, counted, weighted, st_scaled, st_turned, st_hi, st_lo, lora_done, y_copied, y_summed, chain_sem, stored) = (
             sem(x) for x in "cat_done dense_done low_read hidden_sum h_raw_done h_stats_done h_var h_rstd_done h_ready ht_done ht_copied gates_done "
             "gap_ready gap_exp is_chosen counted weighted st_scaled st_turned st_hi st_lo lora_done y_copied y_summed chain stored".split())
        ny = pre[0]

        block = ctx.enter_context(nc.Block())

        @block.sync
        def _(sp):
            ov = out.rearrange("(t p) d -> p t d", p=P)
            for c in range(C):
                sp.wait_ge(ny.x_done, (c + 1) * CT)
                sp.dma_start(ov[:, c * CT:(c + 1) * CT, :], X[:, c * CT:(c + 1) * CT, :]).then_inc(stored, 16)
            sp.wait_ge(stored, 16 * C)

        @block.gpsimd
        def _(pool):
            def norm_x(c):
                n = pre[c % 2]
                inverse_deviation(nc, pool, consts, n.stats, n.rstd, n.stats_done, n.var_eps, n.rstd_done, c // 2)

            norm_x(0)
            for c in range(C):
                if c + 1 < C:
                    norm_x(c + 1)
                inverse_deviation(nc, pool, consts, h_stats, h_rstd, h_stats_done, h_var, h_rstd_done, c)
            for c in range(C):
                inverse_deviation(nc, pool, consts, ny.stats_y, ny.rstd_y, ny.y_stats_done, ny.y_var_eps, ny.y_rstd_done, c)
                for t in range(CT):
                    pool.wait_ge(ny.y_rows_done, c * CT + t + 1)
                    nc.gpsimd.tensor_tensor(X[:, c * CT + t, :], X[:, c * CT + t, :], y[:, c * CT + t, :], ALU.add).then_inc(ny.x_done, 1)

        @block.scalar
        def _(act):
            def hi_rows(c):
                n = pre[c % 2]
                for k in range(KD):
                    act.wait_ge(n.turned, c // 2 * KD + k + 1)
                    nc.scalar.copy(xth[:, k, c * CW:(c + 1) * CW], banks[k][:]).then_inc(n.hi_done, 1)

            def gate(c):
                act.wait_ge(ht_done, c + 1)
                nc.scalar.copy(hidden_t[:], BGATE[:, 0:P]).then_inc(ht_copied, 1)
                act.wait_ge(gap_ready, c + 1)
                nc.scalar.activation(second[:], second[:], ACT.Exp).then_inc(gap_exp, 1)

            hi_rows(0)
            for c in range(C):
                if c + 1 < C:
                    hi_rows(c + 1)
                for t in range(c * CT, (c + 1) * CT):
                    act.wait_ge(cat_done, t + 1)
                    nc.scalar.copy(low[:, t, :], BCAT[:, 0:ER_ALL]).then_inc(low_read, 1)
                    act.wait_ge(dense_done, t + 1)
                    nc.scalar.copy(y[:, t, :], BDENSE[t % 2][:]).then_inc(y_copied, 1)
                    if c >= 1 and t % CT == 1:
                        gate(c - 1)
            gate(C - 1)
            for t in range(NT):
                act.wait_ge(st_turned, t + 1)
                if t >= 3:
                    act.wait_ge(lora_done, t - 2)
                nc.scalar.copy(sth[:, t % 3, :], banks[t % 4][:, 0:P]).then_inc(st_hi, 1)

        @block.vector
        def _(dve):
            chain = Count(chain_sem)

            def rows(c):
                return lambda t: X[:, c * CT + t, :]

            def norm_rows(c):
                n = pre[c % 2]
                if c >= 2:
                    dve.wait_ge(n.turned, KD)
                statistics(nc, dve, consts, n.raw, n.stats, n.raw_done, n.stats_done, rows(c), c // 2)
                normalise(nc, dve, n.xn, rows(c), n.stats, n.rstd, n.rstd_done, n.rows_done, c // 2)

            def lo_rows(c):
                n, cols = pre[c % 2], slice(c * CW, (c + 1) * CW)
                for k in range(KD):
                    dve.wait_ge(n.hi_done, c // 2 * KD + k + 1)
                    nc.vector.tensor_tensor(xtl[:, k, cols], banks[k][:], f32(xth[:, k, cols]), ALU.subtract).then_inc(n.lo_done, 1)

            def over_tiles(row, w):
                return row[:].rearrange("p (o n) -> p o n", o=1).to_broadcast([P, CT, w])

            def hidden_rows(c):
                dve.wait_ge(hidden_sum, (c + 1) * CT)
                if c >= 1:
                    dve.wait_ge(h_rstd_done, c)
                statistics(nc, dve, consts, h_raw, h_stats, h_raw_done, h_stats_done, lambda t: hidden[:, c % 2, t, :], c)
                dve.wait_ge(h_rstd_done, c + 1)
                for t in range(CT):
                    ins = nc.vector.tensor_scalar(hidden[:, c % 2, t, :], hidden[:, c % 2, t, :], h_stats[:, t, 0:1], h_rstd[:, t:t + 1], ALU.subtract, ALU.mult)
                    chain.mark(ins)
                dve.wait_ge(chain.sem, chain.n)
                chain.link(dve, nc.vector.tensor_tensor(hidden[:, c % 2], hidden[:, c % 2], over_tiles(gamma, NH), ALU.mult))
                chain.link(dve, nc.vector.tensor_tensor(hidden[:, c % 2], hidden[:, c % 2], over_tiles(beta, NH), ALU.add))
                nc.vector.tensor_scalar(hidden[:, c % 2], hidden[:, c % 2], 0.0, None, ALU.max).then_inc(h_ready, 1)

            def choose(c):
                tiles = slice(c * CT, (c + 1) * CT)
                dve.wait_ge(gates_done, c + 1)
                chain.link(dve, nc.vector.tensor_tensor(gates[:], BGATE[:, P:P + CT * NE].rearrange("p (t e) -> p t e", e=NE),
                                                        over_tiles(gb2, NE), ALU.add))
                for t in range(CT):
                    chain.mark(nc.vector.max(top[:, t, :], gates[:, t, :]))
                dve.wait_ge(chain.sem, chain.n)
                for t in range(CT):
                    chain.mark(nc.vector.max_index(where[:, t, :], top[:, t, :], gates[:, t, :]))
                nc.vector.tensor_tensor(second[:], top[:, :, 1], top[:, :, 0], ALU.subtract).then_inc(gap_ready, 1)
                dve.wait_ge(chain.sem, chain.n)
                chain.link(dve, nc.vector.tensor_copy(where_f[:], where[:]))
                for k in range(2):
                    nc.vector.tensor_tensor(chosen[:, tiles, k, :], over_tiles(experts, NE), where_f[:, :, k:k + 1].to_broadcast([P, CT, NE]),
                                            ALU.is_equal).then_inc(is_chosen, 1)
                dve.wait_ge(gap_exp, c + 1)
                chain.link(dve, nc.vector.tensor_scalar(share[:, tiles, 1], second[:], 1.0, None, ALU.add))
                chain.link(dve, nc.vector.reciprocal(share[:, tiles, 0], share[:, tiles, 1]))
                chain.link(dve, nc.vector.tensor_tensor(share[:, tiles, 1], second[:], share[:, tiles, 0], ALU.mult))

            norm_rows(0)
            for c in range(C):
                if c + 1 < C:
                    norm_rows(c + 1)
                if c == 0:
                    lo_rows(0)
                if c + 1 < C:
                    lo_rows(c + 1)
                for t in range(c * CT, (c + 1) * CT):
                    dve.wait_ge(low_read, t + 1)
                    if t % CT == 0 and c >= 2:
                        dve.wait_ge(ht_done, c - 1)
                    nc.vector.tensor_tensor(hidden[:, c % 2, t % CT, :], BCAT[:, ER_ALL:CATW], gb1[:], ALU.add).then_inc(hidden_sum, 1)
                    if c >= 1 and t % CT == 1:
                        choose(c - 1)
                hidden_rows(c)
            choose(C - 1)
            dve.wait_ge(counted, 1)
            chain.link(dve, nc.vector.tensor_scalar(allowed[:], BGATE[:, 2 * P:2 * P + 2 * NE].rearrange("p (k e) -> p k e", e=NE),
                                                    float(CAPACITY), None, ALU.is_le))
            for k in range(2):
                chain.mark(nc.vector.scalar_tensor_tensor(out=part[:, k, :, :], in0=chosen[:, :, k, :], scalar=1.0 / ER,
                                                          in1=share[:, :, k:k + 1].to_broadcast([P, NT, NE]), op0=ALU.mult, op1=ALU.mult))
            dve.wait_ge(chain.sem, chain.n)
            for k in range(2):
                chain.mark(nc.vector.tensor_tensor(part[:, k, :, :], part[:, k, :, :],
                                                   allowed[:, k:k + 1, :].to_broadcast([P, NT, NE]), ALU.mult))
            dve.wait_ge(chain.sem, chain.n)
            nc.vector.tensor_tensor(weight[:], part[:, 0, :, :], part[:, 1, :, :], ALU.add).then_inc(weighted, 1)
            dve.wait_ge(weighted, 1)
            for s in range(NT + 5):
                if s < NT:
                    if s >= 3:
                        dve.wait_ge(st_turned, s - 2)
                    nc.vector.tensor_tensor(scaled[:, s % 3, :].rearrange("p (e r) -> p e r", r=ER), low[:, s, :].rearrange("p (e r) -> p e r", r=ER),
                                            weight[:, s, :].rearrange("p (e o) -> p e o", o=1).to_broadcast([P, NE, ER]), ALU.mult).then_inc(st_scaled, 1)
                if 1 <= s < NT + 1:
                    t = s - 1
                    dve.wait_ge(st_hi, t + 1)
                    nc.vector.tensor_tensor(stl[:, t % 3, :], banks[t % 4][:, 0:P], f32(sth[:, t % 3, :]), ALU.subtract).then_inc(st_lo, 1)
                if 3 <= s < NT + 3:
                    t = s - 3
                    dve.wait_ge(lora_done, t + 1)
                    dve.wait_ge(y_copied, t + 1)
                    nc.vector.tensor_tensor(y[:, t, :], y[:, t, :], BLORA[t % 3][:], ALU.add).then_inc(y_summed, 1)
                    if t % CT == CT - 1:
                        c = t // CT
                        dve.wait_ge(y_summed, (c + 1) * CT)

                        def y_rows(t):
                            return y[:, c * CT + t, :]

                        if c >= 1:
                            dve.wait_ge(ny.y_rstd_done, c)
                        statistics(nc, dve, consts, ny.raw_y, ny.stats_y, ny.y_raw_done, ny.y_stats_done, y_rows, c)
                        normalise(nc, dve, y[:, c * CT:(c + 1) * CT, :], y_rows, ny.stats_y, ny.rstd_y, ny.y_rstd_done, ny.y_rows_done, c)

        @block.tensor
        def _(pe):
            def turn(c):
                if c >= 1:
                    pe.wait_ge(pre[(c - 1) % 2].lo_done, ((c - 1) // 2 + 1) * KD)
                turn_rows(nc, pe, pre[c % 2], consts, lambda k: banks[k], c // 2)

            def gate(c):
                pe.wait_ge(h_ready, c + 1)
                nc.tensor.transpose(BGATE[:, 0:P], hidden[:, c % 2].rearrange("p t n -> p (t n)"), consts.ident[:]).then_inc(ht_done, 1)
                pe.wait_ge(ht_copied, c + 1)
                nc.tensor.matmul(BGATE[:, P:P + CT * NE], hidden_t[:], gw2[:], start=True, stop=True).then_inc(gates_done, 1)

            turn(0)
            for c in range(C):
                if c + 1 < C:
                    turn(c + 1)
                n = pre[c % 2]
                pe.wait_ge(n.lo_done, (c // 2 + 1) * KD)
                for t in range(c * CT, (c + 1) * CT):
                    tok = slice(t * P, (t + 1) * P)
                    if t >= 1:
                        pe.wait_ge(hidden_sum, t)
                    for k in range(KD):
                        last = product(nc, BCAT[:, 0:CATW], (xth[:, k, tok], xtl[:, k, tok]), (cat_h[:, k, :], cat_l[:, k, :]), k == 0, k == KD - 1)
                    last.then_inc(cat_done, 1)
                    if t >= 2:
                        pe.wait_ge(y_copied, t - 1)
                    for k in range(KD):
                        last = product(nc, BDENSE[t % 2][:], (xth[:, k, tok], xtl[:, k, tok]), (dense_h[:, k, :], dense_l[:, k, :]), k == 0, k == KD - 1)
                    last.then_inc(dense_done, 1)
                    if c >= 1 and t % CT == 1:
                        gate(c - 1)
            gate(C - 1)
            pe.wait_ge(is_chosen, 2 * C)
            for t in range(NT):
                last = nc.tensor.matmul(BGATE[:, 2 * P:2 * P + 2 * NE], ones[:], chosen[:, t, :, :].rearrange("p k e -> p (k e)"),
                                        start=t == 0, stop=t == NT - 1)
            last.then_inc(counted, 1)
            for s in range(NT + 2):
                if s < NT:
                    pe.wait_ge(st_scaled, s + 1)
                    if s >= 4:
                        pe.wait_ge(st_lo, s - 3)
                    nc.tensor.transpose(banks[s % 4][:, 0:P], scaled[:, s % 3, :], consts.ident[:]).then_inc(st_turned, 1)
                if s >= 2:
                    t = s - 2
                    pe.wait_ge(st_lo, t + 1)
                    if t >= 3:
                        pe.wait_ge(y_summed, t - 2)
                    product(nc, BLORA[t % 3][:], (sth[:, t % 3, :], stl[:, t % 3, :]), (lb_h[:], lb_l[:]), True, True).then_inc(lora_done, 1)
    signals.clear()


def program(nc, a, out, parts=4):
    ctx = ExitStack()
    with ctx:
        banks = [ctx.enter_context(nc.psum_tensor(f"bank{i}", [P, 512], F32)) for i in range(8)]
        consts = Constants(nc, ctx, a)
        X = ctx.enter_context(nc.sbuf_tensor("X", [P, NT, D], F32))
        stored = ctx.enter_context(nc.semaphore("stored"))
        with ExitStack() as ffn_ctx:
            ffn = FfnWeights(nc, ffn_ctx, a)
            part1(nc, a, X, ffn, consts, banks)
            if parts >= 2:
                part2(nc, a, X, ffn, consts, banks)
        if parts >= 3:
            part3(nc, a, X, consts, banks)
        if parts >= 4:
            part4(nc, a, X, out, consts, banks)
            return
        with nc.Block() as block:
            @block.sync
            def _(sp):
                sp.dma_start(out.rearrange("(t p) d -> p t d", p=P), X[:]).then_inc(stored, 16)
                sp.wait_ge(stored, 16)


class Inputs:
    pass


def _stacked(w):
    w = w.reshape(2, 4, E0, -1)
    return np.concatenate([w, w, w, np.zeros_like(w)], axis=2).reshape(2 * P, -1)


def kernel(parts=4, **inputs):
    import concourse.bacc as bacc
    from concourse.bass_utils import run_bass_kernel_spmd

    v = {k: np.asarray(x) for k, x in inputs.items()}
    lay = {}
    lay["x"] = v["L0_attn_x"].reshape(T, D)
    wqk = v["L0_attn_Wqk_w"].reshape(HEADS0 * E0, 2, D)
    bqk = v["L0_attn_Wqk_b"].reshape(HEADS0 * E0, 2)
    lay["wqk"] = np.concatenate([_stacked(wqk[:, s]) for s in range(2)]).T
    lay["bqk"] = np.concatenate([_stacked(bqk[:, s]) for s in range(2)]).reshape(4, P).T
    lay["wv"], lay["bv"] = v["L0_attn_Wv_w"].T, v["L0_attn_Wv_b"]
    lay["wo0"], lay["bo"] = v["L0_attn_Wo_w"].T, v["L0_attn_Wo_b"]
    pad = IP - INNER
    for n in ("gate", "up"):
        lay[f"{n}_q"] = np.pad(v[f"L0_ffn_{n}_q"], ((0, pad), (0, 0))).T
        lay[f"{n}_scale"] = np.pad(v[f"L0_ffn_{n}_scale"], (0, pad)).reshape(NI, P).T
        lay[f"{n}_A"] = np.tile(v[f"L0_ffn_{n}_A"], (1, 4))
        lay[f"{n}_B"] = np.tile(np.pad(v[f"L0_ffn_{n}_B"], ((0, 0), (0, pad))), (4, 1))
    lay["down_q"] = np.pad(v["L0_ffn_down_q"], ((0, 0), (0, pad))).T
    lay["down_scale"] = v["L0_ffn_down_scale"]
    lay["down_A"] = np.tile(np.pad(v["L0_ffn_down_A"], ((0, pad), (0, 0))), (1, 4))
    lay["down_B"] = np.tile(v["L0_ffn_down_B"], (4, 1))
    for n in ("wq", "wk", "wv", "wo"):
        lay[f"{n}1"] = v[f"L1_attn_{n}"]
    lay["dense"] = v["L1_ffn_weight"].T
    lay["lora_A"] = v["L1_ffn_lora_A"].transpose(1, 0, 2).reshape(D, NE * ER)
    lay["lora_B"] = v["L1_ffn_lora_B"].reshape(NE * ER, D)
    lay["gw1"] = v["L1_ffn_gw1"].T
    lay["gw2"] = np.zeros((CT, NH, CT, NE), np.float32)
    for t in range(CT):
        lay["gw2"][t, :, t, :] = v["L1_ffn_gw2"].T
    lay["gw2"] = lay["gw2"].reshape(P, CT * NE)
    for n in ("gb1", "ln_gamma", "ln_beta", "gb2"):
        lay[n] = v[f"L1_ffn_{n}"]

    row = np.arange(P)
    lo_rows = [(row % 32 // 8 == 2), (row % 32 // 8 == 1), (row // 32 % 2 == 1), (row // 64 == 1)]
    lay["masks"] = -np.stack(lo_rows, 1).astype(np.float32)
    lay["ident"] = np.eye(P, dtype=np.float32)
    half = HD // 2
    inv_freq = np.float32(10000.0) ** (-np.arange(half, dtype=np.float32) / np.float32(half))
    angle = inv_freq[:, None] * np.arange(SEQ, dtype=np.float32)[None, :]
    lay["cos"] = np.tile(np.cos(angle), (2, 1))
    lay["sin"] = np.concatenate([-np.sin(angle), np.sin(angle)])
    older, same = row[None, :] > row[:, None], row[None, :] <= row[:, None]
    lay["window"] = np.where(np.concatenate([older, same], 1), 0, MASKED).astype(np.float32)
    lay["experts"] = np.tile(np.arange(NE, dtype=np.float32), (P, 1))

    nc = bacc.Bacc("TRN2", target_bir_lowering=False, num_devices=1, dynamic_dma_scratch_size=1024)
    a, arrays = Inputs(), {}
    for name, x in lay.items():
        arrays[f"in_{name}"] = np.ascontiguousarray(x)
        a.__dict__[name] = nc.dram_tensor(f"in_{name}", x.shape, mybir.dt.from_np(x.dtype), kind="ExternalInput").ap()
    out = nc.dram_tensor("out", (T, D), F32, kind="ExternalOutput").ap()
    a.parked = nc.dram_tensor("parked", (T, D), F32, kind="Internal").ap()
    program(nc, a, out, parts)
    r = run_bass_kernel_spmd(nc, [arrays], core_ids=[0])
    return r.results[0]["out"].reshape(BATCH, SEQ, D)
```

```python
from contextlib import ExitStack

import numpy as np

import concourse.bass as bass
from concourse import mybir

F32, F32R, I32, U32 = mybir.dt.float32, mybir.dt.float32r, mybir.dt.int32, mybir.dt.uint32
ALU, ACT, AX = mybir.AluOpType, mybir.ActivationFunctionType, mybir.AxisListType

P = 128
BATCH, SEQ, D = 8, 256, 512
T = BATCH * SEQ
NT = T // P
KD = D // P
C, CT = 4, 4
CW = CT * P
CB = CW // SEQ
EPS = 1e-5

HEADS0, E0 = 8, 8
ROWS0 = 32

INNER, RANK = 1376, 32
NI = -(-INNER // P)
IP = NI * P
Q_ZERO, Q_STEP, LR_SCALE = 7.5, 0.005, 0.02

KV, G, HD = 8, 4, 128
SCALE1 = HD ** -0.5
MASKED = -1e30

NE, ER = 8, 16
NH = 4 * NE
CAPACITY = int(3.0 * T / NE)


class Count:

    def __init__(self, sem, per=0):
        self.sem, self.per, self.base, self.n = sem, per, 0, 0

    def turn(self, c):
        self.base, self.n = c * self.per, 0

    def mark(self, ins):
        self.n += 1
        return ins.then_inc(self.sem, 1)

    def link(self, eng, ins):
        self.mark(ins)
        eng.wait_ge(self.sem, self.base + self.n)


def product(nc, out, lhs, rhs, start, stop):
    nc.tensor.matmul(out, lhs[0], rhs[0], start=start, stop=False)
    nc.tensor.matmul(out, lhs[0], rhs[1], start=False, stop=False)
    return nc.tensor.matmul(out, lhs[1], rhs[0], start=False, stop=stop)


def f32(ap):
    return ap.bitcast(F32)


class Constants:

    def __init__(self, nc, ctx, a):
        self.ident = ctx.enter_context(nc.sbuf_tensor("ident", [P, P], F32))
        self.masks = ctx.enter_context(nc.sbuf_tensor("masks", [P, 4], F32))
        self.minus_half = ctx.enter_context(nc.sbuf_tensor("minus_half", [P, CT], F32))
        self.minus_zero = ctx.enter_context(nc.sbuf_tensor("minus_zero", [P, 1], F32))
        self.ready = ctx.enter_context(nc.semaphore("consts_ready"))
        self.passed = {e.engine: ctx.enter_context(nc.semaphore(f"passed{i}")) for i, e in enumerate((nc.vector, nc.gpsimd, nc.tensor))}
        with nc.Block() as block:
            @block.sync
            def _(sp):
                sp.dma_start(self.ident[:], a.ident).then_inc(self.ready, 16)
                sp.dma_start(self.masks[:], a.masks).then_inc(self.ready, 16)
                sp.wait_ge(self.ready, 32)

            @block.gpsimd
            def _(pool):
                nc.gpsimd.memset(self.minus_half[:], -0.5)
                nc.gpsimd.memset(self.minus_zero[:], -Q_ZERO)


class Signals:

    def __init__(self, nc, tag):
        self.nc, self.tag, self.made = nc, tag, []

    def sem(self, name):
        self.made.append(self.nc.alloc_semaphore(f"{self.tag}_{name}"))
        return self.made[-1]

    def clear(self):
        numbers = sorted(s.num for s in self.made)
        firsts = [x for x in numbers if x - 1 not in numbers]
        with self.nc.Block() as block:
            @block.sync
            def _(sp):
                for first in firsts:
                    stop = next(x for x in range(first, numbers[-1] + 2) if x not in numbers)
                    sp.sem_clear(range(first, stop))
        for s in self.made:
            self.nc.release_semaphore(s)


class Norm:

    def __init__(self, nc, ctx, signals, tag, xt_width=CW):
        def sb(name, shape, dt=F32):
            return ctx.enter_context(nc.sbuf_tensor(f"{signals.tag}_{tag}_{name}", shape, dt))

        def sem(name):
            return signals.sem(f"{tag}_{name}")

        self.raw = sb("raw", [P, CT, 6])
        self.stats = sb("stats", [P, CT, 2])
        self.rstd = sb("rstd", [P, CT])
        self.xn = sb("xn", [P, CT, D])
        if xt_width:
            self.xth, self.xtl = sb("xth", [P, KD, xt_width], F32R), sb("xtl", [P, KD, xt_width], F32R)
        self.raw_y = sb("raw_y", [P, CT, 6])
        self.stats_y = sb("stats_y", [P, CT, 2])
        self.rstd_y = sb("rstd_y", [P, CT])
        self.raw_done, self.stats_done, self.var_eps, self.rstd_done = sem("raw_done"), sem("stats_done"), sem("var_eps"), sem("rstd_done")
        self.rows_done, self.turned, self.hi_done, self.lo_done = sem("rows_done"), sem("turned"), sem("hi_done"), sem("lo_done")
        self.y_raw_done, self.y_stats_done, self.y_var_eps, self.y_rstd_done = sem("y_raw_done"), sem("y_stats_done"), sem("y_var_eps"), sem("y_rstd_done")
        self.y_rows_done, self.x_done = sem("y_rows_done"), sem("x_done")


def statistics(nc, eng, consts, raw, stats, raw_done, stats_done, rows, c):
    for t in range(CT):
        nc.vector.bn_stats(raw[:, t, :], rows(t)).then_inc(raw_done, 1)
    for t in range(CT):
        eng.wait_ge(raw_done, c * CT + t + 1)
        eng.sem_inc(consts.passed[eng.engine], 1)
        nc.vector.bn_aggr(stats[:, t, :], raw[:, t, :]).then_inc(stats_done, 1)


def inverse_deviation(nc, eng, consts, stats, rstd, stats_done, var_eps, rstd_done, c):
    eng.wait_ge(stats_done, (c + 1) * CT)
    eng.sem_inc(consts.passed[eng.engine], 1)
    nc.gpsimd.tensor_scalar(rstd[:, :], stats[:, :, 1], EPS, None, ALU.add).then_inc(var_eps, 1)
    eng.wait_ge(var_eps, c + 1)
    nc.gpsimd.tensor_tensor(rstd[:, :], rstd[:, :], consts.minus_half[:], ALU.pow).then_inc(rstd_done, 1)


def normalise(nc, eng, out, rows, stats, rstd, rstd_done, done, c):
    eng.wait_ge(rstd_done, c + 1)
    for t in range(CT):
        nc.vector.tensor_scalar(out[:, t, :], rows(t), stats[:, t, 0:1], rstd[:, t:t + 1],
                                ALU.subtract, ALU.mult).then_inc(done, 1)


def turn_rows(nc, eng, norm, consts, bank_of, c):
    eng.wait_ge(norm.rows_done, (c + 1) * CT)
    for k in range(KD):
        for t in range(CT):
            last = nc.tensor.transpose(bank_of(k)[:, t * P:(t + 1) * P], norm.xn[:, t, k * P:(k + 1) * P], consts.ident[:])
        last.then_inc(norm.turned, 1)


def residual(nc, eng, norm, X, c):
    for t in range(CT):
        eng.wait_ge(norm.y_rows_done, c * CT + t + 1)
        nc.gpsimd.tensor_tensor(X[:, c * CT + t, :], X[:, c * CT + t, :], norm.xn[:, t, :], ALU.add).then_inc(norm.x_done, 1)


def part1(nc, a, X, ffn, consts, banks):
    ctx, signals = ExitStack(), Signals(nc, "p1")
    with ctx:
        def sb(name, shape, dt=F32):
            return ctx.enter_context(nc.sbuf_tensor(f"p1_{name}", shape, dt))

        def sem(name):
            return signals.sem(name)

        M4 = 4
        NU, UNIT = 4 * CB * 2, 4
        VC = HEADS0 * E0
        n = Norm(nc, ctx, signals, "n")
        wqk_h, wqk_l = sb("wqk_h", [P, KD, M4 * P], F32R), sb("wqk_l", [P, KD, M4 * P], F32R)
        wv_h, wv_l = sb("wv_h", [P, KD, VC], F32R), sb("wv_l", [P, KD, VC], F32R)
        wo_h, wo_l = sb("wo_h", [VC, D], F32R), sb("wo_l", [VC, D], F32R)
        bqk, bv, bo = sb("bqk", [P, M4]), sb("bv", [P, VC]), sb("bo", [P, D])
        x_first, x_rest, w_in = sem("x_first"), sem("x_rest"), sem("w_in")
        w_hi, w_lo = sem("w_hi"), sem("w_lo")
        xv = a.x.rearrange("(t p) d -> p t d", p=P)

        with ExitStack() as raw_ctx:
            wqk_raw, wv_raw, wo_raw = (raw_ctx.enter_context(nc.sbuf_tensor(f"p1_{name}", shape, F32)) for name, shape in
                                       (("wqk_raw", [P, KD, M4 * P]), ("wv_raw", [P, KD, VC]), ("wo_raw", [VC, D])))
            block = raw_ctx.enter_context(nc.Block())

            @block.sync
            def _(sp):
                sp.dma_start(wqk_raw[:], a.wqk.rearrange("(k p) m -> p k m", p=P)).then_inc(w_in, 16)
                sp.dma_start(wv_raw[:], a.wv.rearrange("(k p) m -> p k m", p=P)).then_inc(w_in, 16)
                sp.dma_start(wo_raw[:], a.wo0).then_inc(w_in, 16)
                for dst, src in ((bqk[:], a.bqk),
                                 (bv[:], a.bv.rearrange("(o n) -> o n", o=1).to_broadcast([P, VC])),
                                 (bo[:], a.bo.rearrange("(o n) -> o n", o=1).to_broadcast([P, D]))):
                    sp.dma_start(dst, src).then_inc(w_in, 16)
                sp.dma_start(X[:, 0:CT, :], xv[:, 0:CT, :]).then_inc(x_first, 16)

            @block.scalar
            def _(act):
                act.wait_ge(w_in, 16 * 6)
                nc.scalar.copy(wqk_h[:], wqk_raw[:]).then_inc(w_hi, 1)
                nc.scalar.copy(wv_h[:], wv_raw[:]).then_inc(w_hi, 1)
                nc.scalar.copy(wo_h[:], wo_raw[:]).then_inc(w_hi, 1)

            @block.vector
            def _(dve):
                for i, (lo, raw, hi) in enumerate(((wqk_l, wqk_raw, wqk_h), (wv_l, wv_raw, wv_h), (wo_l, wo_raw, wo_h))):
                    dve.wait_ge(w_hi, i + 1)
                    nc.vector.tensor_tensor(lo[:], raw[:], f32(hi[:]), ALU.subtract).then_inc(w_lo, 1)

        qk32, qkh = sb("qk32", [P, 2, CW]), sb("qkh", [P, 2, CW], F32R)
        stack = sb("stack", [P, M4, CW], F32R)
        v32, v2 = sb("v32", [P, CT, VC]), sb("v2", [P, CT, HEADS0, 2 * E0], F32R)
        negmax, sums, rsums = sb("negmax", [P, NU, 2]), sb("sums", [P, 2 * CB, HEADS0]), sb("rsums", [P, 2 * CB, HEADS0])
        probs = sb("probs", [P, 3, 512])
        pth, ptl = sb("pth", [P, 3, 512], F32R), sb("ptl", [P, 3, 512], F32R)
        osum, on = sb("osum", [P, 2 * CB, VC]), sb("on", [P, 2 * CB, VC])
        oth, otl = qkh[0:VC, 0, :], qkh[0:VC, 1, :]
        q_raw = [sb(f"q_raw{i}", [P, rows, row], I32) for i, (w, q, rows, row) in enumerate(ffn.rows)]
        b_raw, b_hi = sb("b_raw", [P, D]), sb("b_hi", [P, D], F32R)

        q_in, q_used = [sem(f"q_in{i}") for i in range(len(ffn.rows))], [sem(f"q_used{i}") for i in range(len(ffn.rows))]
        small_in, b_in, b_hi_done = sem("small_in"), sem("b_in"), sem("b_hi_done")
        qk_done, qk_hi, stacked = sem("qk_done"), sem("qk_hi"), sem("stacked")
        v_done, v_sum, v_hi, v_lo = sem("v_done"), sem("v_sum"), sem("v_hi"), sem("v_lo")
        scored, maxed, exped, pt_done, pt_hi, pt_lo, pv_done = (sem(x) for x in "scored maxed exped pt_done pt_hi pt_lo pv_done".split())
        o_chain, o_normed, ot_done, ot_hi, ot_lo = (sem(x) for x in "o_chain o_normed ot_done ot_hi ot_lo".split())
        wo_done, y_ready = sem("wo_done"), sem("y_ready")

        def q_rows(c, i):
            w, q, rows, _ = ffn.rows[i]
            rows = rows if not isinstance(c, int) else min(rows, w.shape[1] - c * rows)
            return bass.ds(c * ffn.rows[i][2], rows), rows

        block = ctx.enter_context(nc.Block())

        @block.sync
        def _(sp):
            sp.dma_start(X[:, CT:NT, :], xv[:, CT:NT, :]).then_inc(x_rest, 16)
            for dst, src in ffn.small:
                sp.dma_start(dst, src).then_inc(small_in, 16)

            def load_rows(c):
                for i, (_, q, _, _) in enumerate(ffn.rows):
                    at, rows = q_rows(c, i)
                    if not (isinstance(c, int) and c == 0):
                        sp.wait_ge(q_used[i], c)
                    sp.dma_start(q_raw[i][:, 0:rows, :], q[:, at, :]).then_inc(q_in[i], 16)

            load_rows(0)
            with nc.sync.Fori(1, C - 1) as c:
                load_rows(c)
            load_rows(C - 1)
            for i, (dst, src, w) in enumerate(ffn.stacks):
                if i >= 1:
                    sp.wait_ge(b_hi_done, 4 * i)
                sp.dma_start(b_raw[:, 0:w], src).then_inc(b_in, 16)
            sp.wait_ge(small_in, 16 * len(ffn.small))

        @block.gpsimd
        def _(pool):
            pool.sem_inc(n.x_done, 1)
            inverse_deviation(nc, pool, consts, n.stats, n.rstd, n.stats_done, n.var_eps, n.rstd_done, 0)

            def turn(c, ahead):
                if ahead:
                    inverse_deviation(nc, pool, consts, n.stats, n.rstd, n.stats_done, n.var_eps, n.rstd_done, c + 1)
                if not ahead:
                    for i, (dst, src, w) in enumerate(ffn.stacks):
                        pool.wait_ge(b_in, 16 * (i + 1))
                        nc.gpsimd.tensor_scalar(b_raw[:, 0:w], b_raw[:, 0:w], LR_SCALE, None, ALU.mult).then_inc(b_hi_done, 1)
                        pool.wait_ge(b_hi_done, 4 * i + 1)
                        nc.gpsimd.tensor_copy(b_hi[:, 0:w], b_raw[:, 0:w]).then_inc(b_hi_done, 1)
                        pool.wait_ge(b_hi_done, 4 * i + 2)
                        nc.gpsimd.tensor_scalar(b_hi[:, 0:w], f32(b_hi[:, 0:w]), consts.masks[:, 2:3], None, ALU.mult).then_inc(b_hi_done, 1)
                        pool.wait_ge(b_hi_done, 4 * i + 3)
                        nc.gpsimd.tensor_tensor(dst, b_raw[:, 0:w], f32(b_hi[:, 0:w]), ALU.add).then_inc(b_hi_done, 1)
                        pool.wait_ge(b_hi_done, 4 * i + 4)
                inverse_deviation(nc, pool, consts, n.stats_y, n.rstd_y, n.y_stats_done, n.y_var_eps, n.y_rstd_done, c)
                residual(nc, pool, n, X, c)

            with nc.gpsimd.Fori(0, C - 1) as c:
                turn(c, True)
            turn(C - 1, False)

        @block.scalar
        def _(act):
            def hi_rows(c):
                for k in range(KD):
                    act.wait_ge(n.turned, c * KD + k + 1)
                    nc.scalar.copy(n.xth[:, k, :], banks[k][:]).then_inc(n.hi_done, 1)

            hi_rows(0)

            def turn(c, ahead):
                for m in range(M4):
                    act.wait_ge(qk_done, c * M4 + m + 1)
                    if m >= 2:
                        act.wait_ge(stacked, c * M4 + m - 1)
                    nc.scalar.activation(qk32[:, m % 2, :], banks[m][:], ACT.Identity, bias=bqk[:, m:m + 1])
                    nc.scalar.activation(qkh[:, m % 2, :], banks[m][:], ACT.Identity, bias=bqk[:, m:m + 1]).then_inc(qk_hi, 1)
                act.wait_ge(v_sum, c + 1)
                nc.scalar.copy(v2[:, :, :, 0:E0], v32[:].rearrange("p t (h e) -> p t h e", e=E0)).then_inc(v_hi, 1)
                for i, (w, _, _, _) in enumerate(ffn.rows):
                    at, rows = q_rows(c, i)
                    act.wait_ge(q_in[i], 16 * (c + 1))
                    nc.scalar.activation(w[:, at, :], q_raw[i][:, 0:rows, :], ACT.Identity, bias=consts.minus_zero[:]).then_inc(q_used[i], 1)
                for s in range(NU + 3):
                    if s < NU:
                        act.wait_ge(maxed, c * NU + s + 1)
                        if s >= 3:
                            act.wait_ge(pt_done, c * NU + s - 2)
                        for j in range(2):
                            nc.scalar.activation(probs[:, s % 3, j * SEQ:(j + 1) * SEQ], banks[s % 4][:, j * SEQ:(j + 1) * SEQ],
                                                 ACT.Exp, bias=negmax[:, s, j:j + 1],
                                                 accum_out=sums[:, s // 4, 4 * j + s % 4:4 * j + s % 4 + 1]).then_inc(exped, 1)
                    if s >= 3:
                        u = s - 3
                        act.wait_ge(pt_done, c * NU + u + 1)
                        if u >= 3:
                            act.wait_ge(pv_done, c * NU + u - 2)
                        nc.scalar.copy(pth[:, u % 3, :], banks[4 + u % 2][:]).then_inc(pt_hi, 1)
                if ahead:
                    hi_rows(c + 1)
                act.wait_ge(ot_done, c + 1)
                nc.scalar.copy(oth, banks[6][0:VC, :]).then_inc(ot_hi, 1)

            with nc.scalar.Fori(0, C - 1) as c:
                turn(c, True)
            turn(C - 1, False)

        @block.vector
        def _(dve):
            def lo_rows(c):
                for k in range(KD):
                    dve.wait_ge(n.hi_done, c * KD + k + 1)
                    nc.vector.tensor_tensor(n.xtl[:, k, :], banks[k][:], f32(n.xth[:, k, :]), ALU.subtract).then_inc(n.lo_done, 1)

            def rows(c):
                return lambda t: X[:, c * CT + t, :]

            dve.wait_ge(x_first, 16)
            statistics(nc, dve, consts, n.raw, n.stats, n.raw_done, n.stats_done, rows(0), 0)
            normalise(nc, dve, n.xn, rows(0), n.stats, n.rstd, n.rstd_done, n.rows_done, 0)
            lo_rows(0)
            dve.wait_ge(x_rest, 16)

            def turn(c, ahead):
                for m in range(M4):
                    dve.wait_ge(qk_hi, c * M4 + m + 1)
                    nc.vector.scalar_tensor_tensor(out=stack[:, m, :], in0=f32(qkh[:, m % 2, :]), scalar=consts.masks[:, m // 2:m // 2 + 1],
                                                   in1=qk32[:, m % 2, :], op0=ALU.mult, op1=ALU.add).then_inc(stacked, 1)
                dve.wait_ge(v_done, c + 1)
                nc.vector.tensor_tensor(v32[:], banks[7][:, 0:CT * VC].rearrange("p (t v) -> p t v", v=VC),
                                        bv[:].rearrange("p (o v) -> p o v", o=1).to_broadcast([P, CT, VC]), ALU.add).then_inc(v_sum, 1)
                dve.wait_ge(v_hi, c + 1)
                nc.vector.tensor_tensor(v2[:, :, :, E0:2 * E0], v32[:].rearrange("p t (h e) -> p t h e", e=E0),
                                        f32(v2[:, :, :, 0:E0]), ALU.subtract).then_inc(v_lo, 1)
                if ahead:
                    statistics(nc, dve, consts, n.raw, n.stats, n.raw_done, n.stats_done, rows(c + 1), c + 1)
                dve.wait_ge(n.x_done, c * CT + 1)
                for s in range(NU + 8):
                    if s < NU:
                        dve.wait_ge(scored, c * NU + s + 1)
                        nc.vector.tensor_reduce(negmax[:, s, :], banks[s % 4][:].rearrange("p (j k) -> p j k", j=2), AX.X, ALU.max,
                                                negate=True).then_inc(maxed, 1)
                    if 3 <= s < NU + 3:
                        u = s - 3
                        dve.wait_ge(pt_hi, c * NU + u + 1)
                        nc.vector.tensor_tensor(ptl[:, u % 3, :], banks[4 + u % 2][:], f32(pth[:, u % 3, :]), ALU.subtract).then_inc(pt_lo, 1)
                    if s >= 10 and (s - 10) % 4 == 0:
                        g = (s - 10) // 4
                        dve.wait_ge(pv_done, c * NU + 4 * g + 4)
                        nc.vector.tensor_reduce(osum[:, g, :], banks[6 + g % 2][:, 0:2 * VC].rearrange("p (h s e) -> p h e s", s=2, e=E0),
                                                AX.X, ALU.add)
                        nc.vector.reciprocal(rsums[:, g, :], sums[:, g, :]).then_inc(o_chain, 1)
                        dve.wait_ge(o_chain, c * 2 * CB + g + 1)
                        nc.vector.scalar_tensor_tensor(out=on[:, g, :].rearrange("p (h e) -> p h e", e=E0),
                                                       in0=osum[:, g, :].rearrange("p (h e) -> p h e", e=E0), scalar=float((HEADS0 * E0) ** -0.5),
                                                       in1=rsums[:, g, :].rearrange("p (h o) -> p h o", o=1).to_broadcast([P, HEADS0, E0]),
                                                       op0=ALU.mult, op1=ALU.mult).then_inc(o_normed, 1)
                    if s == 8 and ahead:
                        normalise(nc, dve, n.xn, rows(c + 1), n.stats, n.rstd, n.rstd_done, n.rows_done, c + 1)
                if ahead:
                    lo_rows(c + 1)
                dve.wait_ge(ot_hi, c + 1)
                nc.vector.tensor_tensor(otl, banks[6][0:VC, :], f32(oth), ALU.subtract).then_inc(ot_lo, 1)
                for t in range(CT):
                    dve.wait_ge(wo_done, c * CT + t + 1)
                    nc.vector.tensor_tensor(n.xn[:, t, :], banks[4 + t % 2][:], bo[:], ALU.add).then_inc(y_ready, 1)
                dve.wait_ge(y_ready, (c + 1) * CT)
                statistics(nc, dve, consts, n.raw_y, n.stats_y, n.y_raw_done, n.y_stats_done, lambda t: n.xn[:, t, :], c)
                normalise(nc, dve, n.xn, lambda t: n.xn[:, t, :], n.stats_y, n.rstd_y, n.y_rstd_done, n.y_rows_done, c)

            with nc.vector.Fori(0, C - 1) as c:
                turn(c, True)
            turn(C - 1, False)

        @block.tensor
        def _(pe):
            turn_rows(nc, pe, n, consts, lambda k: banks[k], 0)

            def turn(c, ahead):
                pe.wait_ge(n.lo_done, (c + 1) * KD)
                for m in range(M4):
                    for k in range(KD):
                        last = product(nc, banks[m][:], (wqk_h[:, k, m * P:(m + 1) * P], wqk_l[:, k, m * P:(m + 1) * P]),
                                       (n.xth[:, k, :], n.xtl[:, k, :]), k == 0, k == KD - 1)
                    last.then_inc(qk_done, 1)
                for t in range(CT):
                    for k in range(KD):
                        last = product(nc, banks[7][:, t * VC:(t + 1) * VC], (n.xth[:, k, t * P:(t + 1) * P], n.xtl[:, k, t * P:(t + 1) * P]),
                                       (wv_h[:, k, :], wv_l[:, k, :]), k == 0, k == KD - 1)
                last.then_inc(v_done, 1)
                for s in range(NU + 5):
                    if s < NU:
                        b, qt, i = s // 8, (s // 4) % 2, s % 4
                        if s == 0:
                            pe.wait_ge(stacked, (c + 1) * M4)
                        if s >= 4:
                            pe.wait_ge(exped, 2 * (c * NU + s - 3))
                        r = slice(i * ROWS0, (i + 1) * ROWS0)
                        q0 = (b * 2 + qt) * P
                        for j in range(2):
                            last = nc.tensor.matmul(banks[i][:, j * SEQ:(j + 1) * SEQ], stack[r, j, q0:q0 + P],
                                                    stack[r, 2 + j, b * SEQ:(b + 1) * SEQ], start=True, stop=True)
                        last.then_inc(scored, 1)
                    if 3 <= s < NU + 3:
                        u = s - 3
                        pe.wait_ge(exped, 2 * (c * NU + u + 1))
                        if u >= 2:
                            pe.wait_ge(pt_lo, c * NU + u - 1)
                        for f in range(4):
                            last = nc.tensor.transpose(banks[4 + u % 2][:, f * P:(f + 1) * P], probs[:, u % 3, f * P:(f + 1) * P], consts.ident[:])
                        last.then_inc(pt_done, 1)
                    if s >= 5:
                        u = s - 5
                        b, i, g = u // 8, u % 4, u // 4
                        if u == 0:
                            pe.wait_ge(v_lo, c + 1)
                        pe.wait_ge(pt_lo, c * NU + u + 1)
                        if i == 0 and g >= 2:
                            pe.wait_ge(o_normed, c * 2 * CB + g - 1)
                        for j in range(2):
                            h = 4 * j + i
                            out = banks[6 + g % 2][:, h * 2 * E0:(h + 1) * 2 * E0]
                            for f in range(2):
                                nc.tensor.matmul(out, pth[:, u % 3, (2 * j + f) * P:(2 * j + f + 1) * P], v2[:, 2 * b + f, h, :],
                                                 start=f == 0, stop=False)
                            for f in range(2):
                                last = nc.tensor.matmul(out[:, 0:E0], ptl[:, u % 3, (2 * j + f) * P:(2 * j + f + 1) * P],
                                                        v2[:, 2 * b + f, h, 0:E0], start=False, stop=f == 1)
                        last.then_inc(pv_done, 1)
                if ahead:
                    turn_rows(nc, pe, n, consts, lambda k: banks[k], c + 1)
                pe.wait_ge(o_normed, (c + 1) * 2 * CB)
                pe.sem_inc(consts.passed[pe.engine], 1)
                for g in range(2 * CB):
                    last = nc.tensor.transpose(banks[6][0:VC, g * P:(g + 1) * P], on[:, g, :], consts.ident[:])
                last.then_inc(ot_done, 1)
                pe.wait_ge(ot_lo, c + 1)
                for t in range(CT):
                    if t >= 2:
                        pe.wait_ge(y_ready, c * CT + t - 1)
                    product(nc, banks[4 + t % 2][:], (oth[:, t * P:(t + 1) * P], otl[:, t * P:(t + 1) * P]),
                            (wo_h[:], wo_l[:]), True, True).then_inc(wo_done, 1)

            with nc.tensor.Fori(0, C - 1) as c:
                turn(c, True)
            turn(C - 1, False)
    signals.clear()


class FfnWeights:

    def __init__(self, nc, ctx, a):
        def sb(name, shape, dt=F32):
            return ctx.enter_context(nc.sbuf_tensor(f"ffn_{name}", shape, dt))

        self.gate, self.up, self.down = sb("gate", [P, KD, IP], F32R), sb("up", [P, KD, IP], F32R), sb("down", [P, NI, D], F32R)
        self.scales = sb("scales", [P, 2, NI])
        self.down_scale = sb("down_scale", [P, D])
        self.b_gate, self.b_up, self.b_down = sb("b_gate", [P, IP], F32R), sb("b_up", [P, IP], F32R), sb("b_down", [P, D], F32R)
        gq, uq, dq = (w.rearrange("(k p) n -> p k n", p=P) for w in (a.gate_q, a.up_q, a.down_q))
        self.rows = [(self.gate, gq, KD // C, IP), (self.up, uq, KD // C, IP), (self.down, dq, -(-NI // C), D)]
        self.small = [(self.scales[:, 0, :], a.gate_scale),
                      (self.scales[:, 1, :], a.up_scale),
                      (self.down_scale[:], a.down_scale.rearrange("(o n) -> o n", o=1).to_broadcast([P, D]))]
        self.stacks = [(w[:, s:min(s + D, w.shape[1])], b[:, s:min(s + D, w.shape[1])], min(D, w.shape[1] - s)) for w, b in
                       ((self.b_gate, a.gate_B), (self.b_up, a.up_B), (self.b_down, a.down_B)) for s in range(0, w.shape[1], D)]


def part2(nc, a, X, ffn, consts, banks):
    ctx, signals = ExitStack(), Signals(nc, "p2")
    with ctx:
        def sb(name, shape, dt=F32):
            return ctx.enter_context(nc.sbuf_tensor(f"p2_{name}", shape, dt))

        def sem(name):
            return signals.sem(name)

        RING = 4
        BG, BU, BL, BR, BY = banks[0], banks[1], banks[2], banks[3], banks[4:8]
        ag_h, ag_l = sb("ag_h", [P, KD, P], F32R), sb("ag_l", [P, KD, P], F32R)
        au_h, au_l = sb("au_h", [P, KD, P], F32R), sb("au_l", [P, KD, P], F32R)
        ad_h, ad_l = sb("ad_h", [P, NI, P], F32R), sb("ad_l", [P, NI, P], F32R)
        a_in, a_hi, a_lo, scales_done = sem("a_in"), sem("a_hi"), sem("a_lo"), sem("scales_done")

        with ExitStack() as raw_ctx:
            raws = [raw_ctx.enter_context(nc.sbuf_tensor(f"p2_raw{i}", [P, k, P], F32)) for i, k in enumerate((KD, KD, NI))]
            block = raw_ctx.enter_context(nc.Block())

            @block.sync
            def _(sp):
                for raw, src in zip(raws, (a.gate_A, a.up_A, a.down_A)):
                    sp.dma_start(raw[:], src.rearrange("(k p) n -> p k n", p=P)).then_inc(a_in, 16)

            @block.scalar
            def _(act):
                act.wait_ge(a_in, 48)
                for raw, hi in zip(raws, (ag_h, au_h, ad_h)):
                    nc.scalar.copy(hi[:], raw[:]).then_inc(a_hi, 1)

            @block.vector
            def _(dve):
                nc.vector.tensor_scalar(ffn.scales[:], ffn.scales[:], Q_STEP, None, ALU.mult).then_inc(scales_done, 1)
                nc.vector.tensor_scalar(ffn.down_scale[:], ffn.down_scale[:], Q_STEP, None, ALU.mult).then_inc(scales_done, 1)
                for i, (raw, hi, lo) in enumerate(zip(raws, (ag_h, au_h, ad_h), (ag_l, au_l, ad_l))):
                    dve.wait_ge(a_hi, i + 1)
                    nc.vector.tensor_tensor(lo[:], raw[:], f32(hi[:]), ALU.subtract).then_inc(a_lo, 1)

        n = Norm(nc, ctx, signals, "n")
        r32, rh = sb("r32", [P, 2, CW]), sb("rh", [P, 2, CW], F32R)
        rstack = sb("rstack", [P, 3, CW], F32R)
        gu = sb("gu", [P, 2, 2, CW])
        hh, hl = sb("hh", [P, RING, CW], F32R), sb("hl", [P, RING, CW], F32R)
        (r_done, r_hi, r_stacked, main_done, rank_done, scaled, summed, silued, multiplied, h_hi, h_lo, down_done, rank_down_done,
         y_scaled, y_ready) = (sem(x) for x in "r_done r_hi r_stacked main_done rank_done scaled summed silued multiplied h_hi h_lo down_done rank_down_done y_scaled y_ready".split())

        block = ctx.enter_context(nc.Block())

        @block.gpsimd
        def _(pool):
            pool.sem_inc(n.x_done, 1)
            inverse_deviation(nc, pool, consts, n.stats, n.rstd, n.stats_done, n.var_eps, n.rstd_done, 0)

            def turn(c, ahead):
                for s in range(NI):
                    pool.wait_ge(silued, c * NI + s + 1)
                    pool.wait_ge(summed, c * 2 * NI + 2 * s + 2)
                    nc.gpsimd.tensor_tensor(gu[:, s % 2, 0, :], gu[:, s % 2, 0, :], gu[:, s % 2, 1, :], ALU.mult).then_inc(multiplied, 1)
                    if s == 4 and ahead:
                        inverse_deviation(nc, pool, consts, n.stats, n.rstd, n.stats_done, n.var_eps, n.rstd_done, c + 1)
                inverse_deviation(nc, pool, consts, n.stats_y, n.rstd_y, n.y_stats_done, n.y_var_eps, n.y_rstd_done, c)
                residual(nc, pool, n, X, c)

            with nc.gpsimd.Fori(0, C - 1) as c:
                turn(c, True)
            turn(C - 1, False)

        @block.scalar
        def _(act):
            def hi_rows(c):
                for k in range(KD):
                    act.wait_ge(n.turned, c * KD + k + 1)
                    nc.scalar.copy(n.xth[:, k, :], banks[k][:]).then_inc(n.hi_done, 1)

            def h_hi_of(c, s):
                act.wait_ge(multiplied, c * NI + s + 1)
                if s >= RING:
                    act.wait_ge(down_done, c * NI + s - RING + 1)
                nc.scalar.copy(hh[:, s % RING, :], gu[:, s % 2, 0, :]).then_inc(h_hi, 1)

            def r_hi_of(bank, slot):
                nc.scalar.copy(r32[:, slot, :], bank[:])
                nc.scalar.copy(rh[:, slot, :], bank[:]).then_inc(r_hi, 1)

            hi_rows(0)

            def turn(c, ahead):
                for m, bank in enumerate((BG, BU)):
                    act.wait_ge(r_done, c * 2 + m + 1)
                    r_hi_of(bank, m)
                for s in range(NI):
                    act.wait_ge(main_done, c * 2 * NI + 2 * s + 1)
                    if s >= 2:
                        act.wait_ge(h_lo, c * NI + s - 1)
                    nc.scalar.activation(gu[:, s % 2, 0, :], BG[:], ACT.Copy, scale=ffn.scales[:, 0, s:s + 1]).then_inc(scaled, 1)
                    if s >= 1:
                        h_hi_of(c, s - 1)
                    act.wait_ge(main_done, c * 2 * NI + 2 * s + 2)
                    nc.scalar.activation(gu[:, s % 2, 1, :], BU[:], ACT.Copy, scale=ffn.scales[:, 1, s:s + 1]).then_inc(scaled, 1)
                    act.wait_ge(summed, c * 2 * NI + 2 * s + 1)
                    nc.scalar.activation(gu[:, s % 2, 0, :], gu[:, s % 2, 0, :], ACT.Silu).then_inc(silued, 1)
                h_hi_of(c, NI - 1)
                act.wait_ge(down_done, (c + 1) * NI)
                r_hi_of(BR, 0)
                if ahead:
                    hi_rows(c + 1)

            with nc.scalar.Fori(0, C - 1) as c:
                turn(c, True)
            turn(C - 1, False)

        @block.vector
        def _(dve):
            def lo_rows(c):
                for k in range(KD):
                    dve.wait_ge(n.hi_done, c * KD + k + 1)
                    nc.vector.tensor_tensor(n.xtl[:, k, :], banks[k][:], f32(n.xth[:, k, :]), ALU.subtract).then_inc(n.lo_done, 1)

            def rows(c):
                return lambda t: X[:, c * CT + t, :]

            def h_lo_of(c, s):
                dve.wait_ge(h_hi, c * NI + s + 1)
                nc.vector.tensor_tensor(hl[:, s % RING, :], gu[:, s % 2, 0, :], f32(hh[:, s % RING, :]), ALU.subtract).then_inc(h_lo, 1)

            def r_stack_of(c, m, slot):
                dve.wait_ge(r_hi, c * 3 + m + 1)
                nc.vector.scalar_tensor_tensor(out=rstack[:, m, :], in0=f32(rh[:, slot, :]), scalar=consts.masks[:, 3:4],
                                               in1=r32[:, slot, :], op0=ALU.mult, op1=ALU.add).then_inc(r_stacked, 1)

            dve.sem_inc(y_ready, 1)
            statistics(nc, dve, consts, n.raw, n.stats, n.raw_done, n.stats_done, rows(0), 0)
            normalise(nc, dve, n.xn, rows(0), n.stats, n.rstd, n.rstd_done, n.rows_done, 0)
            lo_rows(0)

            def turn(c, ahead):
                r_stack_of(c, 0, 0)
                r_stack_of(c, 1, 1)
                for s in range(NI):
                    for m in range(2):
                        dve.wait_ge(scaled, c * 2 * NI + 2 * s + m + 1)
                        dve.wait_ge(rank_done, c * 2 * NI + 2 * s + m + 1)
                        nc.vector.tensor_tensor(gu[:, s % 2, m, :], gu[:, s % 2, m, :], BL[:], ALU.add).then_inc(summed, 1)
                        if m == 0 and s >= 1:
                            h_lo_of(c, s - 1)
                    if s == 1 and ahead:
                        statistics(nc, dve, consts, n.raw, n.stats, n.raw_done, n.stats_done, rows(c + 1), c + 1)
                    if s == 7:
                        dve.wait_ge(n.x_done, c * CT + 1)
                        if ahead:
                            normalise(nc, dve, n.xn, rows(c + 1), n.stats, n.rstd, n.rstd_done, n.rows_done, c + 1)
                h_lo_of(c, NI - 1)
                r_stack_of(c, 2, 0)
                if ahead:
                    lo_rows(c + 1)
                dve.wait_ge(down_done, (c + 1) * NI)
                for t in range(CT):
                    nc.vector.tensor_tensor(n.xn[:, t, :], BY[t][:], ffn.down_scale[:], ALU.mult).then_inc(y_scaled, 1)
                for t in range(CT):
                    dve.wait_ge(y_scaled, c * CT + t + 1)
                    dve.wait_ge(rank_down_done, c * CT + t + 1)
                    nc.vector.tensor_tensor(n.xn[:, t, :], n.xn[:, t, :], banks[t][:], ALU.add).then_inc(y_ready, 1)
                dve.wait_ge(y_ready, (c + 1) * CT + 1)
                statistics(nc, dve, consts, n.raw_y, n.stats_y, n.y_raw_done, n.y_stats_done, lambda t: n.xn[:, t, :], c)
                normalise(nc, dve, n.xn, lambda t: n.xn[:, t, :], n.stats_y, n.rstd_y, n.y_rstd_done, n.y_rows_done, c)

            with nc.vector.Fori(0, C - 1) as c:
                turn(c, True)
            turn(C - 1, False)

        @block.tensor
        def _(pe):
            turn_rows(nc, pe, n, consts, lambda k: banks[k], 0)

            def main(bank, w, s):
                for k in range(KD):
                    nc.tensor.matmul(bank[:], w[:, k, s * P:(s + 1) * P], n.xth[:, k, :], start=k == 0, stop=False)
                    last = nc.tensor.matmul(bank[:], w[:, k, s * P:(s + 1) * P], n.xtl[:, k, :], start=False, stop=k == KD - 1)
                return last

            def turn(c, ahead):
                pe.wait_ge(y_ready, c * CT + 1)
                pe.wait_ge(n.lo_done, (c + 1) * KD)
                for bank, hi, lo in ((BG, ag_h, ag_l), (BU, au_h, au_l)):
                    for k in range(KD):
                        last = product(nc, bank[:], (hi[:, k, :], lo[:, k, :]), (n.xth[:, k, :], n.xtl[:, k, :]), k == 0, k == KD - 1)
                    last.then_inc(r_done, 1)
                for s in range(NI + 2):
                    if s < NI:
                        for m, (bank, w, b) in enumerate(((BG, ffn.gate, ffn.b_gate), (BU, ffn.up, ffn.b_up))):
                            if s == 0:
                                pe.wait_ge(r_stacked, c * 3 + m + 1)
                            else:
                                pe.wait_ge(scaled, c * 2 * NI + 2 * s + m - 1)
                            main(bank, w, s).then_inc(main_done, 1)
                            if s + m > 0:
                                pe.wait_ge(summed, c * 2 * NI + 2 * s + m)
                            nc.tensor.matmul(BL[:], b[:, s * P:(s + 1) * P], rstack[:, m, :], start=True, stop=True).then_inc(rank_done, 1)
                    if s >= 2:
                        j = s - 2
                        pe.wait_ge(h_lo, c * NI + j + 1)
                        for t in range(CT):
                            tok = slice(t * P, (t + 1) * P)
                            nc.tensor.matmul(BY[t][:], hh[:, j % RING, tok], ffn.down[:, j, :], start=j == 0, stop=False)
                            nc.tensor.matmul(BY[t][:], hl[:, j % RING, tok], ffn.down[:, j, :], start=False, stop=j == NI - 1)
                        last = product(nc, BR[:], (ad_h[:, j, :], ad_l[:, j, :]), (hh[:, j % RING, :], hl[:, j % RING, :]), j == 0, j == NI - 1)
                        last.then_inc(down_done, 1)
                if ahead:
                    pe.wait_ge(r_stacked, c * 3 + 3)
                    turn_rows(nc, pe, n, consts, lambda k: banks[k], c + 1)
                pe.wait_ge(r_stacked, c * 3 + 3)
                for t in range(CT):
                    if ahead:
                        pe.wait_ge(n.lo_done, (c + 1) * KD + t + 1)
                    nc.tensor.matmul(banks[t][:], rstack[:, 2, t * P:(t + 1) * P], ffn.b_down[:], start=True, stop=True).then_inc(rank_down_done, 1)

            with nc.tensor.Fori(0, C - 1) as c:
                turn(c, True)
            turn(C - 1, False)
    signals.clear()


def part3(nc, a, X, consts, banks):
    ctx, signals = ExitStack(), Signals(nc, "p3")
    with ctx:
        def sb(name, shape, dt=F32):
            return ctx.enter_context(nc.sbuf_tensor(f"p3_{name}", shape, dt))

        def sem(name):
            return signals.sem(name)

        GW = G * HD
        NM = 1 + G
        NJ = NM + 1
        NU = G * CB
        NW = 3 * CB
        NV = 2 * CB
        UW = 3 * P
        SECOND, FIRST = slice(0, 2 * P), slice(2 * P, 3 * P)

        parked_done, x_back = sem("parked_done"), sem("x_back")
        tables_in, q_raw_in, o_raw_in, w_hi, qkv_split, o_split = (sem(x) for x in "tables_in q_raw_in o_raw_in w_hi qkv_split o_split".split())
        with ExitStack() as mid_ctx:
            def mid(name, shape, dt=F32):
                return mid_ctx.enter_context(nc.sbuf_tensor(f"p3_{name}", shape, dt))

            xth, xtl = mid("xth", [P, KD, T], F32R), mid("xtl", [P, KD, T], F32R)
            wq_h, wq_l = mid("wq_h", [P, KD, GW], F32R), mid("wq_l", [P, KD, GW], F32R)
            wk_h, wk_l = mid("wk_h", [P, KD, HD], F32R), mid("wk_l", [P, KD, HD], F32R)
            wv_h, wv_l = mid("wv_h", [P, KD, HD], F32R), mid("wv_l", [P, KD, HD], F32R)
            wo_h, wo_l = mid("wo_h", [P, G, D], F32R), mid("wo_l", [P, G, D], F32R)
            raw = mid("raw", [P, KD, GW])
            raw_k, raw_v = mid("raw_k", [P, KD, HD]), mid("raw_v", [P, KD, HD])
            cos, sin = mid("cos", [P, SEQ]), mid("sin", [P, SEQ])
            window = mid("window", [P, 2 * P])

            wq_g, wk_g, wv_g = (w.rearrange("(k p) n -> p k n", p=P) for w in (a.wq1, a.wk1, a.wv1))
            wo_g = a.wo1.rearrange("(h p) n -> p h n", p=P)

            qkv_pieces = [(raw_k[:], wk_h[:], wk_l[:])]
            qkv_pieces += [tuple(w[:, :, h * HD:(h + 1) * HD] for w in (raw, wq_h, wq_l)) for h in range(G)]
            qkv_pieces += [(raw_v[:], wv_h[:], wv_l[:])]
            o_pieces = [tuple(w[:, h, :] for w in (raw, wo_h, wo_l)) for h in range(G)]
            NQ = len(qkv_pieces)
            NPIECE = NQ + G

            def hi_piece(act, g, i):
                if i == 0:
                    act.wait_ge(q_raw_in, g * 48 + 48)
                if i == NQ:
                    act.wait_ge(o_raw_in, g * 16 + 16)
                r, hi, lo = (qkv_pieces + o_pieces)[i]
                nc.scalar.copy(hi, r).then_inc(w_hi, 1)

            def lo_piece(pool, g, i):
                pool.wait_ge(w_hi, g * NPIECE + i + 1)
                r, hi, lo = (qkv_pieces + o_pieces)[i]
                nc.gpsimd.tensor_tensor(lo, r, f32(hi), ALU.subtract).then_inc(qkv_split if i < NQ else o_split, 1)

            def load_qkv(sp, g):
                sp.dma_start(raw[:], wq_g[:, :, bass.ds(g * GW, GW)]).then_inc(q_raw_in, 16)
                sp.dma_start(raw_k[:], wk_g[:, :, bass.ds(g * HD, HD)]).then_inc(q_raw_in, 16)
                sp.dma_start(raw_v[:], wv_g[:, :, bass.ds(g * HD, HD)]).then_inc(q_raw_in, 16)

            with ExitStack() as pre_ctx:
                pre = [Norm(nc, pre_ctx, signals, f"n{i}", xt_width=0) for i in range(2)]
                block = pre_ctx.enter_context(nc.Block())

                @block.sync
                def _(sp):
                    load_qkv(sp, 0)
                    sp.dma_start(a.parked.rearrange("(t p) d -> p t d", p=P), X[:]).then_inc(parked_done, 16)
                    sp.dma_start(cos[:], a.cos).then_inc(tables_in, 16)
                    sp.dma_start(sin[:], a.sin).then_inc(tables_in, 16)
                    sp.dma_start(window[:], a.window).then_inc(tables_in, 16)

                @block.gpsimd
                def _(pool):
                    for c in range(C):
                        n = pre[c % 2]
                        inverse_deviation(nc, pool, consts, n.stats, n.rstd, n.stats_done, n.var_eps, n.rstd_done, c // 2)
                    for i in range(NQ):
                        lo_piece(pool, 0, i)

                @block.scalar
                def _(act):
                    for i in range(NQ):
                        hi_piece(act, 0, i)
                    for c in range(C):
                        n = pre[c % 2]
                        for k in range(KD):
                            act.wait_ge(n.turned, c // 2 * KD + k + 1)
                            nc.scalar.copy(xth[:, k, c * CW:(c + 1) * CW], banks[4 * (c % 2) + k][:]).then_inc(n.hi_done, 1)

                @block.vector
                def _(dve):
                    def lo_rows(c):
                        n = pre[c % 2]
                        for k in range(KD):
                            dve.wait_ge(n.hi_done, c // 2 * KD + k + 1)
                            cols = slice(c * CW, (c + 1) * CW)
                            nc.vector.tensor_tensor(xtl[:, k, cols], banks[4 * (c % 2) + k][:], f32(xth[:, k, cols]), ALU.subtract).then_inc(n.lo_done, 1)

                    for c in range(C + 1):
                        if c < C:
                            n = pre[c % 2]
                            if c >= 2:
                                dve.wait_ge(n.turned, KD)
                            statistics(nc, dve, consts, n.raw, n.stats, n.raw_done, n.stats_done, lambda t: X[:, c * CT + t, :], c // 2)
                            normalise(nc, dve, n.xn, lambda t: X[:, c * CT + t, :], n.stats, n.rstd, n.rstd_done, n.rows_done, c // 2)
                        if c >= 1:
                            lo_rows(c - 1)

                @block.tensor
                def _(pe):
                    for c in range(C):
                        n = pre[c % 2]
                        if c >= 2:
                            pe.wait_ge(n.lo_done, KD)
                        turn_rows(nc, pe, n, consts, lambda k: banks[4 * (c % 2) + k], c // 2)

            qh, ql = mid("qh", [P, G, CW], F32R), mid("ql", [P, G, CW], F32R)
            kh, kl = mid("kh", [P, CW], F32R), mid("kl", [P, CW], F32R)
            vh, vl = mid("vh", [P, CT, HD], F32R), mid("vl", [P, CT, HD], F32R)
            vt = mid("vt", [P, CW])
            swap, turn_cos = mid("swap", [P, 2, CW]), mid("turn_cos", [P, 2, CW])
            probs = mid("probs", [P, NU, UW])
            top, neg, sums, rsums = (mid(x, [P, NU, 2]) for x in ("top", "neg", "sums", "rsums"))
            pth, ptl = mid("pth", [P, 2, G * P], F32R), mid("ptl", [P, 2, G * P], F32R)
            oth, otl = mid("oth", [P, G, CW], F32R), mid("otl", [P, G, CW], F32R)
            (proj_done, vt_copied, v_turned, swapped, cosed, sined, rotated, rot_hi, rot_lo, v_hi, v_lo, scored, masked, negated, exped, inverted, normed,
             pt_done, pt_hi, pt_lo, pv_done, o_hi, o_lo, wo_done, y_ready) = (sem(x) for x in (
                 "proj_done vt_copied v_turned swapped cosed sined rotated rot_hi rot_lo v_hi v_lo scored masked negated exped inverted normed "
                 "pt_done pt_hi pt_lo pv_done o_hi o_lo wo_done y_ready").split())

            def wait(eng, sem, value):
                if not isinstance(value, int) or value > 0:
                    eng.wait_ge(sem, value)

            def groups(eng, item):
                item(0, 0, before=False)
                with eng.Fori(0, KV - 1) as g:
                    for c in range(1, C):
                        item(g, c)
                    item(g + 1, 0)
                for c in range(1, C):
                    item(KV - 1, c)
                item(KV, 0, now=False)

            GATHERED = {0: 0, 2: 1, 3: 2, 5: 3}

            def bank_of_tile(m):
                return banks[m % 4]

            def bank_of_unit(u):
                return banks[(NJ + u) % 4]

            block = mid_ctx.enter_context(nc.Block())

            @block.sync
            def _(sp):
                sp.wait_ge(parked_done, 16)

                def item(g, c, before=True, now=True):
                    if c == 0 and now:
                        sp.wait_ge(qkv_split, g * NQ + NQ)
                        sp.dma_start(raw[:], wo_g[:, bass.ds(g * G, G), :]).then_inc(o_raw_in, 16)
                    if c == 1 and not (isinstance(g, int) and g == KV - 1):
                        sp.wait_ge(o_split, g * G + G)
                        load_qkv(sp, g + 1)

                groups(nc.sync, item)

            @block.gpsimd
            def _(pool):
                pool.wait_ge(parked_done, 16)
                pool.wait_ge(tables_in, 48)
                nc.gpsimd.memset(X[:], 0.0).then_inc(y_ready, 1)

                def item(g, c, before=True, now=True):
                    n = g * C + c
                    for m in range(NM if now else 0):
                        par = (c + m) % 2
                        shape = [P, CB, SEQ]
                        wait(pool, swapped, n * NM + m + 1)
                        nc.gpsimd.tensor_tensor(swap[:, par, :].rearrange("p (b s) -> p b s", b=CB), swap[:, par, :].rearrange("p (b s) -> p b s", b=CB),
                                                sin[:].rearrange("p (o s) -> p o s", o=1).to_broadcast(shape), ALU.mult).then_inc(sined, 1)
                        wait(pool, cosed, n * NM + m + 1)
                        wait(pool, sined, n * NM + m + 1)
                        nc.gpsimd.tensor_tensor(turn_cos[:, par, :], turn_cos[:, par, :], swap[:, par, :], ALU.add).then_inc(rotated, 1)
                        if c == 1 and m >= 1:
                            lo_piece(pool, g, NQ + m - 1)
                    if c == C - 1 and not (isinstance(g, int) and g == KV - 1):
                        for i in range(NQ):
                            lo_piece(pool, g + 1, i)

                groups(nc.gpsimd, item)

            @block.scalar
            def _(act):
                half = HD // 2

                def item(g, c, before=True, now=True):
                    n = g * C + c

                    def gather(x):
                        t = GATHERED[x]
                        wait(act, pv_done, (n - 1) * NW + x + 1)
                        nc.scalar.copy(oth[:, :, t * P:(t + 1) * P], banks[6 + t % 2][:].rearrange("p (h t) -> p h t", h=G)).then_inc(o_hi, 1)

                    for s in range(NW):
                        if now and s < NM:
                            par, bank = (c + s) % 2, bank_of_tile(s)
                            wait(act, proj_done, n * NJ + s + 1)
                            wait(act, rotated, n * NM + s - 1)
                            nc.scalar.copy(swap[0:half, par, :], bank[half:HD, :])
                            nc.scalar.copy(swap[half:HD, par, :], bank[0:half, :]).then_inc(swapped, 1)
                        if now and s == NM:
                            wait(act, proj_done, (n + 1) * NJ)
                            nc.scalar.copy(vt[:], bank_of_tile(NM)[:]).then_inc(vt_copied, 1)
                        if before:
                            wait(act, pt_done, (n - 1) * NW + s + 1)
                            if s >= 2:
                                wait(act, pv_done, (n - 1) * NW + s - 1)
                            nc.scalar.copy(pth[:, s % 2, :], banks[4 + s % 2][:]).then_inc(pt_hi, 1)
                            if c == 1 and s >= 1 and s <= G:
                                hi_piece(act, g, NQ + s - 1)
                        if now and 1 <= s < NM + 1:
                            par = (c + s - 1) % 2
                            wait(act, rotated, n * NM + s)
                            nc.scalar.copy(kh[:] if s == 1 else qh[:, s - 2, :], turn_cos[:, par, :]).then_inc(rot_hi, 1)
                        if before and s - 2 in GATHERED:
                            gather(s - 2)
                    for u in range(NU):
                        if before and u == 1:
                            gather(NW - 1)
                        if now and u == 3:
                            wait(act, v_turned, n + 1)
                            nc.scalar.copy(vh[:].rearrange("p t d -> p (t d)"), banks[6][:]).then_inc(v_hi, 1)
                        if not now:
                            continue
                        wait(act, negated, n * NU + u + 1)
                        for q, cols in enumerate((FIRST, SECOND)):
                            nc.scalar.activation(probs[:, u, cols], probs[:, u, cols], ACT.Exp, bias=neg[:, u, q:q + 1], scale=SCALE1,
                                                 accum_out=sums[:, u, q:q + 1]).then_inc(exped, 1)
                        if c == C - 1 and u < NQ and not (isinstance(g, int) and g == KV - 1):
                            hi_piece(act, g + 1, u)

                groups(nc.scalar, item)

            @block.vector
            def _(dve):
                def item(g, c, before=True, now=True):
                    n = g * C + c

                    def gather(x):
                        t = GATHERED[x]
                        wait(dve, o_hi, (n - 1) * NV + t + 1)
                        tok = slice(t * P, (t + 1) * P)
                        nc.vector.tensor_tensor(otl[:, :, tok], banks[6 + t % 2][:].rearrange("p (h t) -> p h t", h=G),
                                                f32(oth[:, :, tok]), ALU.subtract).then_inc(o_lo, 1)

                    def divide(u):
                        wait(dve, exped, 2 * (n * NU + u + 1))
                        nc.vector.reciprocal(rsums[:, u, :], sums[:, u, :]).then_inc(inverted, 1)
                        wait(dve, inverted, n * NU + u + 1)
                        for q, cols in enumerate((FIRST, SECOND)):
                            nc.vector.tensor_scalar(probs[:, u, cols], probs[:, u, cols], rsums[:, u, q:q + 1], None, ALU.mult).then_inc(normed, 1)

                    for s in range(NW):
                        if now and s < NM:
                            par = (c + s) % 2
                            wait(dve, swapped, n * NM + s + 1)
                            wait(dve, rot_lo, n * NM + s - 1)
                            nc.vector.tensor_tensor(turn_cos[:, par, :].rearrange("p (b s) -> p b s", b=CB),
                                                    bank_of_tile(s)[:].rearrange("p (b s) -> p b s", b=CB),
                                                    cos[:].rearrange("p (o s) -> p o s", o=1).to_broadcast([P, CB, SEQ]), ALU.mult).then_inc(cosed, 1)
                        if before:
                            wait(dve, pt_hi, (n - 1) * NW + s + 1)
                            nc.vector.tensor_tensor(ptl[:, s % 2, :], banks[4 + s % 2][:], f32(pth[:, s % 2, :]), ALU.subtract).then_inc(pt_lo, 1)
                        if now and 1 <= s < NM + 1:
                            par = (c + s - 1) % 2
                            wait(dve, rot_hi, n * NM + s)
                            hi, lo = (kh[:], kl[:]) if s == 1 else (qh[:, s - 2, :], ql[:, s - 2, :])
                            nc.vector.tensor_tensor(lo, turn_cos[:, par, :], f32(hi), ALU.subtract).then_inc(rot_lo, 1)
                        if before and s - 2 in GATHERED:
                            gather(s - 2)
                    for u in range(NU + 1):
                        if now and u < NU:
                            wait(dve, scored, n * NU + u + 1)
                            dve.sem_inc(consts.passed[dve.engine], 1)
                            bank = bank_of_unit(u)
                            for q, (cols, win) in enumerate(((FIRST, window[:, P:2 * P]), (SECOND, window[:]))):
                                nc.vector.tensor_tensor_reduce(out=probs[:, u, cols], in0=bank[:, cols], in1=win, scale=1.0, scalar=4 * MASKED,
                                                               op0=ALU.add, op1=ALU.max, accum_out=top[:, u, q:q + 1]).then_inc(masked, 1)
                            wait(dve, masked, 2 * (n * NU + u + 1))
                            nc.vector.tensor_scalar(neg[:, u, :], top[:, u, :], -SCALE1, None, ALU.mult).then_inc(negated, 1)
                        if now and u >= 1:
                            divide(u - 1)
                        if before and u == 1:
                            gather(NW - 1)
                        if now and u == 2:
                            wait(dve, v_hi, n + 1)
                            nc.vector.tensor_tensor(vl[:].rearrange("p t d -> p (t d)"), banks[6][:], f32(vh[:].rearrange("p t d -> p (t d)")),
                                                    ALU.subtract).then_inc(v_lo, 1)
                        if before and u % 2 == 0 and u >= 2:
                            t = u // 2 - 1
                            wait(dve, wo_done, (n - 1) * CT + t + 1)
                            nc.vector.tensor_tensor(X[:, (c - 1) % C * CT + t, :], X[:, (c - 1) % C * CT + t, :], banks[4 + t % 2][:],
                                                    ALU.add).then_inc(y_ready, 1)

                dve.wait_ge(tables_in, 48)
                dve.wait_ge(y_ready, 1)
                groups(nc.vector, item)

            @block.tensor
            def _(pe):
                def item(g, c, before=True, now=True):
                    n = g * C + c
                    cols = slice(c * CW, (c + 1) * CW)

                    def tile(m):
                        if c == 0:
                            wait(pe, qkv_split, g * NQ + m + 1)
                        if m < 4:
                            wait(pe, masked, 2 * ((n - 1) * NU + (m - NJ) % 4 + 5) if before else 0)
                        else:
                            wait(pe, cosed, n * NM + m - 3)
                        for k in range(KD):
                            if m == 0:
                                w = (wk_h[:, k, :], wk_l[:, k, :])
                            elif m == NM:
                                w = (wv_h[:, k, :], wv_l[:, k, :])
                            else:
                                w = tuple(x[:, k, (m - 1) * HD:m * HD] for x in (wq_h, wq_l))
                            last = product(nc, bank_of_tile(m)[:], w, (xth[:, k, cols], xtl[:, k, cols]), k == 0, k == KD - 1)
                        last.then_inc(proj_done, 1)

                    def turn_values():
                        wait(pe, vt_copied, n + 1)
                        if before:
                            wait(pe, o_lo, (n - 1) * NV + 3)
                        for t in range(CT):
                            last = nc.tensor.transpose(banks[6][:, t * HD:(t + 1) * HD], vt[:, t * P:(t + 1) * P], consts.ident[:])
                        last.then_inc(v_turned, 1)

                    def turn(w):
                        b, part = w // 3, (2, 0, 1)[w % 3]
                        if w % 3 == 0:
                            wait(pe, normed, 2 * ((n - 1) * NU + (b + 1) * G))
                        if w < 2:
                            wait(pe, y_ready, (n - 1) * CT + 1)
                        else:
                            wait(pe, pt_lo, (n - 1) * NW + w - 1)
                        for h in range(G):
                            last = nc.tensor.transpose(banks[4 + w % 2][:, h * P:(h + 1) * P], probs[:, b * G + h, part * P:(part + 1) * P], consts.ident[:])
                        last.then_inc(pt_done, 1)

                    def weigh(x):
                        b, part = x // 3, x % 3
                        q, kt = (0, 0) if part == 0 else (1, part - 1)
                        if part < 2 and b == 1:
                            wait(pe, o_lo, (n - 1) * NV + q + 1)
                        if x == 0:
                            wait(pe, v_lo, n)
                        wait(pe, pt_lo, (n - 1) * NW + x + 1)
                        product(nc, banks[6 + q][:], (vh[:, 2 * b + kt, :], vl[:, 2 * b + kt, :]), (pth[:, x % 2, :], ptl[:, x % 2, :]),
                                part < 2, part != 1).then_inc(pv_done, 1)

                    for s in range(NW):
                        if now:
                            tile(s)
                        if before:
                            turn(s)
                        if before and s >= 1:
                            weigh(s - 1)
                    for u in range(NU):
                        if now:
                            b, h = u // G, u % G
                            if b == 0:
                                wait(pe, rot_lo, n * NM + h + 2)
                            if u < 3:
                                wait(pe, cosed, n * NM + u + 3)
                            elif u == 3:
                                wait(pe, vt_copied, n + 1)
                            else:
                                wait(pe, masked, 2 * (n * NU + u - 3))
                            bank, s0 = bank_of_unit(u), b * SEQ
                            product(nc, bank[:, FIRST], (qh[:, h, s0:s0 + P], ql[:, h, s0:s0 + P]), (kh[:, s0:s0 + P], kl[:, s0:s0 + P]), True, True)
                            product(nc, bank[:, SECOND], (qh[:, h, s0 + P:s0 + SEQ], ql[:, h, s0 + P:s0 + SEQ]),
                                    (kh[:, s0:s0 + SEQ], kl[:, s0:s0 + SEQ]), True, True).then_inc(scored, 1)
                        if before:
                            t = u // 2
                            tok = slice(t * P, (t + 1) * P)
                            if u % 2 == 0:
                                wait(pe, o_lo, (n - 1) * NV + t + 1)
                                if t == 0 and c == 1:
                                    wait(pe, o_split, g * G + G)
                                if t >= 2:
                                    wait(pe, y_ready, (n - 1) * CT + t)
                            for h in (0, 1) if u % 2 == 0 else (2, 3):
                                last = product(nc, banks[4 + t % 2][:], (oth[:, h, tok], otl[:, h, tok]), (wo_h[:, h, :], wo_l[:, h, :]), h == 0, h == G - 1)
                            if u % 2 == 1:
                                last.then_inc(wo_done, 1)
                            if u == 0:
                                weigh(NW - 1)
                        if now and u == 1:
                            turn_values()

                groups(nc.tensor, item)

        n = Norm(nc, ctx, signals, "ny", xt_width=0)
        xr = sb("xr", [P, NT, D])
        block = ctx.enter_context(nc.Block())

        @block.sync
        def _(sp):
            sp.dma_start(xr[:], a.parked.rearrange("(t p) d -> p t d", p=P)).then_inc(x_back, 16)

        @block.gpsimd
        def _(pool):
            pool.wait_ge(x_back, 16)
            for c in range(C):
                inverse_deviation(nc, pool, consts, n.stats_y, n.rstd_y, n.y_stats_done, n.y_var_eps, n.y_rstd_done, c)
                for t in range(CT):
                    pool.wait_ge(n.y_rows_done, c * CT + t + 1)
                    nc.gpsimd.tensor_tensor(X[:, c * CT + t, :], xr[:, c * CT + t, :], n.xn[:, t, :], ALU.add).then_inc(n.x_done, 1)

        @block.vector
        def _(dve):
            for c in range(C):
                def rows(t):
                    return X[:, c * CT + t, :]
                statistics(nc, dve, consts, n.raw_y, n.stats_y, n.y_raw_done, n.y_stats_done, rows, c)
                if c >= 1:
                    dve.wait_ge(n.x_done, c * CT)
                normalise(nc, dve, n.xn, rows, n.stats_y, n.rstd_y, n.y_rstd_done, n.y_rows_done, c)
    signals.clear()


def part4(nc, a, X, out, consts, banks):
    ctx, signals = ExitStack(), Signals(nc, "p4")
    with ctx:
        def sb(name, shape, dt=F32):
            return ctx.enter_context(nc.sbuf_tensor(f"p4_{name}", shape, dt))

        sem = signals.sem
        ER_ALL = NE * ER
        CATW = ER_ALL + NH
        BCAT, BDENSE, BGATE, BLORA = banks[4], banks[5:7], banks[7], banks[4:7]
        w_in, w_hi, w_lo, ones_set = sem("w_in"), sem("w_hi"), sem("w_lo"), sem("ones_set")
        cat_h, cat_l = sb("cat_h", [P, KD, CATW], F32R), sb("cat_l", [P, KD, CATW], F32R)
        dense_h, dense_l = sb("dense_h", [P, KD, D], F32R), sb("dense_l", [P, KD, D], F32R)
        lb_h, lb_l = sb("lb_h", [ER_ALL, D], F32R), sb("lb_l", [ER_ALL, D], F32R)
        gw2 = sb("gw2", [P, CT * NE])
        gb1, gamma, beta, gb2, experts = sb("gb1", [P, NH]), sb("gamma", [P, NH]), sb("beta", [P, NH]), sb("gb2", [P, NE]), sb("experts", [P, NE])
        ones = sb("ones", [P, P])
        pre = [Norm(nc, ctx, signals, f"n{i}", xt_width=0) for i in range(2)]
        xth, xtl = sb("xth", [P, KD, T], F32R), sb("xtl", [P, KD, T], F32R)
        y = sb("y", [P, NT, D])
        low = sb("low", [P, NT, ER_ALL])
        hidden = sb("hidden", [P, 2, CT, NH])
        h_raw, h_stats, h_rstd = sb("h_raw", [P, CT, 6]), sb("h_stats", [P, CT, 2]), sb("h_rstd", [P, CT])
        hidden_t = sb("hidden_t", [P, P])
        gates, top, where, where_f = sb("gates", [P, CT, NE]), sb("top", [P, CT, 8]), sb("where", [P, CT, 8], U32), sb("where_f", [P, CT, 8])
        second, share = sb("second", [P, CT]), sb("share", [P, NT, 2])
        chosen = sb("chosen", [P, NT, 2, NE])
        allowed, part, weight = sb("allowed", [P, 2, NE]), sb("part", [P, 2, NT, NE]), sb("weight", [P, NT, NE])
        scaled = sb("scaled", [P, 3, ER_ALL])
        sth, stl = sb("sth", [P, 3, P], F32R), sb("stl", [P, 3, P], F32R)

        with ExitStack() as raw_ctx:
            cat_raw, dense_raw, lb_raw = (raw_ctx.enter_context(nc.sbuf_tensor(f"p4_{name}", shape, F32)) for name, shape in
                                          (("cat_raw", [P, KD, CATW]), ("dense_raw", [P, KD, D]), ("lb_raw", [ER_ALL, D])))
            block = raw_ctx.enter_context(nc.Block())

            @block.sync
            def _(sp):
                sp.dma_start(cat_raw[:, :, 0:ER_ALL], a.lora_A.rearrange("(k p) n -> p k n", p=P)).then_inc(w_in, 16)
                sp.dma_start(cat_raw[:, :, ER_ALL:CATW], a.gw1.rearrange("(k p) n -> p k n", p=P)).then_inc(w_in, 16)
                sp.dma_start(dense_raw[:], a.dense.rearrange("(k p) n -> p k n", p=P)).then_inc(w_in, 16)
                sp.dma_start(lb_raw[:], a.lora_B).then_inc(w_in, 16)
                sp.dma_start(gw2[:], a.gw2).then_inc(w_in, 16)
                sp.dma_start(experts[:], a.experts).then_inc(w_in, 16)
                for dst, src, w in ((gb1, a.gb1, NH), (gamma, a.ln_gamma, NH), (beta, a.ln_beta, NH), (gb2, a.gb2, NE)):
                    sp.dma_start(dst[:], src.rearrange("(o n) -> o n", o=1).to_broadcast([P, w])).then_inc(w_in, 16)

            @block.gpsimd
            def _(pool):
                nc.gpsimd.memset(ones[:], 1.0).then_inc(ones_set, 1)

            @block.scalar
            def _(act):
                act.wait_ge(w_in, 160)
                for hi, raw in ((cat_h, cat_raw), (dense_h, dense_raw), (lb_h, lb_raw)):
                    nc.scalar.copy(hi[:], raw[:]).then_inc(w_hi, 1)

            @block.vector
            def _(dve):
                for i, (lo, raw, hi) in enumerate(((cat_l, cat_raw, cat_h), (dense_l, dense_raw, dense_h), (lb_l, lb_raw, lb_h))):
                    dve.wait_ge(w_hi, i + 1)
                    nc.vector.tensor_tensor(lo[:], raw[:], f32(hi[:]), ALU.subtract).then_inc(w_lo, 1)

        (cat_done, dense_done, low_read, hidden_sum, h_raw_done, h_stats_done, h_var, h_rstd_done, h_ready, ht_done, ht_copied, gates_done,
         gap_ready, gap_exp, is_chosen, counted, weighted, st_scaled, st_turned, st_hi, st_lo, lora_done, y_copied, y_summed, chain_sem, stored) = (
             sem(x) for x in "cat_done dense_done low_read hidden_sum h_raw_done h_stats_done h_var h_rstd_done h_ready ht_done ht_copied gates_done "
             "gap_ready gap_exp is_chosen counted weighted st_scaled st_turned st_hi st_lo lora_done y_copied y_summed chain stored".split())
        ny = pre[0]

        block = ctx.enter_context(nc.Block())

        @block.sync
        def _(sp):
            ov = out.rearrange("(t p) d -> p t d", p=P)
            for c in range(C):
                sp.wait_ge(ny.x_done, (c + 1) * CT)
                sp.dma_start(ov[:, c * CT:(c + 1) * CT, :], X[:, c * CT:(c + 1) * CT, :]).then_inc(stored, 16)
            sp.wait_ge(stored, 16 * C)

        @block.gpsimd
        def _(pool):
            def norm_x(c):
                n = pre[c % 2]
                inverse_deviation(nc, pool, consts, n.stats, n.rstd, n.stats_done, n.var_eps, n.rstd_done, c // 2)

            norm_x(0)
            for c in range(C):
                if c + 1 < C:
                    norm_x(c + 1)
                inverse_deviation(nc, pool, consts, h_stats, h_rstd, h_stats_done, h_var, h_rstd_done, c)
            for c in range(C):
                inverse_deviation(nc, pool, consts, ny.stats_y, ny.rstd_y, ny.y_stats_done, ny.y_var_eps, ny.y_rstd_done, c)
                for t in range(CT):
                    pool.wait_ge(ny.y_rows_done, c * CT + t + 1)
                    nc.gpsimd.tensor_tensor(X[:, c * CT + t, :], X[:, c * CT + t, :], y[:, c * CT + t, :], ALU.add).then_inc(ny.x_done, 1)

        @block.scalar
        def _(act):
            def hi_rows(c):
                n = pre[c % 2]
                for k in range(KD):
                    act.wait_ge(n.turned, c // 2 * KD + k + 1)
                    nc.scalar.copy(xth[:, k, c * CW:(c + 1) * CW], banks[k][:]).then_inc(n.hi_done, 1)

            def gate(c):
                act.wait_ge(ht_done, c + 1)
                nc.scalar.copy(hidden_t[:], BGATE[:, 0:P]).then_inc(ht_copied, 1)
                act.wait_ge(gap_ready, c + 1)
                nc.scalar.activation(second[:], second[:], ACT.Exp).then_inc(gap_exp, 1)

            hi_rows(0)
            for c in range(C):
                if c + 1 < C:
                    hi_rows(c + 1)
                for t in range(c * CT, (c + 1) * CT):
                    act.wait_ge(cat_done, t + 1)
                    nc.scalar.copy(low[:, t, :], BCAT[:, 0:ER_ALL]).then_inc(low_read, 1)
                    act.wait_ge(dense_done, t + 1)
                    nc.scalar.copy(y[:, t, :], BDENSE[t % 2][:]).then_inc(y_copied, 1)
                    if c >= 1 and t % CT == 1:
                        gate(c - 1)
            gate(C - 1)
            for t in range(NT):
                act.wait_ge(st_turned, t + 1)
                if t >= 3:
                    act.wait_ge(lora_done, t - 2)
                nc.scalar.copy(sth[:, t % 3, :], banks[t % 4][:, 0:P]).then_inc(st_hi, 1)

        @block.vector
        def _(dve):
            chain = Count(chain_sem)

            def rows(c):
                return lambda t: X[:, c * CT + t, :]

            def norm_rows(c):
                n = pre[c % 2]
                if c >= 2:
                    dve.wait_ge(n.turned, KD)
                statistics(nc, dve, consts, n.raw, n.stats, n.raw_done, n.stats_done, rows(c), c // 2)
                normalise(nc, dve, n.xn, rows(c), n.stats, n.rstd, n.rstd_done, n.rows_done, c // 2)

            def lo_rows(c):
                n, cols = pre[c % 2], slice(c * CW, (c + 1) * CW)
                for k in range(KD):
                    dve.wait_ge(n.hi_done, c // 2 * KD + k + 1)
                    nc.vector.tensor_tensor(xtl[:, k, cols], banks[k][:], f32(xth[:, k, cols]), ALU.subtract).then_inc(n.lo_done, 1)

            def over_tiles(row, w):
                return row[:].rearrange("p (o n) -> p o n", o=1).to_broadcast([P, CT, w])

            def hidden_rows(c):
                dve.wait_ge(hidden_sum, (c + 1) * CT)
                if c >= 1:
                    dve.wait_ge(h_rstd_done, c)
                statistics(nc, dve, consts, h_raw, h_stats, h_raw_done, h_stats_done, lambda t: hidden[:, c % 2, t, :], c)
                dve.wait_ge(h_rstd_done, c + 1)
                for t in range(CT):
                    ins = nc.vector.tensor_scalar(hidden[:, c % 2, t, :], hidden[:, c % 2, t, :], h_stats[:, t, 0:1], h_rstd[:, t:t + 1], ALU.subtract, ALU.mult)
                    chain.mark(ins)
                dve.wait_ge(chain.sem, chain.n)
                chain.link(dve, nc.vector.tensor_tensor(hidden[:, c % 2], hidden[:, c % 2], over_tiles(gamma, NH), ALU.mult))
                chain.link(dve, nc.vector.tensor_tensor(hidden[:, c % 2], hidden[:, c % 2], over_tiles(beta, NH), ALU.add))
                nc.vector.tensor_scalar(hidden[:, c % 2], hidden[:, c % 2], 0.0, None, ALU.max).then_inc(h_ready, 1)

            def choose(c):
                tiles = slice(c * CT, (c + 1) * CT)
                dve.wait_ge(gates_done, c + 1)
                chain.link(dve, nc.vector.tensor_tensor(gates[:], BGATE[:, P:P + CT * NE].rearrange("p (t e) -> p t e", e=NE),
                                                        over_tiles(gb2, NE), ALU.add))
                for t in range(CT):
                    chain.mark(nc.vector.max(top[:, t, :], gates[:, t, :]))
                dve.wait_ge(chain.sem, chain.n)
                for t in range(CT):
                    chain.mark(nc.vector.max_index(where[:, t, :], top[:, t, :], gates[:, t, :]))
                nc.vector.tensor_tensor(second[:], top[:, :, 1], top[:, :, 0], ALU.subtract).then_inc(gap_ready, 1)
                dve.wait_ge(chain.sem, chain.n)
                chain.link(dve, nc.vector.tensor_copy(where_f[:], where[:]))
                for k in range(2):
                    nc.vector.tensor_tensor(chosen[:, tiles, k, :], over_tiles(experts, NE), where_f[:, :, k:k + 1].to_broadcast([P, CT, NE]),
                                            ALU.is_equal).then_inc(is_chosen, 1)
                dve.wait_ge(gap_exp, c + 1)
                chain.link(dve, nc.vector.tensor_scalar(share[:, tiles, 1], second[:], 1.0, None, ALU.add))
                chain.link(dve, nc.vector.reciprocal(share[:, tiles, 0], share[:, tiles, 1]))
                chain.link(dve, nc.vector.tensor_tensor(share[:, tiles, 1], second[:], share[:, tiles, 0], ALU.mult))

            norm_rows(0)
            for c in range(C):
                if c + 1 < C:
                    norm_rows(c + 1)
                if c == 0:
                    lo_rows(0)
                if c + 1 < C:
                    lo_rows(c + 1)
                for t in range(c * CT, (c + 1) * CT):
                    dve.wait_ge(low_read, t + 1)
                    if t % CT == 0 and c >= 2:
                        dve.wait_ge(ht_done, c - 1)
                    nc.vector.tensor_tensor(hidden[:, c % 2, t % CT, :], BCAT[:, ER_ALL:CATW], gb1[:], ALU.add).then_inc(hidden_sum, 1)
                    if c >= 1 and t % CT == 1:
                        choose(c - 1)
                hidden_rows(c)
            choose(C - 1)
            dve.wait_ge(counted, 1)
            chain.link(dve, nc.vector.tensor_scalar(allowed[:], BGATE[:, 2 * P:2 * P + 2 * NE].rearrange("p (k e) -> p k e", e=NE),
                                                    float(CAPACITY), None, ALU.is_le))
            for k in range(2):
                chain.mark(nc.vector.scalar_tensor_tensor(out=part[:, k, :, :], in0=chosen[:, :, k, :], scalar=1.0 / ER,
                                                          in1=share[:, :, k:k + 1].to_broadcast([P, NT, NE]), op0=ALU.mult, op1=ALU.mult))
            dve.wait_ge(chain.sem, chain.n)
            for k in range(2):
                chain.mark(nc.vector.tensor_tensor(part[:, k, :, :], part[:, k, :, :],
                                                   allowed[:, k:k + 1, :].to_broadcast([P, NT, NE]), ALU.mult))
            dve.wait_ge(chain.sem, chain.n)
            nc.vector.tensor_tensor(weight[:], part[:, 0, :, :], part[:, 1, :, :], ALU.add).then_inc(weighted, 1)
            dve.wait_ge(weighted, 1)
            for s in range(NT + 5):
                if s < NT:
                    if s >= 3:
                        dve.wait_ge(st_turned, s - 2)
                    nc.vector.tensor_tensor(scaled[:, s % 3, :].rearrange("p (e r) -> p e r", r=ER), low[:, s, :].rearrange("p (e r) -> p e r", r=ER),
                                            weight[:, s, :].rearrange("p (e o) -> p e o", o=1).to_broadcast([P, NE, ER]), ALU.mult).then_inc(st_scaled, 1)
                if 1 <= s < NT + 1:
                    t = s - 1
                    dve.wait_ge(st_hi, t + 1)
                    nc.vector.tensor_tensor(stl[:, t % 3, :], banks[t % 4][:, 0:P], f32(sth[:, t % 3, :]), ALU.subtract).then_inc(st_lo, 1)
                if 3 <= s < NT + 3:
                    t = s - 3
                    dve.wait_ge(lora_done, t + 1)
                    dve.wait_ge(y_copied, t + 1)
                    nc.vector.tensor_tensor(y[:, t, :], y[:, t, :], BLORA[t % 3][:], ALU.add).then_inc(y_summed, 1)
                    if t % CT == CT - 1:
                        c = t // CT
                        dve.wait_ge(y_summed, (c + 1) * CT)

                        def y_rows(t):
                            return y[:, c * CT + t, :]

                        if c >= 1:
                            dve.wait_ge(ny.y_rstd_done, c)
                        statistics(nc, dve, consts, ny.raw_y, ny.stats_y, ny.y_raw_done, ny.y_stats_done, y_rows, c)
                        normalise(nc, dve, y[:, c * CT:(c + 1) * CT, :], y_rows, ny.stats_y, ny.rstd_y, ny.y_rstd_done, ny.y_rows_done, c)

        @block.tensor
        def _(pe):
            def turn(c):
                if c >= 1:
                    pe.wait_ge(pre[(c - 1) % 2].lo_done, ((c - 1) // 2 + 1) * KD)
                turn_rows(nc, pe, pre[c % 2], consts, lambda k: banks[k], c // 2)

            def gate(c):
                pe.wait_ge(h_ready, c + 1)
                nc.tensor.transpose(BGATE[:, 0:P], hidden[:, c % 2].rearrange("p t n -> p (t n)"), consts.ident[:]).then_inc(ht_done, 1)
                pe.wait_ge(ht_copied, c + 1)
                nc.tensor.matmul(BGATE[:, P:P + CT * NE], hidden_t[:], gw2[:], start=True, stop=True).then_inc(gates_done, 1)

            turn(0)
            for c in range(C):
                if c + 1 < C:
                    turn(c + 1)
                n = pre[c % 2]
                pe.wait_ge(n.lo_done, (c // 2 + 1) * KD)
                for t in range(c * CT, (c + 1) * CT):
                    tok = slice(t * P, (t + 1) * P)
                    if t >= 1:
                        pe.wait_ge(hidden_sum, t)
                    for k in range(KD):
                        last = product(nc, BCAT[:, 0:CATW], (xth[:, k, tok], xtl[:, k, tok]), (cat_h[:, k, :], cat_l[:, k, :]), k == 0, k == KD - 1)
                    last.then_inc(cat_done, 1)
                    if t >= 2:
                        pe.wait_ge(y_copied, t - 1)
                    for k in range(KD):
                        last = product(nc, BDENSE[t % 2][:], (xth[:, k, tok], xtl[:, k, tok]), (dense_h[:, k, :], dense_l[:, k, :]), k == 0, k == KD - 1)
                    last.then_inc(dense_done, 1)
                    if c >= 1 and t % CT == 1:
                        gate(c - 1)
            gate(C - 1)
            pe.wait_ge(is_chosen, 2 * C)
            for t in range(NT):
                last = nc.tensor.matmul(BGATE[:, 2 * P:2 * P + 2 * NE], ones[:], chosen[:, t, :, :].rearrange("p k e -> p (k e)"),
                                        start=t == 0, stop=t == NT - 1)
            last.then_inc(counted, 1)
            for s in range(NT + 2):
                if s < NT:
                    pe.wait_ge(st_scaled, s + 1)
                    if s >= 4:
                        pe.wait_ge(st_lo, s - 3)
                    nc.tensor.transpose(banks[s % 4][:, 0:P], scaled[:, s % 3, :], consts.ident[:]).then_inc(st_turned, 1)
                if s >= 2:
                    t = s - 2
                    pe.wait_ge(st_lo, t + 1)
                    if t >= 3:
                        pe.wait_ge(y_summed, t - 2)
                    product(nc, BLORA[t % 3][:], (sth[:, t % 3, :], stl[:, t % 3, :]), (lb_h[:], lb_l[:]), True, True).then_inc(lora_done, 1)
    signals.clear()


def program(nc, a, out):
    ctx = ExitStack()
    with ctx:
        banks = [ctx.enter_context(nc.psum_tensor(f"bank{i}", [P, 512], F32)) for i in range(8)]
        consts = Constants(nc, ctx, a)
        X = ctx.enter_context(nc.sbuf_tensor("X", [P, NT, D], F32))
        with ExitStack() as ffn_ctx:
            ffn = FfnWeights(nc, ffn_ctx, a)
            part1(nc, a, X, ffn, consts, banks)
            part2(nc, a, X, ffn, consts, banks)
        part3(nc, a, X, consts, banks)
        part4(nc, a, X, out, consts, banks)


class Inputs:
    pass


def _stacked(w):
    w = w.reshape(2, 4, E0, -1)
    return np.concatenate([w, w, w, np.zeros_like(w)], axis=2).reshape(2 * P, -1)


def kernel(**inputs):
    import concourse.bacc as bacc
    from concourse.bass_utils import run_bass_kernel_spmd

    v = {k: np.asarray(x) for k, x in inputs.items()}
    lay = {}
    lay["x"] = v["L0_attn_x"].reshape(T, D)
    wqk = v["L0_attn_Wqk_w"].reshape(HEADS0 * E0, 2, D)
    bqk = v["L0_attn_Wqk_b"].reshape(HEADS0 * E0, 2)
    lay["wqk"] = np.concatenate([_stacked(wqk[:, s]) for s in range(2)]).T
    lay["bqk"] = np.concatenate([_stacked(bqk[:, s]) for s in range(2)]).reshape(4, P).T
    lay["wv"], lay["bv"] = v["L0_attn_Wv_w"].T, v["L0_attn_Wv_b"]
    lay["wo0"], lay["bo"] = v["L0_attn_Wo_w"].T, v["L0_attn_Wo_b"]
    pad = IP - INNER
    for n in ("gate", "up"):
        lay[f"{n}_q"] = np.pad(v[f"L0_ffn_{n}_q"], ((0, pad), (0, 0))).T
        lay[f"{n}_scale"] = np.pad(v[f"L0_ffn_{n}_scale"], (0, pad)).reshape(NI, P).T
        lay[f"{n}_A"] = np.tile(v[f"L0_ffn_{n}_A"], (1, 4))
        lay[f"{n}_B"] = np.tile(np.pad(v[f"L0_ffn_{n}_B"], ((0, 0), (0, pad))), (4, 1))
    lay["down_q"] = np.pad(v["L0_ffn_down_q"], ((0, 0), (0, pad))).T
    lay["down_scale"] = v["L0_ffn_down_scale"]
    lay["down_A"] = np.tile(np.pad(v["L0_ffn_down_A"], ((0, pad), (0, 0))), (1, 4))
    lay["down_B"] = np.tile(v["L0_ffn_down_B"], (4, 1))
    for n in ("wq", "wk", "wv", "wo"):
        lay[f"{n}1"] = v[f"L1_attn_{n}"]
    lay["dense"] = v["L1_ffn_weight"].T
    lay["lora_A"] = v["L1_ffn_lora_A"].transpose(1, 0, 2).reshape(D, NE * ER)
    lay["lora_B"] = v["L1_ffn_lora_B"].reshape(NE * ER, D)
    lay["gw1"] = v["L1_ffn_gw1"].T
    lay["gw2"] = np.zeros((CT, NH, CT, NE), np.float32)
    for t in range(CT):
        lay["gw2"][t, :, t, :] = v["L1_ffn_gw2"].T
    lay["gw2"] = lay["gw2"].reshape(P, CT * NE)
    for n in ("gb1", "ln_gamma", "ln_beta", "gb2"):
        lay[n] = v[f"L1_ffn_{n}"]

    row = np.arange(P)
    lo_rows = [(row % 32 // 8 == 2), (row % 32 // 8 == 1), (row // 32 % 2 == 1), (row // 64 == 1)]
    lay["masks"] = -np.stack(lo_rows, 1).astype(np.float32)
    lay["ident"] = np.eye(P, dtype=np.float32)
    half = HD // 2
    inv_freq = np.float32(10000.0) ** (-np.arange(half, dtype=np.float32) / np.float32(half))
    angle = inv_freq[:, None] * np.arange(SEQ, dtype=np.float32)[None, :]
    lay["cos"] = np.tile(np.cos(angle), (2, 1))
    lay["sin"] = np.concatenate([-np.sin(angle), np.sin(angle)])
    older, same = row[None, :] > row[:, None], row[None, :] <= row[:, None]
    lay["window"] = np.where(np.concatenate([older, same], 1), 0, MASKED).astype(np.float32)
    lay["experts"] = np.tile(np.arange(NE, dtype=np.float32), (P, 1))

    nc = bacc.Bacc("TRN2", target_bir_lowering=False, num_devices=1, dynamic_dma_scratch_size=1024)
    a, arrays = Inputs(), {}
    for name, x in lay.items():
        arrays[f"in_{name}"] = np.ascontiguousarray(x)
        a.__dict__[name] = nc.dram_tensor(f"in_{name}", x.shape, mybir.dt.from_np(x.dtype), kind="ExternalInput").ap()
    out = nc.dram_tensor("out", (T, D), F32, kind="ExternalOutput").ap()
    a.parked = nc.dram_tensor("parked", (T, D), F32, kind="Internal").ap()
    program(nc, a, out)
    r = run_bass_kernel_spmd(nc, [arrays], core_ids=[0])
    return r.results[0]["out"].reshape(BATCH, SEQ, D)
```

```python
from contextlib import ExitStack

import numpy as np

import concourse.bass as bass
from concourse import mybir

F32, F32R, I32, U32 = mybir.dt.float32, mybir.dt.float32r, mybir.dt.int32, mybir.dt.uint32
ALU, ACT, AX = mybir.AluOpType, mybir.ActivationFunctionType, mybir.AxisListType

P = 128
BATCH, SEQ, D = 8, 256, 512
T = BATCH * SEQ
NT = T // P
KD = D // P
C, CT = 4, 4
CW = CT * P
CB = CW // SEQ
EPS = 1e-5

HEADS0, E0 = 8, 8
ROWS0 = 32

INNER, RANK = 1376, 32
NI = -(-INNER // P)
IP = NI * P
Q_ZERO, Q_STEP, LR_SCALE = 7.5, 0.005, 0.02

KV, G, HD = 8, 4, 128
SCALE1 = HD ** -0.5
MASKED = -1e30

NE, ER = 8, 16
NH = 4 * NE
CAPACITY = int(3.0 * T / NE)


class Count:

    def __init__(self, sem, per=0):
        self.sem, self.per, self.base, self.n = sem, per, 0, 0

    def turn(self, c):
        self.base, self.n = c * self.per, 0

    def mark(self, ins):
        self.n += 1
        return ins.then_inc(self.sem, 1)

    def link(self, eng, ins):
        self.mark(ins)
        eng.wait_ge(self.sem, self.base + self.n)


def product(nc, out, lhs, rhs, start, stop):
    nc.tensor.matmul(out, lhs[0], rhs[0], start=start, stop=False)
    nc.tensor.matmul(out, lhs[0], rhs[1], start=False, stop=False)
    return nc.tensor.matmul(out, lhs[1], rhs[0], start=False, stop=stop)


def f32(ap):
    return ap.bitcast(F32)


class Constants:

    def __init__(self, nc, ctx, a):
        self.ident = ctx.enter_context(nc.sbuf_tensor("ident", [P, P], F32))
        self.masks = ctx.enter_context(nc.sbuf_tensor("masks", [P, 4], F32))
        self.minus_half = ctx.enter_context(nc.sbuf_tensor("minus_half", [P, CT], F32))
        self.minus_zero = ctx.enter_context(nc.sbuf_tensor("minus_zero", [P, 1], F32))
        self.ready = ctx.enter_context(nc.semaphore("consts_ready"))
        self.passed = {e.engine: ctx.enter_context(nc.semaphore(f"passed{i}")) for i, e in enumerate((nc.vector, nc.gpsimd, nc.tensor))}
        with nc.Block() as block:
            @block.sync
            def _(sp):
                sp.dma_start(self.ident[:], a.ident).then_inc(self.ready, 16)
                sp.dma_start(self.masks[:], a.masks).then_inc(self.ready, 16)
                sp.wait_ge(self.ready, 32)

            @block.gpsimd
            def _(pool):
                nc.gpsimd.memset(self.minus_half[:], -0.5)
                nc.gpsimd.memset(self.minus_zero[:], -Q_ZERO)


class Signals:

    def __init__(self, nc, tag):
        self.nc, self.tag, self.made = nc, tag, []

    def sem(self, name):
        self.made.append(self.nc.alloc_semaphore(f"{self.tag}_{name}"))
        return self.made[-1]

    def clear(self):
        numbers = sorted(s.num for s in self.made)
        firsts = [x for x in numbers if x - 1 not in numbers]
        with self.nc.Block() as block:
            @block.sync
            def _(sp):
                for first in firsts:
                    stop = next(x for x in range(first, numbers[-1] + 2) if x not in numbers)
                    sp.sem_clear(range(first, stop))
        for s in self.made:
            self.nc.release_semaphore(s)


class Norm:

    def __init__(self, nc, ctx, signals, tag, xn=True, xt_width=CW):
        def sb(name, shape, dt=F32):
            return ctx.enter_context(nc.sbuf_tensor(f"{signals.tag}_{tag}_{name}", shape, dt))

        def sem(name):
            return signals.sem(f"{tag}_{name}")

        self.raw = sb("raw", [P, CT, 6])
        self.stats = sb("stats", [P, CT, 2])
        self.rstd = sb("rstd", [P, CT])
        if xn:
            self.xn = sb("xn", [P, CT, D])
        if xt_width:
            self.xth, self.xtl = sb("xth", [P, KD, xt_width], F32R), sb("xtl", [P, KD, xt_width], F32R)
        self.raw_y = sb("raw_y", [P, CT, 6])
        self.stats_y = sb("stats_y", [P, CT, 2])
        self.rstd_y = sb("rstd_y", [P, CT])
        self.raw_done, self.stats_done, self.var_eps, self.rstd_done = sem("raw_done"), sem("stats_done"), sem("var_eps"), sem("rstd_done")
        self.rows_done, self.turned, self.hi_done, self.lo_done = sem("rows_done"), sem("turned"), sem("hi_done"), sem("lo_done")
        self.y_raw_done, self.y_stats_done, self.y_var_eps, self.y_rstd_done = sem("y_raw_done"), sem("y_stats_done"), sem("y_var_eps"), sem("y_rstd_done")
        self.y_rows_done, self.x_done = sem("y_rows_done"), sem("x_done")


class Arrivals:

    def __init__(self, nc, ctx, signals):
        self.buf = ctx.enter_context(nc.sbuf_tensor("arrivals", [P, KD * D], F32))
        self.a_in, self.q_in, self.parked = signals.sem("a_in"), signals.sem("q_in"), signals.sem("parked")

    def a_raw(self, i):
        return self.buf[:, i * KD * P:(i + 1) * KD * P].rearrange("p (k n) -> p k n", k=KD)

    def group_raw(self):
        return self.buf[:].rearrange("p (k n) -> p k n", k=KD)


def statistics(nc, eng, consts, raw, stats, raw_done, stats_done, rows, c):
    for t in range(CT):
        nc.vector.bn_stats(raw[:, t, :], rows(t)).then_inc(raw_done, 1)
    for t in range(CT):
        eng.wait_ge(raw_done, c * CT + t + 1)
        eng.sem_inc(consts.passed[eng.engine], 1)
        nc.vector.bn_aggr(stats[:, t, :], raw[:, t, :]).then_inc(stats_done, 1)


def inverse_deviation(nc, eng, consts, stats, rstd, stats_done, var_eps, rstd_done, c):
    eng.wait_ge(stats_done, (c + 1) * CT)
    eng.sem_inc(consts.passed[eng.engine], 1)
    nc.gpsimd.tensor_scalar(rstd[:, :], stats[:, :, 1], EPS, None, ALU.add).then_inc(var_eps, 1)
    eng.wait_ge(var_eps, c + 1)
    nc.gpsimd.tensor_tensor(rstd[:, :], rstd[:, :], consts.minus_half[:], ALU.pow).then_inc(rstd_done, 1)


def normalise(nc, eng, out, rows, stats, rstd, rstd_done, done, c):
    eng.wait_ge(rstd_done, c + 1)
    for t in range(CT):
        nc.vector.tensor_scalar(out[:, t, :], rows(t), stats[:, t, 0:1], rstd[:, t:t + 1],
                                ALU.subtract, ALU.mult).then_inc(done, 1)


def turn_rows(nc, eng, norm, consts, bank_of, c):
    eng.wait_ge(norm.rows_done, (c + 1) * CT)
    for k in range(KD):
        for t in range(CT):
            last = nc.tensor.transpose(bank_of(k)[:, t * P:(t + 1) * P], norm.xn[:, t, k * P:(k + 1) * P], consts.ident[:])
        last.then_inc(norm.turned, 1)


def residual(nc, eng, norm, X, c, number, tiles=range(CT)):
    for t in tiles:
        eng.wait_ge(norm.y_rows_done, number * CT + t + 1)
        nc.gpsimd.tensor_tensor(X[:, c * CT + t, :], X[:, c * CT + t, :], norm.xn[:, t, :], ALU.add).then_inc(norm.x_done, 1)


def part1(nc, a, X, n, ffn, arrivals, consts, banks):
    ctx, signals = ExitStack(), Signals(nc, "p1")
    with ctx:
        def sb(name, shape, dt=F32):
            return ctx.enter_context(nc.sbuf_tensor(f"p1_{name}", shape, dt))

        def sem(name):
            return signals.sem(name)

        M4 = 4
        NU = 4 * CB * 2
        VC = HEADS0 * E0
        wqk_h, wqk_l = sb("wqk_h", [P, KD, M4 * P], F32R), sb("wqk_l", [P, KD, M4 * P], F32R)
        wv_h, wv_l = sb("wv_h", [P, KD, VC], F32R), sb("wv_l", [P, KD, VC], F32R)
        wo_h, wo_l = sb("wo_h", [P, D], F32R), sb("wo_l", [P, D], F32R)
        bo = sb("bo", [P, D])
        rows_max = max(rows * row for _, _, rows, row in ffn.rows)
        q_raw, spare = arrivals.buf[:, 0:rows_max].bitcast(I32), arrivals.buf[:, rows_max:] 
        negmax, spare = spare[:, 0:2 * NU].rearrange("p (u j) -> p u j", j=2), spare[:, 2 * NU:]
        sums, rsums = (spare[:, i * 2 * CB * HEADS0:(i + 1) * 2 * CB * HEADS0].rearrange("p (b q h) -> p b q h", b=CB, q=2) for i in range(2))
        bqk, spare = spare[:, 4 * CB * HEADS0:4 * CB * HEADS0 + M4], spare[:, 4 * CB * HEADS0 + M4:]
        v32, bv = spare[:, 0:CT * VC].rearrange("p (t v) -> p t v", v=VC), spare[:, CT * VC:(CT + 1) * VC]
        x_first, x_rest, w_in = sem("x_first"), sem("x_rest"), sem("w_in")
        w_hi, w_lo = sem("w_hi"), sem("w_lo")
        xv = a.x.rearrange("(t p) d -> p t d", p=P)

        with ExitStack() as raw_ctx:
            wqk_raw, wv_raw, wo_raw = (raw_ctx.enter_context(nc.sbuf_tensor(f"p1_{name}", shape, F32)) for name, shape in
                                       (("wqk_raw", [P, KD, M4 * P]), ("wv_raw", [P, KD, VC]), ("wo_raw", [P, D])))
            block = raw_ctx.enter_context(nc.Block())

            @block.sync
            def _(sp):
                sp.dma_start(X[:, 0:CT, :], xv[:, 0:CT, :]).then_inc(x_first, 16)
                sp.dma_start(wqk_raw[:], a.wqk.rearrange("(k p) m -> p k m", p=P)).then_inc(w_in, 16)
                sp.dma_start(wv_raw[:], a.wv.rearrange("(k p) m -> p k m", p=P)).then_inc(w_in, 16)
                sp.dma_start(wo_raw[:], a.wo0).then_inc(w_in, 16)
                for dst, src in ((bqk, a.bqk),
                                 (bv, a.bv.rearrange("(o n) -> o n", o=1).to_broadcast([P, VC])),
                                 (bo[:], a.bo.rearrange("(o n) -> o n", o=1).to_broadcast([P, D]))):
                    sp.dma_start(dst, src).then_inc(w_in, 16)

            @block.scalar
            def _(act):
                act.wait_ge(w_in, 16 * 6)
                nc.scalar.copy(wqk_h[:], wqk_raw[:]).then_inc(w_hi, 1)
                nc.scalar.copy(wv_h[:], wv_raw[:]).then_inc(w_hi, 1)
                nc.scalar.copy(wo_h[:], wo_raw[:]).then_inc(w_hi, 1)

            @block.gpsimd
            def _(pool):
                inverse_deviation(nc, pool, consts, n.stats, n.rstd, n.stats_done, n.var_eps, n.rstd_done, 0)

            @block.vector
            def _(dve):
                dve.wait_ge(x_first, 16)
                first_rows = lambda t: X[:, t, :]
                statistics(nc, dve, consts, n.raw, n.stats, n.raw_done, n.stats_done, first_rows, 0)
                normalise(nc, dve, n.xn, first_rows, n.stats, n.rstd, n.rstd_done, n.rows_done, 0)
                for i, (lo, raw, hi) in enumerate(((wqk_l, wqk_raw, wqk_h), (wv_l, wv_raw, wv_h), (wo_l, wo_raw, wo_h))):
                    dve.wait_ge(w_hi, i + 1)
                    nc.vector.tensor_tensor(lo[:], raw[:], f32(hi[:]), ALU.subtract).then_inc(w_lo, 1)

        qk32, qkh = sb("qk32", [P, 2, CW]), sb("qkh", [P, 2, CW], F32R)
        stack = sb("stack", [P, M4, CW], F32R)
        STEP = P + E0
        vm = sb("vm", [P, CT, HEADS0 * STEP], F32R)
        probs = sb("probs", [P, 3, 512])
        pth, ptl = sb("pth", [P, 2, 4, SEQ], F32R), sb("ptl", [P, 2, 4, SEQ], F32R)
        spread, divisor, o32 = qk32[:, 1, 0:2 * P].rearrange("p (q n) -> p q n", q=2), qk32[:, 0, 0:SEQ], qk32[:, 0, SEQ:2 * SEQ]
        oth, otl = qkh[:, 0, :], qkh[:, 1, :]
        b_raw, b_hi = arrivals.buf[:, 0:2 * D].rearrange("p (i n) -> p i n", i=2), wqk_h[:, 0:2, :]

        q_in, q_used = sem("q_in"), sem("q_used")
        small_in, b_in, b_hi_done, b_stacked = sem("small_in"), [sem("b_in0"), sem("b_in1")], sem("b_hi_done"), sem("b_stacked")
        qk_done, qk_hi, stacked = sem("qk_done"), sem("qk_hi"), sem("stacked")
        v_done, v_sum, v_hi, v_lo = sem("v_done"), sem("v_sum"), sem("v_hi"), sem("v_lo")
        scored, maxed, exped, pt_done, pt_hi, pt_lo, pv_done = (sem(x) for x in "scored maxed exped pt_done pt_hi pt_lo pv_done".split())
        v_cleared, inverted, spread_done, divisor_done, divisor_copied, o_done, ot_hi, ot_lo = (
            sem(x) for x in "v_cleared inverted spread_done divisor_done divisor_copied o_done ot_hi ot_lo".split())
        wo_done, y_ready = sem("wo_done"), sem("y_ready")

        def vm_part(start):
            return vm[:].rearrange("p t (h w) -> p t h w", w=STEP)[:, :, :, start:start + E0]

        def pair_part(buffer, u):
            return buffer[:, u // 2 % 2, :, u % 2 * P:(u % 2 + 1) * P]

        NQ = len(ffn.rows)

        def q_rows(c, i):
            w, q, rows, row = ffn.rows[i]
            at, n = c * rows, min(rows, w.shape[1] - c * rows) if isinstance(c, int) else rows
            return w[:, bass.ds(at, n), :], q[:, bass.ds(at, n), :], q_raw[:, 0:n * row].rearrange("p (r n) -> p r n", n=row)

        block = ctx.enter_context(nc.Block())

        @block.sync
        def _(sp):
            sp.dma_start(X[:, CT:NT, :], xv[:, CT:NT, :]).then_inc(x_rest, 16)
            for dst, src in ffn.small:
                sp.dma_start(dst, src).then_inc(small_in, 16)

            def load_rows(c):
                for i in range(NQ):
                    _, src, raw = q_rows(c, i)
                    if not (isinstance(c, int) and c * NQ + i == 0):
                        sp.wait_ge(q_used, c * NQ + i)
                    sp.dma_start(raw, src).then_inc(q_in, 16)

            load_rows(0)
            with nc.sync.Fori(1, C - 1) as c:
                load_rows(c)
            load_rows(C - 1)
            sp.wait_ge(q_used, C * NQ)
            for i, (dst, src, w) in enumerate(ffn.stacks):
                if i >= 2:
                    sp.wait_ge(b_stacked, i - 1)
                sp.dma_start(b_raw[:, i % 2, 0:w], src).then_inc(b_in[i % 2], 16)
            for i, src in enumerate((a.gate_A, a.up_A)):
                sp.wait_ge(b_stacked, len(ffn.stacks))
                sp.dma_start(arrivals.a_raw(i), src.rearrange("(k p) n -> p k n", p=P)).then_inc(arrivals.a_in, 16)
            sp.wait_ge(small_in, 16 * len(ffn.small))

        @block.gpsimd
        def _(pool):
            nc.gpsimd.memset(f32(vm[:]), 0.0).then_inc(v_cleared, 1)
            pool.sem_inc(n.x_done, 1)

            def turn(c, last_turn):
                inverse_deviation(nc, pool, consts, n.stats, n.rstd, n.stats_done, n.var_eps, n.rstd_done, c + 1)
                if not last_turn:
                    inverse_deviation(nc, pool, consts, n.stats_y, n.rstd_y, n.y_stats_done, n.y_var_eps, n.y_rstd_done, c)
                    residual(nc, pool, n, X, c, c)

            with nc.gpsimd.Fori(0, C - 1) as c:
                turn(c, False)
            turn(C - 1, True)

        @block.scalar
        def _(act):
            def hi_rows(c):
                for k in range(KD):
                    act.wait_ge(n.turned, c * KD + k + 1)
                    nc.scalar.copy(n.xth[:, k, :], banks[k][:]).then_inc(n.hi_done, 1)

            def divisor_rows(c, b):
                cols = slice(b * SEQ, (b + 1) * SEQ)
                act.wait_ge(divisor_done, c * CB + b + 1)
                nc.scalar.copy(divisor, banks[6 + b][:, SEQ:2 * SEQ]).then_inc(divisor_copied, 1)
                act.wait_ge(o_done, c * CB + b + 1)
                nc.scalar.copy(oth[:, cols], o32).then_inc(ot_hi, 1)

            hi_rows(0)
            act.wait_ge(v_cleared, 1)

            def turn(c, last_turn):
                for m in range(M4):
                    act.wait_ge(qk_done, c * M4 + m + 1)
                    if m >= 2:
                        act.wait_ge(stacked, c * M4 + m - 1)
                    nc.scalar.activation(qk32[:, m % 2, :], banks[m][:], ACT.Identity, bias=bqk[:, m:m + 1])
                    nc.scalar.activation(qkh[:, m % 2, :], banks[m][:], ACT.Identity, bias=bqk[:, m:m + 1]).then_inc(qk_hi, 1)
                for s in range(NU + 6):
                    if s >= 3 and s < NU + 3:
                        u = s - 3
                        act.wait_ge(pt_done, c * NU + u + 1)
                        if u >= 4:
                            act.wait_ge(pv_done, c * NU + u // 2 * 2 - 2)
                        nc.scalar.copy(pair_part(pth, u), banks[4 + u % 2][:].rearrange("p (f q) -> p f q", q=P)).then_inc(pt_hi, 1)
                    if s < NU:
                        act.wait_ge(maxed, c * NU + s + 1)
                        if s >= 3:
                            act.wait_ge(pt_done, c * NU + s - 2)
                        for j in range(2):
                            nc.scalar.activation(probs[:, s % 3, j * SEQ:(j + 1) * SEQ], banks[s % 4][:, j * SEQ:(j + 1) * SEQ],
                                                 ACT.Exp, bias=negmax[:, s, j:j + 1],
                                                 accum_out=sums[:, s // 8, s % 2, 4 * j + s // 2 % 4:4 * j + s // 2 % 4 + 1]).then_inc(exped, 1)
                    if s == 2:
                        act.wait_ge(v_sum, c + 1)
                        nc.scalar.copy(vm_part(0), v32.rearrange("p t (h e) -> p t h e", e=E0)).then_inc(v_hi, 1)
                    if s in (1, 5, 9):
                        i = s // 4
                        dst, _, raw = q_rows(c, i)
                        act.wait_ge(q_in, 16 * (c * NQ + i + 1))
                        nc.scalar.activation(dst, raw, ACT.Identity, bias=consts.minus_zero[:]).then_inc(q_used, 1)
                    if last_turn and 0 <= s - 10 < len(ffn.stacks):
                        i = s - 10
                        w = ffn.stacks[i][2]
                        act.wait_ge(b_in[i % 2], 16 * (i // 2 + 1))
                        if i >= 2:
                            act.wait_ge(b_stacked, i - 1)
                        nc.scalar.copy(b_hi[:, i % 2, 0:w], b_raw[:, i % 2, 0:w]).then_inc(b_hi_done, 1)
                    if s == 14:
                        divisor_rows(c, 0)
                divisor_rows(c, 1)
                hi_rows(c + 1)

            with nc.scalar.Fori(0, C - 1) as c:
                turn(c, False)
            turn(C - 1, True)

        @block.vector
        def _(dve):
            def lo_rows(c):
                for k in range(KD):
                    dve.wait_ge(n.hi_done, c * KD + k + 1)
                    nc.vector.tensor_tensor(n.xtl[:, k, :], banks[k][:], f32(n.xth[:, k, :]), ALU.subtract).then_inc(n.lo_done, 1)

            def rows(c):
                first = 0 if isinstance(c, int) and c == C else c * CT
                return lambda t: X[:, first + t, :]

            def result_rows(c, b):
                cols = slice(b * SEQ, (b + 1) * SEQ)
                dve.wait_ge(divisor_copied, c * CB + b + 1)
                nc.vector.tensor_tensor(o32, banks[6 + b][:, 0:SEQ], divisor, ALU.mult).then_inc(o_done, 1)
                dve.wait_ge(ot_hi, c * CB + b + 1)
                nc.vector.tensor_tensor(otl[:, cols], o32, f32(oth[:, cols]), ALU.subtract).then_inc(ot_lo, 1)

            dve.sem_inc(y_ready, 1)
            lo_rows(0)
            dve.wait_ge(x_rest, 16)

            def turn(c, last_turn):
                for m in range(M4):
                    dve.wait_ge(qk_hi, c * M4 + m + 1)
                    nc.vector.scalar_tensor_tensor(out=stack[:, m, :], in0=f32(qkh[:, m % 2, :]), scalar=consts.masks[:, m // 2:m // 2 + 1],
                                                   in1=qk32[:, m % 2, :], op0=ALU.mult, op1=ALU.add).then_inc(stacked, 1)
                dve.wait_ge(n.x_done, c * CT + 1)

                def maxima(u):
                    dve.wait_ge(scored, c * NU + u + 1)
                    nc.vector.tensor_reduce(negmax[:, u, :], banks[u % 4][:].rearrange("p (j k) -> p j k", j=2), AX.X, ALU.max,
                                            negate=True).then_inc(maxed, 1)

                maxima(0)
                for s in range(NU + 3):
                    if s + 1 < NU:
                        maxima(s + 1)
                    if s == 1:
                        if last_turn:
                            dve.wait_ge(n.x_done, CT + 1)
                        statistics(nc, dve, consts, n.raw, n.stats, n.raw_done, n.stats_done, rows(c + 1), c + 1)
                    if s == 2:
                        dve.wait_ge(v_done, c + 1)
                        nc.vector.tensor_tensor(v32, banks[5][:, 0:CT * VC].rearrange("p (t v) -> p t v", v=VC),
                                                bv.rearrange("p (o v) -> p o v", o=1).to_broadcast([P, CT, VC]), ALU.add).then_inc(v_sum, 1)
                    if s == 3:
                        dve.wait_ge(v_hi, c + 1)
                        nc.vector.tensor_tensor(vm_part(VC), v32.rearrange("p t (h e) -> p t h e", e=E0), f32(vm_part(0)), ALU.subtract).then_inc(v_lo, 1)
                    if s >= 3:
                        u = s - 3
                        dve.wait_ge(pt_hi, c * NU + u + 1)
                        nc.vector.tensor_tensor(pair_part(ptl, u), banks[4 + u % 2][:].rearrange("p (f q) -> p f q", q=P),
                                                f32(pair_part(pth, u)), ALU.subtract).then_inc(pt_lo, 1)
                    if s % 8 == 0 and s > 0:
                        b = s // 8 - 1
                        dve.wait_ge(exped, 2 * (c * NU + s))
                        nc.vector.reciprocal(rsums[:, b], sums[:, b]).then_inc(inverted, 1)
                        dve.wait_ge(inverted, c * CB + b + 1)
                        if b == 1:
                            dve.wait_ge(divisor_done, c * CB + b)
                        for q in range(2):
                            part = rsums[:, b, q].rearrange("p (h o) -> p h o", o=1).to_broadcast([P, HEADS0, E0])
                            for k in range(2):
                                ins = nc.vector.tensor_scalar(spread[:, q, k * VC:(k + 1) * VC].rearrange("p (h e) -> p h e", e=E0), part,
                                                              float(VC ** -0.5), None, ALU.mult)
                        ins.then_inc(spread_done, 1)
                    if last_turn and 0 <= s - 11 < len(ffn.stacks):
                        i = s - 11
                        dst, _, w = ffn.stacks[i]
                        dve.wait_ge(b_hi_done, i + 1)
                        nc.vector.scalar_tensor_tensor(out=dst, in0=f32(b_hi[:, i % 2, 0:w]), scalar=consts.masks[:, 2:3], in1=b_raw[:, i % 2, 0:w],
                                                       op0=ALU.mult, op1=ALU.add).then_inc(b_stacked, 1)
                    if s == 14:
                        result_rows(c, 0)
                    if s == 10:
                        normalise(nc, dve, n.xn, rows(c + 1), n.stats, n.rstd, n.rstd_done, n.rows_done, c + 1)
                result_rows(c, 1)
                lo_rows(c + 1)
                for t in range(CT):
                    dve.wait_ge(wo_done, c * CT + t + 1)
                    nc.vector.tensor_tensor(n.xn[:, t, :], banks[4 + t][:], bo[:], ALU.add).then_inc(y_ready, 1)
                if not last_turn:
                    dve.wait_ge(y_ready, (c + 1) * CT + 1)
                    statistics(nc, dve, consts, n.raw_y, n.stats_y, n.y_raw_done, n.y_stats_done, lambda t: n.xn[:, t, :], c)
                    normalise(nc, dve, n.xn, lambda t: n.xn[:, t, :], n.stats_y, n.rstd_y, n.y_rstd_done, n.y_rows_done, c)

            with nc.vector.Fori(0, C - 1) as c:
                turn(c, False)
            turn(C - 1, True)

        @block.tensor
        def _(pe):
            turn_rows(nc, pe, n, consts, lambda k: banks[k], 0)

            def turn(c, last_turn):
                pe.wait_ge(n.lo_done, (c + 1) * KD)
                for m in range(M4):
                    for k in range(KD):
                        last = product(nc, banks[m][:], (wqk_h[:, k, m * P:(m + 1) * P], wqk_l[:, k, m * P:(m + 1) * P]),
                                       (n.xth[:, k, :], n.xtl[:, k, :]), k == 0, k == KD - 1)
                    last.then_inc(qk_done, 1)

                def values(tiles):
                    for t in tiles:
                        for k in range(KD):
                            last = product(nc, banks[5][:, t * VC:(t + 1) * VC], (n.xth[:, k, t * P:(t + 1) * P], n.xtl[:, k, t * P:(t + 1) * P]),
                                           (wv_h[:, k, :], wv_l[:, k, :]), k == 0, k == KD - 1)
                    if tiles[-1] == CT - 1:
                        last.then_inc(v_done, 1)

                pe.wait_ge(y_ready, c * CT + 1)
                values(range(CT // 2))

                def scores(u):
                    b, i, qt = u // 8, u // 2 % 4, u % 2
                    if u == 0:
                        pe.wait_ge(stacked, (c + 1) * M4)
                    if u >= 4:
                        pe.wait_ge(exped, 2 * (c * NU + u - 3))
                    r = slice(i * ROWS0, (i + 1) * ROWS0)
                    q0 = (b * 2 + qt) * P
                    for j in range(2):
                        last = nc.tensor.matmul(banks[u % 4][:, j * SEQ:(j + 1) * SEQ], stack[r, j, q0:q0 + P],
                                                stack[r, 2 + j, b * SEQ:(b + 1) * SEQ], start=True, stop=True)
                    last.then_inc(scored, 1)

                scores(0)
                for s in range(NU + 6):
                    if s + 1 < NU:
                        scores(s + 1)
                    if s == 2:
                        values(range(CT // 2, CT))
                    if 3 <= s < NU + 3:
                        u = s - 3
                        pe.wait_ge(exped, 2 * (c * NU + u + 1))
                        if u == 1:
                            pe.wait_ge(v_sum, c + 1)
                        if u >= 2:
                            pe.wait_ge(pt_lo, c * NU + u - 1)
                        for f in range(4):
                            last = nc.tensor.transpose(banks[4 + u % 2][:, f * P:(f + 1) * P], probs[:, u % 3, (f % 2 * 2 + f // 2) * P:][:, 0:P], consts.ident[:])
                        last.then_inc(pt_done, 1)
                    if s >= 6:
                        pair, j = (s - 6) // 2, s % 2
                        b, h = pair // 4, 4 * j + pair % 4
                        if s == 6:
                            pe.wait_ge(v_lo, c + 1)
                        if j == 0:
                            pe.wait_ge(pt_lo, c * NU + 2 * pair + 2)
                        for f in range(2):
                            for part in (pth, ptl):
                                last = nc.tensor.matmul(banks[6 + b][:, 0:SEQ], vm[:, 2 * b + f, h * P:(h + 1) * P], part[:, pair % 2, 2 * f + j, :],
                                                        start=pair % 4 == 0 and j == 0 and f == 0 and part is pth,
                                                        stop=pair % 4 == 3 and j == 1 and f == 1 and part is ptl)
                        last.then_inc(pv_done, 1)
                        if pair % 4 == 3 and j == 1:
                            pe.wait_ge(spread_done, c * CB + b + 1)
                            for q in range(2):
                                last = nc.tensor.transpose(banks[6 + b][:, SEQ + q * P:SEQ + (q + 1) * P], spread[:, q, :], consts.ident[:])
                            last.then_inc(divisor_done, 1)
                turn_rows(nc, pe, n, consts, lambda k: banks[k], c + 1)
                for t in range(CT):
                    if t % 2 == 0:
                        pe.wait_ge(ot_lo, c * CB + t // 2 + 1)
                    product(nc, banks[4 + t][:], (oth[:, t * P:(t + 1) * P], otl[:, t * P:(t + 1) * P]),
                            (wo_h[:], wo_l[:]), True, True).then_inc(wo_done, 1)

            with nc.tensor.Fori(0, C - 1) as c:
                turn(c, False)
            turn(C - 1, True)
    signals.clear()


class FfnWeights:

    def __init__(self, nc, ctx, a):
        def sb(name, shape, dt=F32):
            return ctx.enter_context(nc.sbuf_tensor(f"ffn_{name}", shape, dt))

        self.gate, self.up, self.down = sb("gate", [P, KD, IP], F32R), sb("up", [P, KD, IP], F32R), sb("down", [P, NI, D], F32R)
        self.scales = sb("scales", [P, 2, NI])
        self.b_gate, self.b_up, self.b_down = sb("b_gate", [P, IP], F32R), sb("b_up", [P, IP], F32R), sb("b_down", [P, D], F32R)
        gq, uq, dq = (w.rearrange("(k p) n -> p k n", p=P) for w in (a.gate_q, a.up_q, a.down_q))
        self.rows = [(self.gate, gq, KD // C, IP), (self.up, uq, KD // C, IP), (self.down, dq, -(-NI // C), D)]
        self.small = [(self.scales[:, 0, :], a.gate_scale),
                      (self.scales[:, 1, :], a.up_scale)]
        self.stacks = [(w[:, s:min(s + D, w.shape[1])], b[:, s:min(s + D, w.shape[1])], min(D, w.shape[1] - s)) for w, b in
                       ((self.b_gate, a.gate_B), (self.b_up, a.up_B), (self.b_down, a.down_B)) for s in range(0, w.shape[1], D)]


def part2(nc, a, X, n, ffn, arrivals, consts, banks):
    ctx, signals = ExitStack(), Signals(nc, "p2")
    with ctx:
        def sb(name, shape, dt=F32):
            return ctx.enter_context(nc.sbuf_tensor(f"p2_{name}", shape, dt))

        def sem(name):
            return signals.sem(name)

        RING = 4
        BG, BU, BL, BR, BY = banks[0], banks[1], banks[2], banks[3], banks[4:8]
        ag_h, ag_l = sb("ag_h", [P, KD, P], F32R), sb("ag_l", [P, KD, P], F32R)
        au_h, au_l = sb("au_h", [P, KD, P], F32R), sb("au_l", [P, KD, P], F32R)
        ad_h, ad_l = sb("ad_h", [P, NI, P], F32R), sb("ad_l", [P, NI, P], F32R)
        down_scale = sb("down_scale", [P, D])
        ad_raw = sb("ad_raw", [P, NI, P])
        scale_in, ad_in, a_hi, a_lo, scales_done = sem("scale_in"), sem("ad_in"), sem("a_hi"), sem("a_lo"), sem("scales_done")

        a_parts = ((arrivals.a_raw(0), ag_h, ag_l), (arrivals.a_raw(1), au_h, au_l), (ad_raw[:], ad_h, ad_l))
        r32, rh = sb("r32", [P, 2, CW]), sb("rh", [P, 2, CW], F32R)
        rstack = sb("rstack", [P, 3, CW], F32R)
        gu = sb("gu", [P, 2, 2, CW])
        hh, hl = sb("hh", [P, RING, CW], F32R), sb("hl", [P, RING, CW], F32R)
        (r_done, r_hi, r_stacked, main_done, rank_done, scaled, summed, silued, multiplied, h_hi, h_lo, down_done, rank_down_done,
         y_scaled, y_ready) = (sem(x) for x in "r_done r_hi r_stacked main_done rank_done scaled summed silued multiplied h_hi h_lo down_done rank_down_done y_scaled y_ready".split())

        block = ctx.enter_context(nc.Block())

        @block.sync
        def _(sp):
            sp.dma_start(ad_raw[:], a.down_A.rearrange("(k p) n -> p k n", p=P)).then_inc(ad_in, 16)
            sp.dma_start(down_scale[:], a.down_scale.rearrange("(o n) -> o n", o=1).to_broadcast([P, D])).then_inc(scale_in, 16)
            sp.wait_ge(a_lo, 2)
            sp.dma_start(arrivals.group_raw(), a.wq1.rearrange("(k p) n -> p k n", p=P)[:, :, 0:D]).then_inc(arrivals.q_in, 16)
            for c in range(C):
                tiles = slice(c * CT, (c + 1) * CT)
                sp.wait_ge(n.x_done, (C + c + 1) * CT + 1)
                if c >= 1:
                    sp.wait_ge(arrivals.parked, 16 * c)
                sp.dma_start(a.parked.rearrange("(t p) d -> p t d", p=P)[:, tiles, :], X[:, tiles, :]).then_inc(arrivals.parked, 16)

        @block.gpsimd
        def _(pool):
            def deviation_y(c):
                inverse_deviation(nc, pool, consts, n.stats_y, n.rstd_y, n.y_stats_done, n.y_var_eps, n.y_rstd_done, C + c)

            def add_result(c, tiles):
                residual(nc, pool, n, X, C - 1 if isinstance(c, int) and c < 0 else c, C + c, tiles)

            def turn(c, ahead):
                for s in range(NI):
                    pool.wait_ge(silued, c * NI + s + 1)
                    pool.wait_ge(summed, c * 2 * NI + 2 * s + 2)
                    nc.gpsimd.tensor_tensor(gu[:, s % 2, 0, :], gu[:, s % 2, 0, :], gu[:, s % 2, 1, :], ALU.mult).then_inc(multiplied, 1)
                    if s == 1:
                        deviation_y(c - 1)
                    if 2 <= s < 2 + CT:
                        add_result(c - 1, [s - 2])
                    if s == 4:
                        inverse_deviation(nc, pool, consts, n.stats, n.rstd, n.stats_done, n.var_eps, n.rstd_done, C + c + 1)

            turn(0, True)
            with nc.gpsimd.Fori(1, C - 1) as c:
                turn(c, True)
            turn(C - 1, False)
            deviation_y(C - 1)
            add_result(C - 1, range(CT))

        @block.scalar
        def _(act):
            def hi_rows(c):
                for k in range(KD):
                    act.wait_ge(n.turned, (C + c) * KD + k + 1)
                    nc.scalar.copy(n.xth[:, k, :], banks[k][:]).then_inc(n.hi_done, 1)

            def h_hi_of(c, s):
                act.wait_ge(multiplied, c * NI + s + 1)
                if s >= RING:
                    act.wait_ge(down_done, c * NI + s - RING + 1)
                nc.scalar.copy(hh[:, s % RING, :], gu[:, s % 2, 0, :]).then_inc(h_hi, 1)

            def r_hi_of(bank, slot):
                nc.scalar.activation(r32[:, slot, :], bank[:], ACT.Copy, scale=LR_SCALE)
                nc.scalar.activation(rh[:, slot, :], bank[:], ACT.Copy, scale=LR_SCALE).then_inc(r_hi, 1)

            act.wait_ge(arrivals.a_in, 32)
            for i, (raw, hi, _) in enumerate(a_parts):
                if i == 2:
                    act.wait_ge(ad_in, 16)
                nc.scalar.copy(hi[:], raw).then_inc(a_hi, 1)
            act.wait_ge(scales_done, 1)

            def turn(c, ahead):
                for m, bank in enumerate((BG, BU)):
                    act.wait_ge(r_done, c * 2 + m + 1)
                    r_hi_of(bank, m)
                for s in range(NI):
                    act.wait_ge(main_done, c * 2 * NI + 2 * s + 1)
                    if s >= 2:
                        act.wait_ge(h_lo, c * NI + s - 1)
                    nc.scalar.activation(gu[:, s % 2, 0, :], BG[:], ACT.Copy, scale=ffn.scales[:, 0, s:s + 1]).then_inc(scaled, 1)
                    if s >= 1:
                        h_hi_of(c, s - 1)
                    act.wait_ge(main_done, c * 2 * NI + 2 * s + 2)
                    nc.scalar.activation(gu[:, s % 2, 1, :], BU[:], ACT.Copy, scale=ffn.scales[:, 1, s:s + 1]).then_inc(scaled, 1)
                    act.wait_ge(summed, c * 2 * NI + 2 * s + 1)
                    nc.scalar.activation(gu[:, s % 2, 0, :], gu[:, s % 2, 0, :], ACT.Silu).then_inc(silued, 1)
                h_hi_of(c, NI - 1)
                act.wait_ge(down_done, (c + 1) * NI)
                r_hi_of(BR, 0)
                if ahead:
                    hi_rows(c + 1)

            with nc.scalar.Fori(0, C - 1) as c:
                turn(c, True)
            turn(C - 1, False)

        @block.vector
        def _(dve):
            def lo_rows(c):
                for k in range(KD):
                    dve.wait_ge(n.hi_done, (C + c) * KD + k + 1)
                    nc.vector.tensor_tensor(n.xtl[:, k, :], banks[k][:], f32(n.xth[:, k, :]), ALU.subtract).then_inc(n.lo_done, 1)

            def rows(c):
                first = 0 if isinstance(c, int) and c == C else c * CT
                return lambda t: X[:, first + t, :]

            def h_lo_of(c, s):
                dve.wait_ge(h_hi, c * NI + s + 1)
                nc.vector.tensor_tensor(hl[:, s % RING, :], gu[:, s % 2, 0, :], f32(hh[:, s % RING, :]), ALU.subtract).then_inc(h_lo, 1)

            def statistics_y(c):
                dve.wait_ge(y_ready, (c + 2) * CT)
                statistics(nc, dve, consts, n.raw_y, n.stats_y, n.y_raw_done, n.y_stats_done, lambda t: n.xn[:, t, :], C + c)

            def normalise_y(c):
                normalise(nc, dve, n.xn, lambda t: n.xn[:, t, :], n.stats_y, n.rstd_y, n.y_rstd_done, n.y_rows_done, C + c)

            def r_stack_of(c, m, slot):
                dve.wait_ge(r_hi, c * 3 + m + 1)
                nc.vector.scalar_tensor_tensor(out=rstack[:, m, :], in0=f32(rh[:, slot, :]), scalar=consts.masks[:, 3:4],
                                               in1=r32[:, slot, :], op0=ALU.mult, op1=ALU.add).then_inc(r_stacked, 1)

            dve.sem_inc(y_ready, CT)
            nc.vector.tensor_scalar(ffn.scales[:], ffn.scales[:], Q_STEP, None, ALU.mult).then_inc(scales_done, 1)
            for i, (raw, hi, lo) in enumerate(a_parts):
                dve.wait_ge(a_hi, i + 1)
                nc.vector.tensor_tensor(lo[:], raw, f32(hi[:]), ALU.subtract).then_inc(a_lo, 1)
            dve.wait_ge(scale_in, 16)
            nc.vector.tensor_scalar(down_scale[:], down_scale[:], Q_STEP, None, ALU.mult).then_inc(scales_done, 1)
            dve.wait_ge(scales_done, 2)

            def turn(c, ahead):
                r_stack_of(c, 0, 0)
                r_stack_of(c, 1, 1)
                for s in range(NI):
                    for m in range(2):
                        dve.wait_ge(scaled, c * 2 * NI + 2 * s + m + 1)
                        dve.wait_ge(rank_done, c * 2 * NI + 2 * s + m + 1)
                        nc.vector.tensor_tensor(gu[:, s % 2, m, :], gu[:, s % 2, m, :], BL[:], ALU.add).then_inc(summed, 1)
                        if m == 0 and s >= 1:
                            h_lo_of(c, s - 1)
                    if s == 0:
                        statistics_y(c - 1)
                    if s == 2:
                        normalise_y(c - 1)
                    if s == 3:
                        statistics(nc, dve, consts, n.raw, n.stats, n.raw_done, n.stats_done, rows(c + 1), C + c + 1)
                    if s == 7:
                        dve.wait_ge(n.x_done, (C + c) * CT + 1)
                        if not ahead:
                            dve.wait_ge(arrivals.parked, 16)
                        normalise(nc, dve, n.xn if ahead else X[:, 0:CT, :], rows(c + 1), n.stats, n.rstd, n.rstd_done, n.rows_done, C + c + 1)
                h_lo_of(c, NI - 1)
                r_stack_of(c, 2, 0)
                if ahead:
                    lo_rows(c + 1)
                dve.wait_ge(down_done, (c + 1) * NI)
                for t in range(CT + 1):
                    if t < CT:
                        nc.vector.tensor_tensor(n.xn[:, t, :], BY[t][:], down_scale[:], ALU.mult).then_inc(y_scaled, 1)
                    if t == 0:
                        continue
                    t -= 1
                    dve.wait_ge(y_scaled, c * CT + t + 1)
                    dve.wait_ge(rank_down_done, c * CT + t + 1)
                    nc.vector.tensor_tensor(n.xn[:, t, :], n.xn[:, t, :], banks[t][:], ALU.add).then_inc(y_ready, 1)

            turn(0, True)
            with nc.vector.Fori(1, C - 1) as c:
                turn(c, True)
            turn(C - 1, False)
            statistics_y(C - 1)
            normalise_y(C - 1)

        @block.tensor
        def _(pe):
            def main(bank, w, s):
                for k in range(KD):
                    nc.tensor.matmul(bank[:], w[:, k, s * P:(s + 1) * P], n.xth[:, k, :], start=k == 0, stop=False)
                    last = nc.tensor.matmul(bank[:], w[:, k, s * P:(s + 1) * P], n.xtl[:, k, :], start=False, stop=k == KD - 1)
                return last

            def turn(c, ahead):
                pe.wait_ge(n.lo_done, (C + c + 1) * KD)
                pe.wait_ge(a_lo, 2)
                for i, (bank, hi, lo) in enumerate(((BG, ag_h, ag_l), (BU, au_h, au_l))):
                    pe.wait_ge(y_ready, c * CT + i + 1)
                    for k in range(KD):
                        last = product(nc, bank[:], (hi[:, k, :], lo[:, k, :]), (n.xth[:, k, :], n.xtl[:, k, :]), k == 0, k == KD - 1)
                    last.then_inc(r_done, 1)
                for s in range(NI + 2):
                    if s < NI:
                        for m, (bank, w, b) in enumerate(((BG, ffn.gate, ffn.b_gate), (BU, ffn.up, ffn.b_up))):
                            if s == 0:
                                pe.wait_ge(r_stacked, c * 3 + m + 1)
                            else:
                                pe.wait_ge(scaled, c * 2 * NI + 2 * s + m - 1)
                            main(bank, w, s).then_inc(main_done, 1)
                            if s + m == 0:
                                pe.wait_ge(y_ready, (c + 1) * CT)
                            if s + m > 0:
                                pe.wait_ge(summed, c * 2 * NI + 2 * s + m)
                            nc.tensor.matmul(BL[:], b[:, s * P:(s + 1) * P], rstack[:, m, :], start=True, stop=True).then_inc(rank_done, 1)
                    if s >= 2:
                        j = s - 2
                        if j == 0:
                            pe.wait_ge(a_lo, 3)
                        pe.wait_ge(h_lo, c * NI + j + 1)
                        for t in range(CT):
                            tok = slice(t * P, (t + 1) * P)
                            nc.tensor.matmul(BY[t][:], hh[:, j % RING, tok], ffn.down[:, j, :], start=j == 0, stop=False)
                            nc.tensor.matmul(BY[t][:], hl[:, j % RING, tok], ffn.down[:, j, :], start=False, stop=j == NI - 1)
                        last = product(nc, BR[:], (ad_h[:, j, :], ad_l[:, j, :]), (hh[:, j % RING, :], hl[:, j % RING, :]), j == 0, j == NI - 1)
                        last.then_inc(down_done, 1)
                if ahead:
                    pe.wait_ge(r_stacked, c * 3 + 3)
                    turn_rows(nc, pe, n, consts, lambda k: banks[k], C + c + 1)
                pe.wait_ge(r_stacked, c * 3 + 3)
                for t in range(CT):
                    if ahead:
                        pe.wait_ge(n.lo_done, (C + c + 1) * KD + t + 1)
                    nc.tensor.matmul(banks[t][:], rstack[:, 2, t * P:(t + 1) * P], ffn.b_down[:], start=True, stop=True).then_inc(rank_down_done, 1)

            with nc.tensor.Fori(0, C - 1) as c:
                turn(c, True)
            turn(C - 1, False)
    signals.clear()


def part3(nc, a, X, arrivals, consts, banks):
    ctx, signals = ExitStack(), Signals(nc, "p3")
    with ctx:
        def sb(name, shape, dt=F32):
            return ctx.enter_context(nc.sbuf_tensor(f"p3_{name}", shape, dt))

        def sem(name):
            return signals.sem(name)

        GW = G * HD
        NM = 1 + G
        NJ = NM + 1
        NU = G * CB
        NW = 3 * CB
        NV = 2 * CB
        UW = 3 * P
        SECOND, FIRST = slice(0, 2 * P), slice(2 * P, 3 * P)

        x_back, q_raw_in, kv_raw_in = sem("x_back"), arrivals.q_in, sem("kv_raw_in")
        tables_in, o_raw_in, w_hi, qkv_split, o_split = (sem(x) for x in "tables_in o_raw_in w_hi qkv_split o_split".split())
        with ExitStack() as mid_ctx:
            def mid(name, shape, dt=F32):
                return mid_ctx.enter_context(nc.sbuf_tensor(f"p3_{name}", shape, dt))

            xth, xtl = mid("xth", [P, KD, T], F32R), mid("xtl", [P, KD, T], F32R)
            wq_h, wq_l = mid("wq_h", [P, KD, GW], F32R), mid("wq_l", [P, KD, GW], F32R)
            wk_h, wk_l = mid("wk_h", [P, KD, HD], F32R), mid("wk_l", [P, KD, HD], F32R)
            wv_h, wv_l = mid("wv_h", [P, KD, HD], F32R), mid("wv_l", [P, KD, HD], F32R)
            wo_h, wo_l = mid("wo_h", [P, G, D], F32R), mid("wo_l", [P, G, D], F32R)
            raw = arrivals.group_raw()
            raw_k, raw_v = mid("raw_k", [P, KD, HD]), mid("raw_v", [P, KD, HD])
            cos, sin = mid("cos", [P, SEQ]), mid("sin", [P, SEQ])
            window = mid("window", [P, 2 * P])

            wq_g, wk_g, wv_g = (w.rearrange("(k p) n -> p k n", p=P) for w in (a.wq1, a.wk1, a.wv1))
            wo_g = a.wo1.rearrange("(h p) n -> p h n", p=P)

            qkv_pieces = [(raw_k[:], wk_h[:], wk_l[:])]
            qkv_pieces += [tuple(w[:, :, h * HD:(h + 1) * HD] for w in (raw, wq_h, wq_l)) for h in range(G)]
            qkv_pieces += [(raw_v[:], wv_h[:], wv_l[:])]
            o_pieces = [tuple(w[:, h, :] for w in (raw, wo_h, wo_l)) for h in range(G)]
            NQ = len(qkv_pieces)
            NPIECE = NQ + G

            def hi_piece(act, g, i):
                if i == 0 or isinstance(g, int) and g == 0:
                    act.wait_ge(q_raw_in, g * 16 + 16)
                if i == 0 or isinstance(g, int) and g == 0 and i == NQ - 1:
                    act.wait_ge(kv_raw_in, g * 32 + 32)
                if i == NQ:
                    act.wait_ge(o_raw_in, g * 16 + 16)
                r, hi, lo = (qkv_pieces + o_pieces)[i]
                nc.scalar.copy(hi, r).then_inc(w_hi, 1)

            def lo_piece(pool, g, i):
                pool.wait_ge(w_hi, g * NPIECE + i + 1)
                r, hi, lo = (qkv_pieces + o_pieces)[i]
                nc.gpsimd.tensor_tensor(lo, r, f32(hi), ALU.subtract).then_inc(qkv_split if i < NQ else o_split, 1)

            def load_q(sp, g):
                sp.dma_start(raw, wq_g[:, :, bass.ds(g * GW, GW)]).then_inc(q_raw_in, 16)

            def load_kv(sp, g):
                sp.dma_start(raw_k[:], wk_g[:, :, bass.ds(g * HD, HD)]).then_inc(kv_raw_in, 16)
                sp.dma_start(raw_v[:], wv_g[:, :, bass.ds(g * HD, HD)]).then_inc(kv_raw_in, 16)

            n3 = Norm(nc, mid_ctx, signals, "n", xn=False, xt_width=0)

            def chunk_rows(c):
                return X[:, c * CT:(c + 1) * CT, :]

            def rows_of(c):
                return lambda t: X[:, c * CT + t, :]

            def x_bank(c, k):
                return banks[k] if c == 0 else banks[7]

            def turn_x(pe, c, k):
                if k == 0 and c >= 1:
                    pe.wait_ge(n3.rows_done, c * CT)
                if c > 1 or (c == 1 and k > 0):
                    pe.wait_ge(n3.lo_done, c * KD + k)
                for t in range(CT):
                    last = nc.tensor.transpose(x_bank(c, k)[:, t * P:(t + 1) * P], X[:, c * CT + t, k * P:(k + 1) * P], consts.ident[:])
                last.then_inc(n3.turned, 1)

            def hi_x(act, c, k):
                act.wait_ge(n3.turned, c * KD + k + 1)
                nc.scalar.copy(xth[:, k, c * CW:(c + 1) * CW], x_bank(c, k)[:]).then_inc(n3.hi_done, 1)

            def lo_x(dve, c, k):
                dve.wait_ge(n3.hi_done, c * KD + k + 1)
                cols = slice(c * CW, (c + 1) * CW)
                nc.vector.tensor_tensor(xtl[:, k, cols], x_bank(c, k)[:], f32(xth[:, k, cols]), ALU.subtract).then_inc(n3.lo_done, 1)

            def statistics_x(dve, c):
                statistics(nc, dve, consts, n3.raw, n3.stats, n3.raw_done, n3.stats_done, rows_of(c), c - 1)

            def normalise_x(dve, c):
                dve.wait_ge(arrivals.parked, 16 * (c + 1))
                normalise(nc, dve, chunk_rows(c), rows_of(c), n3.stats, n3.rstd, n3.rstd_done, n3.rows_done, c - 1)

            def ahead_of(g, c):
                return c + 1 if isinstance(g, int) and g == 0 and c + 1 < C else None

            def behind_of(g, c):
                return (c - 2) % C if isinstance(g, int) and (g == KV or (g == KV - 1 and c >= 2)) else None

            qh, ql = mid("qh", [P, G, CW], F32R), mid("ql", [P, G, CW], F32R)
            kh, kl = mid("kh", [P, CW], F32R), mid("kl", [P, CW], F32R)
            vh, vl = mid("vh", [P, CT, HD], F32R), mid("vl", [P, CT, HD], F32R)
            vt = mid("vt", [P, CW])
            swap, turn_cos = mid("swap", [P, 2, CW]), mid("turn_cos", [P, 2, CW])
            probs = mid("probs", [P, NU, UW])
            top, neg, sums, rsums = (mid(x, [P, NU, 2]) for x in ("top", "neg", "sums", "rsums"))
            pth, ptl = mid("pth", [P, 2, G * P], F32R), mid("ptl", [P, 2, G * P], F32R)
            oth, otl = mid("oth", [P, G, CW], F32R), mid("otl", [P, G, CW], F32R)
            (proj_done, vt_copied, v_turned, swapped, cosed, sined, rotated, rot_hi, rot_lo, v_hi, v_lo, scored, masked, negated, exped, inverted, normed,
             pt_done, pt_hi, pt_lo, pv_done, o_hi, o_lo, wo_done, y_ready) = (sem(x) for x in (
                 "proj_done vt_copied v_turned swapped cosed sined rotated rot_hi rot_lo v_hi v_lo scored masked negated exped inverted normed "
                 "pt_done pt_hi pt_lo pv_done o_hi o_lo wo_done y_ready").split())

            def wait(eng, sem, value):
                if not isinstance(value, int) or value > 0:
                    eng.wait_ge(sem, value)

            def groups(eng, item):
                item(0, 0, before=False)
                for c in range(1, C):
                    item(0, c)
                item(1, 0)
                with eng.Fori(1, KV - 1) as g:
                    for c in range(1, C):
                        item(g, c)
                    item(g + 1, 0)
                for c in range(1, C):
                    item(KV - 1, c)
                item(KV, 0, now=False)

            GATHERED = {0: 0, 2: 1, 3: 2, 5: 3}

            def bank_of_tile(m):
                return banks[m % 4]

            def bank_of_unit(u):
                return banks[(NJ + u) % 4]

            block = mid_ctx.enter_context(nc.Block())

            @block.sync
            def _(sp):
                load_kv(sp, 0)
                sp.dma_start(cos[:], a.cos).then_inc(tables_in, 16)
                sp.dma_start(sin[:], a.sin).then_inc(tables_in, 16)
                sp.dma_start(window[:], a.window).then_inc(tables_in, 16)
                parked = a.parked.rearrange("(t p) d -> p t d", p=P)

                def item(g, c, before=True, now=True):
                    if c == 0 and now:
                        sp.wait_ge(qkv_split, g * NQ + NQ)
                        sp.dma_start(raw, wo_g[:, bass.ds(g * G, G), :]).then_inc(o_raw_in, 16)
                    if c == 1 and not (isinstance(g, int) and g == KV - 1):
                        sp.wait_ge(o_split, g * G + G)
                        load_q(sp, g + 1)
                        load_kv(sp, g + 1)
                    behind = behind_of(g, c)
                    if behind is not None:
                        if behind == 0:
                            sp.wait_ge(o_split, KV * G)
                        else:
                            sp.wait_ge(n3.x_done, behind * CT)
                        sp.dma_start(raw, parked[:, behind * CT:(behind + 1) * CT, :]).then_inc(x_back, 16)

                groups(nc.sync, item)

            @block.gpsimd
            def _(pool):
                def deviation_x(c):
                    inverse_deviation(nc, pool, consts, n3.stats, n3.rstd, n3.stats_done, n3.var_eps, n3.rstd_done, c - 1)

                def deviation_y(c):
                    inverse_deviation(nc, pool, consts, n3.stats_y, n3.rstd_y, n3.y_stats_done, n3.y_var_eps, n3.y_rstd_done, c)

                def add_x(c):
                    pool.wait_ge(x_back, 16 * (c + 1))
                    for t in range(CT):
                        pool.wait_ge(n3.y_rows_done, c * CT + t + 1)
                        nc.gpsimd.tensor_tensor(X[:, c * CT + t, :], X[:, c * CT + t, :], raw[:, t, :], ALU.add).then_inc(n3.x_done, 1)

                pool.wait_ge(tables_in, 48)

                def item(g, c, before=True, now=True):
                    n = g * C + c
                    ahead, behind = ahead_of(g, c), behind_of(g, c)
                    if ahead is not None:
                        deviation_x(ahead)
                    if behind is not None:
                        deviation_y(behind)
                    for m in range(NM if now else 0):
                        par = (c + m) % 2
                        shape = [P, CB, SEQ]
                        wait(pool, swapped, n * NM + m + 1)
                        nc.gpsimd.tensor_tensor(swap[:, par, :].rearrange("p (b s) -> p b s", b=CB), swap[:, par, :].rearrange("p (b s) -> p b s", b=CB),
                                                sin[:].rearrange("p (o s) -> p o s", o=1).to_broadcast(shape), ALU.mult).then_inc(sined, 1)
                        wait(pool, cosed, n * NM + m + 1)
                        wait(pool, sined, n * NM + m + 1)
                        nc.gpsimd.tensor_tensor(turn_cos[:, par, :], turn_cos[:, par, :], swap[:, par, :], ALU.add).then_inc(rotated, 1)
                        if c == 1 and m >= 1:
                            lo_piece(pool, g, NQ + m - 1)
                    if c == C - 1 and not (isinstance(g, int) and g == KV - 1):
                        for i in range(NQ):
                            lo_piece(pool, g + 1, i)
                    if behind is not None:
                        add_x(behind)

                groups(nc.gpsimd, item)

            @block.scalar
            def _(act):
                half = HD // 2
                for i in range(1, 1 + G):
                    hi_piece(act, 0, i)
                for k in range(KD):
                    hi_x(act, 0, k)
                hi_piece(act, 0, 0)
                hi_piece(act, 0, NQ - 1)

                def item(g, c, before=True, now=True):
                    n = g * C + c
                    ahead = ahead_of(g, c)

                    def gather(x):
                        t = GATHERED[x]
                        wait(act, pv_done, (n - 1) * NW + x + 1)
                        nc.scalar.copy(oth[:, :, t * P:(t + 1) * P], banks[6 + t % 2][:].rearrange("p (h t) -> p h t", h=G)).then_inc(o_hi, 1)

                    for s in range(NW):
                        if now and s < NM:
                            par, bank = (c + s) % 2, bank_of_tile(s)
                            wait(act, proj_done, n * NJ + s + 1)
                            wait(act, rotated, n * NM + s - 1)
                            nc.scalar.copy(swap[0:half, par, :], bank[half:HD, :])
                            nc.scalar.copy(swap[half:HD, par, :], bank[0:half, :]).then_inc(swapped, 1)
                        if now and s == NM:
                            wait(act, proj_done, (n + 1) * NJ)
                            nc.scalar.copy(vt[:], bank_of_tile(NM)[:]).then_inc(vt_copied, 1)
                        if before:
                            wait(act, pt_done, (n - 1) * NW + s + 1)
                            if s >= 2:
                                wait(act, pv_done, (n - 1) * NW + s - 1)
                            nc.scalar.copy(pth[:, s % 2, :], banks[4 + s % 2][:]).then_inc(pt_hi, 1)
                            if c == 1 and s >= 1 and s <= G:
                                hi_piece(act, g, NQ + s - 1)
                        if now and 1 <= s < NM + 1:
                            par = (c + s - 1) % 2
                            wait(act, rotated, n * NM + s)
                            nc.scalar.copy(kh[:] if s == 1 else qh[:, s - 2, :], turn_cos[:, par, :]).then_inc(rot_hi, 1)
                        if before and s - 2 in GATHERED:
                            gather(s - 2)
                    for u in range(NU):
                        if before and u == 1:
                            gather(NW - 1)
                        if now and u == 3:
                            wait(act, v_turned, n + 1)
                            nc.scalar.copy(vh[:].rearrange("p t d -> p (t d)"), banks[6][:]).then_inc(v_hi, 1)
                        if not now:
                            continue
                        wait(act, negated, n * NU + u + 1)
                        for q, cols in enumerate((FIRST, SECOND)):
                            nc.scalar.activation(probs[:, u, cols], probs[:, u, cols], ACT.Exp, bias=neg[:, u, q:q + 1], scale=SCALE1,
                                                 accum_out=sums[:, u, q:q + 1]).then_inc(exped, 1)
                        if c == C - 1 and u < NQ and not (isinstance(g, int) and g == KV - 1):
                            hi_piece(act, g + 1, u)
                        if ahead is not None and 0 <= u - 2 < KD:
                            hi_x(act, ahead, u - 2)

                groups(nc.scalar, item)

            @block.vector
            def _(dve):
                def statistics_y(c):
                    statistics(nc, dve, consts, n3.raw_y, n3.stats_y, n3.y_raw_done, n3.y_stats_done, rows_of(c), c)

                def normalise_y(c):
                    normalise(nc, dve, chunk_rows(c), rows_of(c), n3.stats_y, n3.rstd_y, n3.y_rstd_done, n3.y_rows_done, c)

                def item(g, c, before=True, now=True):
                    n = g * C + c
                    ahead, behind = ahead_of(g, c), behind_of(g, c)
                    if ahead is not None:
                        statistics_x(dve, ahead)
                    if behind is not None:
                        dve.wait_ge(y_ready, (KV - 1) * C * CT + (behind + 1) * CT + 1)
                        statistics_y(behind)

                    def gather(x):
                        t = GATHERED[x]
                        wait(dve, o_hi, (n - 1) * NV + t + 1)
                        tok = slice(t * P, (t + 1) * P)
                        nc.vector.tensor_tensor(otl[:, :, tok], banks[6 + t % 2][:].rearrange("p (h t) -> p h t", h=G),
                                                f32(oth[:, :, tok]), ALU.subtract).then_inc(o_lo, 1)

                    def divide(u):
                        wait(dve, exped, 2 * (n * NU + u + 1))
                        nc.vector.reciprocal(rsums[:, u, :], sums[:, u, :]).then_inc(inverted, 1)
                        wait(dve, inverted, n * NU + u + 1)
                        for q, cols in enumerate((FIRST, SECOND)):
                            nc.vector.tensor_scalar(probs[:, u, cols], probs[:, u, cols], rsums[:, u, q:q + 1], None, ALU.mult).then_inc(normed, 1)

                    for s in range(NW):
                        if now and s < NM:
                            par = (c + s) % 2
                            wait(dve, swapped, n * NM + s + 1)
                            wait(dve, rot_lo, n * NM + s - 1)
                            nc.vector.tensor_tensor(turn_cos[:, par, :].rearrange("p (b s) -> p b s", b=CB),
                                                    bank_of_tile(s)[:].rearrange("p (b s) -> p b s", b=CB),
                                                    cos[:].rearrange("p (o s) -> p o s", o=1).to_broadcast([P, CB, SEQ]), ALU.mult).then_inc(cosed, 1)
                        if before:
                            wait(dve, pt_hi, (n - 1) * NW + s + 1)
                            nc.vector.tensor_tensor(ptl[:, s % 2, :], banks[4 + s % 2][:], f32(pth[:, s % 2, :]), ALU.subtract).then_inc(pt_lo, 1)
                        if now and 1 <= s < NM + 1:
                            par = (c + s - 1) % 2
                            wait(dve, rot_hi, n * NM + s)
                            hi, lo = (kh[:], kl[:]) if s == 1 else (qh[:, s - 2, :], ql[:, s - 2, :])
                            nc.vector.tensor_tensor(lo, turn_cos[:, par, :], f32(hi), ALU.subtract).then_inc(rot_lo, 1)
                        if before and s - 2 in GATHERED:
                            gather(s - 2)
                        if s == 2 and ahead is not None:
                            normalise_x(dve, ahead)
                        if s == 2 and behind is not None:
                            normalise_y(behind)
                    for u in range(NU + 1):
                        if now and u < NU:
                            wait(dve, scored, n * NU + u + 1)
                            dve.sem_inc(consts.passed[dve.engine], 1)
                            bank = bank_of_unit(u)
                            for q, (cols, win) in enumerate(((FIRST, window[:, P:2 * P]), (SECOND, window[:]))):
                                nc.vector.tensor_tensor_reduce(out=probs[:, u, cols], in0=bank[:, cols], in1=win, scale=1.0, scalar=4 * MASKED,
                                                               op0=ALU.add, op1=ALU.max, accum_out=top[:, u, q:q + 1]).then_inc(masked, 1)
                            wait(dve, masked, 2 * (n * NU + u + 1))
                            nc.vector.tensor_scalar(neg[:, u, :], top[:, u, :], -SCALE1, None, ALU.mult).then_inc(negated, 1)
                        if now and u >= 1:
                            divide(u - 1)
                        if before and u == 1:
                            gather(NW - 1)
                        if now and u == 2:
                            wait(dve, v_hi, n + 1)
                            nc.vector.tensor_tensor(vl[:].rearrange("p t d -> p (t d)"), banks[6][:], f32(vh[:].rearrange("p t d -> p (t d)")),
                                                    ALU.subtract).then_inc(v_lo, 1)
                        if before and u % 2 == 0 and u >= 2:
                            t = u // 2 - 1
                            wait(dve, wo_done, (n - 1) * CT + t + 1)
                            place = X[:, (c - 1) % C * CT + t, :]
                            if isinstance(n, int) and n <= C:
                                nc.vector.tensor_copy(place, banks[4 + t % 2][:]).then_inc(y_ready, 1)
                            else:
                                nc.vector.tensor_tensor(place, place, banks[4 + t % 2][:], ALU.add).then_inc(y_ready, 1)
                        if ahead is not None and 0 <= u - 3 < KD:
                            lo_x(dve, ahead, u - 3)

                dve.sem_inc(y_ready, 1)
                first_pieces = [*range(1, 1 + G), 0, NQ - 1]
                for count, i in enumerate(first_pieces):
                    if count == G:
                        for k in range(KD):
                            lo_x(dve, 0, k)
                    dve.wait_ge(w_hi, count + 1)
                    r, hi, lo = qkv_pieces[i]
                    nc.vector.tensor_tensor(lo, r, f32(hi), ALU.subtract).then_inc(qkv_split, 1)
                dve.wait_ge(tables_in, 48)
                groups(nc.vector, item)

            @block.tensor
            def _(pe):
                for k in range(KD):
                    turn_x(pe, 0, k)

                def item(g, c, before=True, now=True):
                    n = g * C + c
                    ahead = ahead_of(g, c)
                    if now and isinstance(g, int) and g == 0:
                        pe.wait_ge(n3.lo_done, (c + 1) * KD)
                    cols = slice(c * CW, (c + 1) * CW)

                    def tile(m):
                        if c == 0:
                            wait(pe, qkv_split, NQ if isinstance(g, int) and g == 0 else g * NQ + m + 1)
                        if m < 4:
                            wait(pe, masked, 2 * ((n - 1) * NU + (m - NJ) % 4 + 5) if before else 0)
                        else:
                            wait(pe, cosed, n * NM + m - 3)
                        for k in range(KD):
                            if m == 0:
                                w = (wk_h[:, k, :], wk_l[:, k, :])
                            elif m == NM:
                                w = (wv_h[:, k, :], wv_l[:, k, :])
                            else:
                                w = tuple(x[:, k, (m - 1) * HD:m * HD] for x in (wq_h, wq_l))
                            last = product(nc, bank_of_tile(m)[:], w, (xth[:, k, cols], xtl[:, k, cols]), k == 0, k == KD - 1)
                        last.then_inc(proj_done, 1)

                    def turn_values():
                        wait(pe, vt_copied, n + 1)
                        if before:
                            wait(pe, o_lo, (n - 1) * NV + 3)
                        for t in range(CT):
                            last = nc.tensor.transpose(banks[6][:, t * HD:(t + 1) * HD], vt[:, t * P:(t + 1) * P], consts.ident[:])
                        last.then_inc(v_turned, 1)

                    def turn(w):
                        b, part = w // 3, (2, 0, 1)[w % 3]
                        if w % 3 == 0:
                            wait(pe, normed, 2 * ((n - 1) * NU + (b + 1) * G))
                        if w < 2:
                            wait(pe, y_ready, (n - 1) * CT + 1)
                        else:
                            wait(pe, pt_lo, (n - 1) * NW + w - 1)
                        for h in range(G):
                            last = nc.tensor.transpose(banks[4 + w % 2][:, h * P:(h + 1) * P], probs[:, b * G + h, part * P:(part + 1) * P], consts.ident[:])
                        last.then_inc(pt_done, 1)

                    def weigh(x):
                        b, part = x // 3, x % 3
                        q, kt = (0, 0) if part == 0 else (1, part - 1)
                        if part < 2 and b == 1:
                            wait(pe, o_lo, (n - 1) * NV + q + 1)
                        if x == 0:
                            wait(pe, v_lo, n)
                        wait(pe, pt_lo, (n - 1) * NW + x + 1)
                        product(nc, banks[6 + q][:], (vh[:, 2 * b + kt, :], vl[:, 2 * b + kt, :]), (pth[:, x % 2, :], ptl[:, x % 2, :]),
                                part < 2, part != 1).then_inc(pv_done, 1)

                    for s in range(NW):
                        if now:
                            tile(s)
                        if before:
                            turn(s)
                        if before and s >= 1:
                            weigh(s - 1)
                    for u in range(NU):
                        if now:
                            b, h = u // G, u % G
                            if b == 0:
                                wait(pe, rot_lo, n * NM + h + 2)
                            if u < 3:
                                wait(pe, cosed, n * NM + u + 3)
                            elif u == 3:
                                wait(pe, vt_copied, n + 1)
                            else:
                                wait(pe, masked, 2 * (n * NU + u - 3))
                            bank, s0 = bank_of_unit(u), b * SEQ
                            product(nc, bank[:, FIRST], (qh[:, h, s0:s0 + P], ql[:, h, s0:s0 + P]), (kh[:, s0:s0 + P], kl[:, s0:s0 + P]), True, True)
                            product(nc, bank[:, SECOND], (qh[:, h, s0 + P:s0 + SEQ], ql[:, h, s0 + P:s0 + SEQ]),
                                    (kh[:, s0:s0 + SEQ], kl[:, s0:s0 + SEQ]), True, True).then_inc(scored, 1)
                        if before:
                            t = u // 2
                            tok = slice(t * P, (t + 1) * P)
                            if u % 2 == 0:
                                wait(pe, o_lo, (n - 1) * NV + t + 1)
                                if t == 0 and c == 1:
                                    wait(pe, o_split, g * G + G)
                                if t >= 2:
                                    wait(pe, y_ready, (n - 1) * CT + t)
                            for h in (0, 1) if u % 2 == 0 else (2, 3):
                                last = product(nc, banks[4 + t % 2][:], (oth[:, h, tok], otl[:, h, tok]), (wo_h[:, h, :], wo_l[:, h, :]), h == 0, h == G - 1)
                            if u % 2 == 1:
                                last.then_inc(wo_done, 1)
                            if u == 0:
                                weigh(NW - 1)
                        if now and u == 1:
                            turn_values()
                        if ahead is not None and 0 <= u - 2 < KD:
                            if before and u == 2:
                                wait(pe, o_lo, n * NV)
                            turn_x(pe, ahead, u - 2)

                groups(nc.tensor, item)

    signals.clear()


def part4(nc, a, X, out, arrivals, consts, banks):
    ctx, signals = ExitStack(), Signals(nc, "p4")
    with ctx:
        def sb(name, shape, dt=F32):
            return ctx.enter_context(nc.sbuf_tensor(f"p4_{name}", shape, dt))

        sem = signals.sem
        ER_ALL = NE * ER
        CATW = ER_ALL + NH
        BCAT, BDENSE, BGATE, BLORA = banks[4:6], banks[6], banks[7], banks[4:7]
        w_in, w_hi, w_lo, rows_in, ones_set = [sem(f"w_in{i}") for i in range(3)], sem("w_hi"), sem("w_lo"), sem("rows_in"), sem("ones_set")
        cat_h, cat_l = sb("cat_h", [P, KD, CATW], F32R), sb("cat_l", [P, KD, CATW], F32R)
        dense_h, dense_l = sb("dense_h", [P, KD, D], F32R), sb("dense_l", [P, KD, D], F32R)
        lb_h, lb_l = sb("lb_h", [ER_ALL, D], F32R), sb("lb_l", [ER_ALL, D], F32R)
        gw2 = sb("gw2", [P, CT * NE])
        gb1, gamma, beta, gb2, experts = sb("gb1", [P, NH]), sb("gamma", [P, NH]), sb("beta", [P, NH]), sb("gb2", [P, NE]), sb("experts", [P, NE])
        ones = sb("ones", [P, P])
        pre = [Norm(nc, ctx, signals, f"n{i}", xt_width=0) for i in range(2)]
        xth, xtl = sb("xth", [P, KD, T], F32R), sb("xtl", [P, KD, T], F32R)
        y = sb("y", [P, NT, D])
        low = sb("low", [P, NT, ER_ALL])
        hidden = sb("hidden", [P, 2, CT, NH])
        h_raw, h_stats, h_rstd = sb("h_raw", [P, CT, 6]), sb("h_stats", [P, CT, 2]), sb("h_rstd", [P, CT])
        hidden_t = sb("hidden_t", [P, P])
        gates, top, where, where_f = sb("gates", [P, CT, NE]), sb("top", [P, CT, 8]), sb("where", [P, CT, 8], U32), sb("where_f", [P, CT, 8])
        second, share = sb("second", [P, CT]), sb("share", [P, NT, 2])
        chosen = sb("chosen", [P, NT, 2, NE])
        allowed, part, weight = sb("allowed", [P, 2, NE]), sb("part", [P, 2, NT, NE]), sb("weight", [P, NT, NE])
        scaled = sb("scaled", [P, 3, ER_ALL])
        x_last = sb("x_last", [P, CT, D])
        n3, x_last_in = Norm(nc, ctx, signals, "n3", xn=False, xt_width=0), sem("x_last_in")
        last_tiles = slice(NT - CT, NT)
        shift = sb("shift", [P, CT])
        sth, stl = sb("sth", [P, 3, P], F32R), sb("stl", [P, 3, P], F32R)

        cat_raw, dense_raw, lb_raw = sb("cat_raw", [P, KD, CATW]), arrivals.group_raw(), sb("lb_raw", [ER_ALL, D])
        weights = ((cat_raw[:], cat_h, cat_l), (dense_raw, dense_h, dense_l), (lb_raw[:], lb_h, lb_l))

        (cat_done, dense_done, low_read, hidden_sum, h_raw_done, h_stats_done, h_var, h_rstd_done, h_ready, ht_done, ht_copied, gates_done,
         gap_ready, gap_exp, is_chosen, counted, weighted, st_scaled, st_turned, st_hi, st_lo, lora_done, y_copied, y_summed, shift_half, shift_done, tail_rows, tail_done, chain_sem, stored) = (
             sem(x) for x in "cat_done dense_done low_read hidden_sum h_raw_done h_stats_done h_var h_rstd_done h_ready ht_done ht_copied gates_done "
             "gap_ready gap_exp is_chosen counted weighted st_scaled st_turned st_hi st_lo lora_done y_copied y_summed shift_half shift_done tail_rows tail_done chain stored".split())
        ny = pre[0]
        TAIL = 2
        AHEAD = 3

        block = ctx.enter_context(nc.Block())

        @block.sync
        def _(sp):
            sp.dma_start(cat_raw[:, :, 0:ER_ALL], a.lora_A.rearrange("(k p) n -> p k n", p=P)).then_inc(w_in[0], 16)
            sp.dma_start(cat_raw[:, :, ER_ALL:CATW], a.gw1.rearrange("(k p) n -> p k n", p=P)).then_inc(w_in[0], 16)
            sp.dma_start(dense_raw, a.dense.rearrange("(k p) n -> p k n", p=P)).then_inc(w_in[1], 16)
            sp.dma_start(x_last[:], a.parked.rearrange("(t p) d -> p t d", p=P)[:, last_tiles, :]).then_inc(x_last_in, 16)
            sp.dma_start(lb_raw[:], a.lora_B).then_inc(w_in[2], 16)
            sp.dma_start(gw2[:], a.gw2).then_inc(rows_in, 16)
            sp.dma_start(experts[:], a.experts).then_inc(rows_in, 16)
            for dst, src, w in ((gb1, a.gb1, NH), (gamma, a.ln_gamma, NH), (beta, a.ln_beta, NH), (gb2, a.gb2, NE)):
                sp.dma_start(dst[:], src.rearrange("(o n) -> o n", o=1).to_broadcast([P, w])).then_inc(rows_in, 16)
            ov = out.rearrange("(t p) d -> p t d", p=P)
            for first, stop in [(c * CT, (c + 1) * CT) for c in range(C - 1)] + [(t, t + 1) for t in range(NT - CT, NT)]:
                if stop > NT - TAIL:
                    sp.wait_ge(tail_done, stop - (NT - TAIL))
                else:
                    sp.wait_ge(ny.x_done, stop)
                sp.dma_start(ov[:, first:stop, :], X[:, first:stop, :]).then_inc(stored, 16)
            sp.wait_ge(stored, 16 * (C - 1 + CT))

        @block.gpsimd
        def _(pool):
            def norm_x(c):
                n = pre[c % 2]
                inverse_deviation(nc, pool, consts, n.stats, n.rstd, n.stats_done, n.var_eps, n.rstd_done, c // 2)

            nc.gpsimd.memset(ones[:], 1.0).then_inc(ones_set, 1)
            norm_x(0)
            for c in range(C):
                if c + 1 < C:
                    norm_x(c + 1)
                if c == 0:
                    inverse_deviation(nc, pool, consts, n3.stats_y, n3.rstd_y, n3.y_stats_done, n3.y_var_eps, n3.y_rstd_done, 0)
                    pool.wait_ge(x_last_in, 16)
                    for t in range(CT):
                        rows = X[:, NT - CT + t, :]
                        pool.wait_ge(n3.y_rows_done, t + 1)
                        nc.gpsimd.tensor_tensor(rows, rows, x_last[:, t, :], ALU.add).then_inc(n3.x_done, 1)
                inverse_deviation(nc, pool, consts, h_stats, h_rstd, h_stats_done, h_var, h_rstd_done, c)
            for c in range(C):
                inverse_deviation(nc, pool, consts, ny.stats_y, ny.rstd_y, ny.y_stats_done, ny.y_var_eps, ny.y_rstd_done, c)
                if c >= 1:
                    pool.wait_ge(ny.y_rows_done, c * CT)
                nc.gpsimd.tensor_scalar(shift[:], ny.stats_y[:, :, 0], -1.0, None, ALU.mult).then_inc(shift_half, 1)
                pool.wait_ge(ny.y_rstd_done, c + 1)
                pool.wait_ge(shift_half, c + 1)
                nc.gpsimd.tensor_tensor(shift[:], shift[:], ny.rstd_y[:], ALU.mult).then_inc(shift_done, 1)
                for t in range(CT if c < C - 1 else CT - TAIL):
                    pool.wait_ge(ny.y_rows_done, c * CT + t + 1)
                    nc.gpsimd.tensor_tensor(X[:, c * CT + t, :], X[:, c * CT + t, :], y[:, c * CT + t, :], ALU.add).then_inc(ny.x_done, 1)

        @block.scalar
        def _(act):
            def hi_rows(c):
                n = pre[c % 2]
                for k in range(KD):
                    act.wait_ge(n.turned, c // 2 * KD + k + 1)
                    nc.scalar.copy(xth[:, k, c * CW:(c + 1) * CW], banks[k][:]).then_inc(n.hi_done, 1)

            def gate(c):
                act.wait_ge(ht_done, c + 1)
                nc.scalar.copy(hidden_t[:], BGATE[:, 0:P]).then_inc(ht_copied, 1)
                act.wait_ge(gap_ready, c + 1)
                nc.scalar.activation(second[:], second[:], ACT.Exp).then_inc(gap_exp, 1)

            for i, (raw, hi, lo) in enumerate(weights):
                act.wait_ge(w_in[i], (2, 1, 1)[i] * 16)
                nc.scalar.copy(hi[:], raw).then_inc(w_hi, 1)
            hi_rows(0)
            for c in range(C):
                for t in range(c * CT, (c + 1) * CT):
                    if c + 1 < C and t % CT == AHEAD:
                        hi_rows(c + 1)
                    act.wait_ge(cat_done, t + 1)
                    nc.scalar.copy(low[:, t, :], BCAT[t % 2][:, 0:ER_ALL]).then_inc(low_read, 1)
                    act.wait_ge(dense_done, t + 1)
                    nc.scalar.copy(y[:, t, :], BDENSE[:]).then_inc(y_copied, 1)
                    if c >= 1 and t % CT == 1:
                        gate(c - 1)
            def normalise_y(c):
                act.wait_ge(shift_done, c + 1)
                for t in range(CT if c < C - 1 else CT - TAIL):
                    rows = y[:, c * CT + t, :]
                    nc.scalar.activation(rows, rows, ACT.Identity, bias=shift[:, t:t + 1], scale=ny.rstd_y[:, t:t + 1]).then_inc(ny.y_rows_done, 1)

            gate(C - 1)
            for t in range(NT):
                act.wait_ge(st_turned, t + 1)
                if t >= 3:
                    act.wait_ge(lora_done, t - 2)
                nc.scalar.copy(sth[:, t % 3, :], banks[t % 4][:, 0:P]).then_inc(st_hi, 1)
                if t >= 2 * CT + 1 and t % CT == 1:
                    normalise_y(t // CT - 2)
            for c in range(C - 2, C):
                normalise_y(c)

        @block.vector
        def _(dve):
            chain = Count(chain_sem)

            def rows(c):
                return lambda t: X[:, c * CT + t, :]

            def norm_rows(c):
                n = pre[c % 2]
                if c >= 2:
                    dve.wait_ge(n.turned, KD)
                if c == C - 1:
                    dve.wait_ge(n3.x_done, CT)
                statistics(nc, dve, consts, n.raw, n.stats, n.raw_done, n.stats_done, rows(c), c // 2)
                normalise(nc, dve, n.xn, rows(c), n.stats, n.rstd, n.rstd_done, n.rows_done, c // 2)

            def lo_rows(c):
                n, cols = pre[c % 2], slice(c * CW, (c + 1) * CW)
                for k in range(KD):
                    dve.wait_ge(n.hi_done, c // 2 * KD + k + 1)
                    nc.vector.tensor_tensor(xtl[:, k, cols], banks[k][:], f32(xth[:, k, cols]), ALU.subtract).then_inc(n.lo_done, 1)

            def over_tiles(row, w):
                return row[:].rearrange("p (o n) -> p o n", o=1).to_broadcast([P, CT, w])

            def hidden_rows(c):
                dve.wait_ge(hidden_sum, (c + 1) * CT)
                if c >= 1:
                    dve.wait_ge(h_rstd_done, c)
                statistics(nc, dve, consts, h_raw, h_stats, h_raw_done, h_stats_done, lambda t: hidden[:, c % 2, t, :], c)
                dve.wait_ge(h_rstd_done, c + 1)
                for t in range(CT):
                    ins = nc.vector.tensor_scalar(hidden[:, c % 2, t, :], hidden[:, c % 2, t, :], h_stats[:, t, 0:1], h_rstd[:, t:t + 1], ALU.subtract, ALU.mult)
                    chain.mark(ins)
                dve.wait_ge(chain.sem, chain.n)
                chain.link(dve, nc.vector.tensor_tensor(hidden[:, c % 2], hidden[:, c % 2], over_tiles(gamma, NH), ALU.mult))
                chain.link(dve, nc.vector.tensor_tensor(hidden[:, c % 2], hidden[:, c % 2], over_tiles(beta, NH), ALU.add))
                nc.vector.tensor_scalar(hidden[:, c % 2], hidden[:, c % 2], 0.0, None, ALU.max).then_inc(h_ready, 1)

            def choose(c):
                tiles = slice(c * CT, (c + 1) * CT)
                dve.wait_ge(gates_done, c + 1)
                chain.link(dve, nc.vector.tensor_tensor(gates[:], BGATE[:, P:P + CT * NE].rearrange("p (t e) -> p t e", e=NE),
                                                        over_tiles(gb2, NE), ALU.add))
                for t in range(CT):
                    chain.mark(nc.vector.max(top[:, t, :], gates[:, t, :]))
                dve.wait_ge(chain.sem, chain.n)
                for t in range(CT):
                    chain.mark(nc.vector.max_index(where[:, t, :], top[:, t, :], gates[:, t, :]))
                nc.vector.tensor_tensor(second[:], top[:, :, 1], top[:, :, 0], ALU.subtract).then_inc(gap_ready, 1)
                dve.wait_ge(chain.sem, chain.n)
                chain.link(dve, nc.vector.tensor_copy(where_f[:], where[:]))
                for k in range(2):
                    nc.vector.tensor_tensor(chosen[:, tiles, k, :], over_tiles(experts, NE), where_f[:, :, k:k + 1].to_broadcast([P, CT, NE]),
                                            ALU.is_equal).then_inc(is_chosen, 1)
                dve.wait_ge(gap_exp, c + 1)
                chain.link(dve, nc.vector.tensor_scalar(share[:, tiles, 1], second[:], 1.0, None, ALU.add))
                chain.link(dve, nc.vector.reciprocal(share[:, tiles, 0], share[:, tiles, 1]))
                chain.link(dve, nc.vector.tensor_tensor(share[:, tiles, 1], second[:], share[:, tiles, 0], ALU.mult))

            norm_rows(0)
            for i, (raw, hi, lo) in enumerate(weights):
                dve.wait_ge(w_hi, i + 1)
                nc.vector.tensor_tensor(lo[:], raw, f32(hi[:]), ALU.subtract).then_inc(w_lo, 1)
            lo_rows(0)
            dve.wait_ge(rows_in, 96)
            for c in range(C):
                if c + 1 < C:
                    norm_rows(c + 1)
                for t in range(c * CT, (c + 1) * CT):
                    if c + 1 < C and t % CT == AHEAD:
                        lo_rows(c + 1)
                    dve.wait_ge(low_read, t + 1)
                    if t % CT == 0 and c >= 2:
                        dve.wait_ge(ht_done, c - 1)
                    nc.vector.tensor_tensor(hidden[:, c % 2, t % CT, :], BCAT[t % 2][:, ER_ALL:CATW], gb1[:], ALU.add).then_inc(hidden_sum, 1)
                    if c >= 1 and t % CT == 1:
                        choose(c - 1)
                    if t == 0:
                        statistics(nc, dve, consts, n3.raw_y, n3.stats_y, n3.y_raw_done, n3.y_stats_done, rows(C - 1), 0)
                    if t == 1:
                        normalise(nc, dve, X[:, last_tiles, :], rows(C - 1), n3.stats_y, n3.rstd_y, n3.y_rstd_done, n3.y_rows_done, 0)
                hidden_rows(c)
            choose(C - 1)
            dve.wait_ge(counted, 1)
            chain.link(dve, nc.vector.tensor_scalar(allowed[:], BGATE[:, 2 * P:2 * P + 2 * NE].rearrange("p (k e) -> p k e", e=NE),
                                                    float(CAPACITY), None, ALU.is_le))
            for k in range(2):
                chain.mark(nc.vector.scalar_tensor_tensor(out=part[:, k, :, :], in0=chosen[:, :, k, :], scalar=1.0 / ER,
                                                          in1=share[:, :, k:k + 1].to_broadcast([P, NT, NE]), op0=ALU.mult, op1=ALU.mult))
            dve.wait_ge(chain.sem, chain.n)
            for k in range(2):
                chain.mark(nc.vector.tensor_tensor(part[:, k, :, :], part[:, k, :, :],
                                                   allowed[:, k:k + 1, :].to_broadcast([P, NT, NE]), ALU.mult))
            dve.wait_ge(chain.sem, chain.n)
            nc.vector.tensor_tensor(weight[:], part[:, 0, :, :], part[:, 1, :, :], ALU.add).then_inc(weighted, 1)
            dve.wait_ge(weighted, 1)
            for s in range(NT + 4):
                if s < NT:
                    if s >= 3:
                        dve.wait_ge(st_turned, s - 2)
                    nc.vector.tensor_tensor(scaled[:, s % 3, :].rearrange("p (e r) -> p e r", r=ER), low[:, s, :].rearrange("p (e r) -> p e r", r=ER),
                                            weight[:, s, :].rearrange("p (e o) -> p e o", o=1).to_broadcast([P, NE, ER]), ALU.mult).then_inc(st_scaled, 1)
                if 1 <= s < NT + 1:
                    t = s - 1
                    dve.wait_ge(st_hi, t + 1)
                    nc.vector.tensor_tensor(stl[:, t % 3, :], banks[t % 4][:, 0:P], f32(sth[:, t % 3, :]), ALU.subtract).then_inc(st_lo, 1)
                if 3 <= s < NT + 3:
                    t = s - 3
                    dve.wait_ge(lora_done, t + 1)
                    dve.wait_ge(y_copied, t + 1)
                    nc.vector.tensor_tensor(y[:, t, :], y[:, t, :], BLORA[t % 3][:], ALU.add).then_inc(y_summed, 1)
                if s >= 4:
                    t = s - 4
                    c = t // CT
                    dve.wait_ge(y_summed, t + 1)
                    if c >= 1 and t % CT == 0:
                        dve.wait_ge(ny.y_stats_done, c * CT)
                    nc.vector.bn_stats(ny.raw_y[:, t % CT, :], y[:, t, :]).then_inc(ny.y_raw_done, 1)
                    if t % CT == CT - 1:
                        if c >= 1:
                            dve.wait_ge(shift_done, c)
                        for j in range(CT):
                            dve.wait_ge(ny.y_raw_done, c * CT + j + 1)
                            nc.vector.bn_aggr(ny.stats_y[:, j, :], ny.raw_y[:, j, :]).then_inc(ny.y_stats_done, 1)
            dve.wait_ge(ny.y_rstd_done, C)
            for t in range(CT - TAIL, CT):
                rows = y[:, NT - CT + t, :]
                nc.vector.tensor_scalar(rows, rows, ny.stats_y[:, t, 0:1], ny.rstd_y[:, t:t + 1], ALU.subtract, ALU.mult).then_inc(tail_rows, 1)
            for i in range(TAIL):
                t = NT - TAIL + i
                dve.wait_ge(tail_rows, i + 1)
                nc.vector.tensor_tensor(X[:, t, :], X[:, t, :], y[:, t, :], ALU.add).then_inc(tail_done, 1)

        @block.tensor
        def _(pe):
            def turn(c):
                if c >= 1:
                    pe.wait_ge(pre[(c - 1) % 2].lo_done, ((c - 1) // 2 + 1) * KD)
                turn_rows(nc, pe, pre[c % 2], consts, lambda k: banks[k], c // 2)

            def gate(c):
                pe.wait_ge(h_ready, c + 1)
                nc.tensor.transpose(BGATE[:, 0:P], hidden[:, c % 2].rearrange("p t n -> p (t n)"), consts.ident[:]).then_inc(ht_done, 1)
                pe.wait_ge(ht_copied, c + 1)
                nc.tensor.matmul(BGATE[:, P:P + CT * NE], hidden_t[:], gw2[:], start=True, stop=True).then_inc(gates_done, 1)

            turn(0)
            pe.wait_ge(w_lo, 3)
            pe.wait_ge(rows_in, 96)
            pe.wait_ge(ones_set, 1)
            for c in range(C):
                n = pre[c % 2]
                pe.wait_ge(n.lo_done, (c // 2 + 1) * KD)
                for t in range(c * CT, (c + 1) * CT):
                    if c + 1 < C and t % CT == AHEAD:
                        turn(c + 1)
                    tok = slice(t * P, (t + 1) * P)
                    if t >= 2:
                        pe.wait_ge(hidden_sum, t - 1)
                    for k in range(KD):
                        last = product(nc, BCAT[t % 2][:, 0:CATW], (xth[:, k, tok], xtl[:, k, tok]), (cat_h[:, k, :], cat_l[:, k, :]), k == 0, k == KD - 1)
                    last.then_inc(cat_done, 1)
                    if t >= 1:
                        pe.wait_ge(y_copied, t)
                    for k in range(KD):
                        last = product(nc, BDENSE[:], (xth[:, k, tok], xtl[:, k, tok]), (dense_h[:, k, :], dense_l[:, k, :]), k == 0, k == KD - 1)
                    last.then_inc(dense_done, 1)
                    if c >= 1 and t % CT == 1:
                        gate(c - 1)
            gate(C - 1)
            pe.wait_ge(is_chosen, 2 * C)
            for t in range(NT):
                last = nc.tensor.matmul(BGATE[:, 2 * P:2 * P + 2 * NE], ones[:], chosen[:, t, :, :].rearrange("p k e -> p (k e)"),
                                        start=t == 0, stop=t == NT - 1)
            last.then_inc(counted, 1)
            for s in range(NT + 2):
                if s < NT:
                    pe.wait_ge(st_scaled, s + 1)
                    if s >= 4:
                        pe.wait_ge(st_lo, s - 3)
                    nc.tensor.transpose(banks[s % 4][:, 0:P], scaled[:, s % 3, :], consts.ident[:]).then_inc(st_turned, 1)
                if s >= 2:
                    t = s - 2
                    pe.wait_ge(st_lo, t + 1)
                    if t >= 3:
                        pe.wait_ge(y_summed, t - 2)
                    product(nc, BLORA[t % 3][:], (sth[:, t % 3, :], stl[:, t % 3, :]), (lb_h[:], lb_l[:]), True, True).then_inc(lora_done, 1)
    signals.clear()


def program(nc, a, out):
    ctx = ExitStack()
    with ctx:
        banks = [ctx.enter_context(nc.psum_tensor(f"bank{i}", [P, 512], F32)) for i in range(8)]
        consts = Constants(nc, ctx, a)
        X = ctx.enter_context(nc.sbuf_tensor("X", [P, NT, D], F32))
        shared, early = Signals(nc, "all"), Signals(nc, "p12")
        arrivals = Arrivals(nc, ctx, shared)
        with ExitStack() as ffn_ctx:
            ffn = FfnWeights(nc, ffn_ctx, a)
            n = Norm(nc, ffn_ctx, early, "n")
            part1(nc, a, X, n, ffn, arrivals, consts, banks)
            part2(nc, a, X, n, ffn, arrivals, consts, banks)
            early.clear()
        part3(nc, a, X, arrivals, consts, banks)
        part4(nc, a, X, out, arrivals, consts, banks)
        shared.clear()


class Inputs:
    pass


def _stacked(w):
    w = w.reshape(2, 4, E0, -1)
    return np.concatenate([w, w, w, np.zeros_like(w)], axis=2).reshape(2 * P, -1)


def kernel(**inputs):
    import concourse.bacc as bacc
    from concourse.bass_utils import run_bass_kernel_spmd

    v = {k: np.asarray(x) for k, x in inputs.items()}
    lay = {}
    lay["x"] = v["L0_attn_x"].reshape(T, D)
    wqk = v["L0_attn_Wqk_w"].reshape(HEADS0 * E0, 2, D)
    bqk = v["L0_attn_Wqk_b"].reshape(HEADS0 * E0, 2)
    lay["wqk"] = np.concatenate([_stacked(wqk[:, s]) for s in range(2)]).T
    lay["bqk"] = np.concatenate([_stacked(bqk[:, s]) for s in range(2)]).reshape(4, P).T
    lay["wv"], lay["bv"] = v["L0_attn_Wv_w"].T, v["L0_attn_Wv_b"]
    lay["wo0"], lay["bo"] = np.tile(v["L0_attn_Wo_w"].T, (2, 1)), v["L0_attn_Wo_b"]
    pad = IP - INNER
    for n in ("gate", "up"):
        lay[f"{n}_q"] = np.pad(v[f"L0_ffn_{n}_q"], ((0, pad), (0, 0))).T
        lay[f"{n}_scale"] = np.pad(v[f"L0_ffn_{n}_scale"], (0, pad)).reshape(NI, P).T
        lay[f"{n}_A"] = np.tile(v[f"L0_ffn_{n}_A"], (1, 4))
        lay[f"{n}_B"] = np.tile(np.pad(v[f"L0_ffn_{n}_B"], ((0, 0), (0, pad))), (4, 1))
    lay["down_q"] = np.pad(v["L0_ffn_down_q"], ((0, 0), (0, pad))).T
    lay["down_scale"] = v["L0_ffn_down_scale"]
    lay["down_A"] = np.tile(np.pad(v["L0_ffn_down_A"], ((0, pad), (0, 0))), (1, 4))
    lay["down_B"] = np.tile(v["L0_ffn_down_B"], (4, 1))
    for n in ("wq", "wk", "wv", "wo"):
        lay[f"{n}1"] = v[f"L1_attn_{n}"]
    lay["dense"] = v["L1_ffn_weight"].T
    lay["lora_A"] = v["L1_ffn_lora_A"].transpose(1, 0, 2).reshape(D, NE * ER)
    lay["lora_B"] = v["L1_ffn_lora_B"].reshape(NE * ER, D)
    lay["gw1"] = v["L1_ffn_gw1"].T
    lay["gw2"] = np.zeros((CT, NH, CT, NE), np.float32)
    for t in range(CT):
        lay["gw2"][t, :, t, :] = v["L1_ffn_gw2"].T
    lay["gw2"] = lay["gw2"].reshape(P, CT * NE)
    for n in ("gb1", "ln_gamma", "ln_beta", "gb2"):
        lay[n] = v[f"L1_ffn_{n}"]

    row = np.arange(P)
    lo_rows = [(row % 32 // 8 == 2), (row % 32 // 8 == 1), (row // 32 % 2 == 1), (row // 64 == 1)]
    lay["masks"] = -np.stack(lo_rows, 1).astype(np.float32)
    lay["ident"] = np.eye(P, dtype=np.float32)
    half = HD // 2
    inv_freq = np.float32(10000.0) ** (-np.arange(half, dtype=np.float32) / np.float32(half))
    angle = inv_freq[:, None] * np.arange(SEQ, dtype=np.float32)[None, :]
    lay["cos"] = np.tile(np.cos(angle), (2, 1))
    lay["sin"] = np.concatenate([-np.sin(angle), np.sin(angle)])
    older, same = row[None, :] > row[:, None], row[None, :] <= row[:, None]
    lay["window"] = np.where(np.concatenate([older, same], 1), 0, MASKED).astype(np.float32)
    lay["experts"] = np.tile(np.arange(NE, dtype=np.float32), (P, 1))

    nc = bacc.Bacc("TRN2", target_bir_lowering=False, num_devices=1, dynamic_dma_scratch_size=768)
    a, arrays = Inputs(), {}
    for name, x in lay.items():
        arrays[f"in_{name}"] = np.ascontiguousarray(x)
        a.__dict__[name] = nc.dram_tensor(f"in_{name}", x.shape, mybir.dt.from_np(x.dtype), kind="ExternalInput").ap()
    out = nc.dram_tensor("out", (T, D), F32, kind="ExternalOutput").ap()
    a.parked = nc.dram_tensor("parked", (T, D), F32, kind="Internal").ap()
    program(nc, a, out)
    r = run_bass_kernel_spmd(nc, [arrays], core_ids=[0])
    return r.results[0]["out"].reshape(BATCH, SEQ, D)
```
